# Optimizing a Trainium2 kernel written in Bass

```python
import numpy as np
import jax
import jax.numpy as jnp

def _softmax(x, axis=-1):
    return jax.nn.softmax(x, axis=axis)

def _gelu(x):
    return jax.nn.gelu(x, approximate=True)

def _silu(x):
    return jax.nn.silu(x)

def _sigmoid(x):
    return jax.nn.sigmoid(x)

def _layernorm(x, axis=-1, eps=1e-05):
    m = jnp.mean(x, axis=axis, keepdims=True)
    v = jnp.var(x, axis=axis, keepdims=True)
    return (x - m) / jnp.sqrt(v + eps)

def _scatter_add(tgt, idx, src, axis=0):
    return tgt.at[idx].add(src)

def _segment_sum(src, seg, n):
    return jax.ops.segment_sum(src, seg, n)
kernel_name = 'mk_macaron_d1_jaxref_r8_82418e'

def setup_inputs(seed: int=0):
    np.random.seed(seed)
    _w = jnp.asarray

    def _L0_attn_setup():
        import jax, jax.numpy as jnp
        import numpy as np
        D_MODEL = 256
        D_STATE = 64
        D_CONV = 4
        EXPAND = 2
        HEADDIM = 64
        NGROUPS = 1
        CHUNK = 64
        D_INNER = EXPAND * D_MODEL
        NHEADS = D_INNER // HEADDIM
        D_XBC = D_INNER + 2 * NGROUPS * D_STATE
        D_IN_PROJ = 2 * D_INNER + 2 * NGROUPS * D_STATE + NHEADS

        def segsum(x):
            T = x.shape[-1]
            mask_strict = jnp.tril(jnp.ones((T, T), bool), k=-1)
            mask_incl = jnp.tril(jnp.ones((T, T), bool), k=0)
            xe = jnp.where(mask_strict, x[..., :, None], 0.0)
            xseg = jnp.cumsum(xe, axis=-2)
            return jnp.where(mask_incl, xseg, -jnp.inf)

        def ssd_scan(X, A, Bm, Cm, block_len=CHUNK):
            b, seqlen, h, p = X.shape
            n = Bm.shape[-1]
            pad_len = (block_len - seqlen % block_len) % block_len
            if pad_len > 0:
                X = jnp.pad(X, ((0, 0), (0, pad_len), (0, 0), (0, 0)))
                A = jnp.pad(A, ((0, 0), (0, pad_len), (0, 0)))
                Bm = jnp.pad(Bm, ((0, 0), (0, pad_len), (0, 0), (0, 0)))
                Cm = jnp.pad(Cm, ((0, 0), (0, pad_len), (0, 0), (0, 0)))
            L = X.shape[1]
            c = L // block_len
            Xc = X.reshape(b, c, block_len, h, p)
            Ac = A.reshape(b, c, block_len, h).transpose(0, 3, 1, 2)
            Bc = Bm.reshape(b, c, block_len, h, n)
            Cc = Cm.reshape(b, c, block_len, h, n)
            A_cum = jnp.cumsum(Ac, axis=-1)
            Lmat = jnp.exp(segsum(Ac))
            CB = jnp.einsum('bclhn,bcshn->bhcls', Cc, Bc)
            Y_diag = jnp.einsum('bhcls,bcshp->bhclp', CB * Lmat, Xc)
            decay_states = jnp.exp(A_cum[..., -1:] - A_cum)
            states = jnp.einsum('bhcl,bclhn,bclhp->bhcpn', decay_states, Bc, Xc)
            init = jnp.zeros((b, h, 1, p, n), X.dtype)
            states = jnp.concatenate([init, states], axis=2)
            chunk_decay = jnp.pad(A_cum[..., -1], ((0, 0), (0, 0), (1, 0)))
            decay_chunk = jnp.exp(segsum(chunk_decay))
            new_states = jnp.einsum('bhzc,bhcpn->bhzpn', decay_chunk, states)[:, :, :-1]
            Y_off = jnp.einsum('bclhn,bhcpn,bhcl->bhclp', Cc, new_states, jnp.exp(A_cum))
            Y = (Y_diag + Y_off).transpose(0, 2, 3, 1, 4).reshape(b, L, h, p)
            if pad_len > 0:
                Y = Y[:, :seqlen]
            return Y

        def rmsnorm_grouped(x, w, ngroups, eps=1e-05):
            gs = x.shape[-1] // ngroups
            xg = x.reshape(*x.shape[:-1], ngroups, gs)
            xg = xg * jax.lax.rsqrt(jnp.mean(xg * xg, axis=-1, keepdims=True) + eps)
            return xg.reshape(x.shape) * w
        key = jax.random.key(seed)
        ks = jax.random.split(key, 8)
        B, L = (2, 512)
        u = jax.random.normal(ks[0], (B, L, D_MODEL), jnp.float32)
        W_in = jax.random.normal(ks[1], (D_IN_PROJ, D_MODEL), jnp.float32) * 0.02
        conv_w = jax.random.normal(ks[2], (D_XBC, D_CONV), jnp.float32) * 0.2
        conv_b = jnp.zeros((D_XBC,), jnp.float32)
        dt = jnp.exp(jax.random.uniform(ks[3], (NHEADS,)) * (np.log(0.1) - np.log(0.001)) + np.log(0.001))
        dt = jnp.clip(dt, 0.0001)
        dt_bias = dt + jnp.log(-jnp.expm1(-dt))
        A_log = jnp.log(jax.random.uniform(ks[4], (NHEADS,), minval=1.0, maxval=16.0))
        D_param = jnp.ones((NHEADS,), jnp.float32)
        norm_w = jnp.ones((D_INNER,), jnp.float32)
        W_out = jax.random.normal(ks[5], (D_MODEL, D_INNER), jnp.float32) * 0.02
        return dict(u=u, W_in=W_in, conv_w=conv_w, conv_b=conv_b, dt_bias=dt_bias, A_log=A_log, D_param=D_param, norm_w=norm_w, W_out=W_out)
    _L0_attn_in = _L0_attn_setup()

    def _L0_ffn_setup():
        import jax, jax.numpy as jnp
        import numpy as np
        HIDDEN = 256
        INTER = 1024
        RETRIEVAL = 128
        NUM_EXPERTS = 512
        NUM_KEYS = 64
        TOP_K = 8
        B, S = (4, 256)
        key = jax.random.key(seed)
        ks = jax.random.split(key, 8)
        sc = 0.02
        return {'hidden_states': jax.random.normal(ks[0], (B, S, HIDDEN), jnp.float32), 'W_q': jax.random.normal(ks[1], (HIDDEN, RETRIEVAL), jnp.float32) * sc, 'keys': jax.random.normal(ks[2], (2, RETRIEVAL // 2, NUM_KEYS), jnp.float32) * sc, 'down_embed': jax.random.normal(ks[3], (NUM_EXPERTS, HIDDEN), jnp.float32) * sc, 'up_embed': jax.random.normal(ks[4], (NUM_EXPERTS, HIDDEN), jnp.float32) * sc, 'gate_w': jax.random.normal(ks[5], (HIDDEN, INTER), jnp.float32) * sc, 'up_w': jax.random.normal(ks[6], (HIDDEN, INTER), jnp.float32) * sc, 'down_w': jax.random.normal(ks[7], (INTER, HIDDEN), jnp.float32) * sc}
    _L0_ffn_in = _L0_ffn_setup()
    _d = {'L0_attn_u': _L0_attn_in['u'], 'L0_attn_W_in': _L0_attn_in['W_in'], 'L0_attn_conv_w': _L0_attn_in['conv_w'], 'L0_attn_conv_b': _L0_attn_in['conv_b'], 'L0_attn_dt_bias': _L0_attn_in['dt_bias'], 'L0_attn_A_log': _L0_attn_in['A_log'], 'L0_attn_D_param': _L0_attn_in['D_param'], 'L0_attn_norm_w': _L0_attn_in['norm_w'], 'L0_attn_W_out': _L0_attn_in['W_out'], 'L0_ffn_W_q': _L0_ffn_in['W_q'], 'L0_ffn_keys': _L0_ffn_in['keys'], 'L0_ffn_down_embed': _L0_ffn_in['down_embed'], 'L0_ffn_up_embed': _L0_ffn_in['up_embed'], 'L0_ffn_gate_w': _L0_ffn_in['gate_w'], 'L0_ffn_up_w': _L0_ffn_in['up_w'], 'L0_ffn_down_w': _L0_ffn_in['down_w']}
    _x0 = _d['L0_attn_u']
    _d['L0_attn_u'] = jax.random.normal(jax.random.fold_in(jax.random.key(seed), 1), (1, 2048, 256), dtype=_x0.dtype)
    del _x0
    return _d

def reference(L0_attn_u, L0_attn_W_in, L0_attn_conv_w, L0_attn_conv_b, L0_attn_dt_bias, L0_attn_A_log, L0_attn_D_param, L0_attn_norm_w, L0_attn_W_out, L0_ffn_W_q, L0_ffn_keys, L0_ffn_down_embed, L0_ffn_up_embed, L0_ffn_gate_w, L0_ffn_up_w, L0_ffn_down_w):

    def _L0_attn_ref(u, W_in, conv_w, conv_b, dt_bias, A_log, D_param, norm_w, W_out):
        import jax, jax.numpy as jnp
        import numpy as np
        D_MODEL = 256
        D_STATE = 64
        D_CONV = 4
        EXPAND = 2
        HEADDIM = 64
        NGROUPS = 1
        CHUNK = 64
        D_INNER = EXPAND * D_MODEL
        NHEADS = D_INNER // HEADDIM
        D_XBC = D_INNER + 2 * NGROUPS * D_STATE
        D_IN_PROJ = 2 * D_INNER + 2 * NGROUPS * D_STATE + NHEADS

        def segsum(x):
            T = x.shape[-1]
            mask_strict = jnp.tril(jnp.ones((T, T), bool), k=-1)
            mask_incl = jnp.tril(jnp.ones((T, T), bool), k=0)
            xe = jnp.where(mask_strict, x[..., :, None], 0.0)
            xseg = jnp.cumsum(xe, axis=-2)
            return jnp.where(mask_incl, xseg, -jnp.inf)

        def ssd_scan(X, A, Bm, Cm, block_len=CHUNK):
            b, seqlen, h, p = X.shape
            n = Bm.shape[-1]
            pad_len = (block_len - seqlen % block_len) % block_len
            if pad_len > 0:
                X = jnp.pad(X, ((0, 0), (0, pad_len), (0, 0), (0, 0)))
                A = jnp.pad(A, ((0, 0), (0, pad_len), (0, 0)))
                Bm = jnp.pad(Bm, ((0, 0), (0, pad_len), (0, 0), (0, 0)))
                Cm = jnp.pad(Cm, ((0, 0), (0, pad_len), (0, 0), (0, 0)))
            L = X.shape[1]
            c = L // block_len
            Xc = X.reshape(b, c, block_len, h, p)
            Ac = A.reshape(b, c, block_len, h).transpose(0, 3, 1, 2)
            Bc = Bm.reshape(b, c, block_len, h, n)
            Cc = Cm.reshape(b, c, block_len, h, n)
            A_cum = jnp.cumsum(Ac, axis=-1)
            Lmat = jnp.exp(segsum(Ac))
            CB = jnp.einsum('bclhn,bcshn->bhcls', Cc, Bc)
            Y_diag = jnp.einsum('bhcls,bcshp->bhclp', CB * Lmat, Xc)
            decay_states = jnp.exp(A_cum[..., -1:] - A_cum)
            states = jnp.einsum('bhcl,bclhn,bclhp->bhcpn', decay_states, Bc, Xc)
            init = jnp.zeros((b, h, 1, p, n), X.dtype)
            states = jnp.concatenate([init, states], axis=2)
            chunk_decay = jnp.pad(A_cum[..., -1], ((0, 0), (0, 0), (1, 0)))
            decay_chunk = jnp.exp(segsum(chunk_decay))
            new_states = jnp.einsum('bhzc,bhcpn->bhzpn', decay_chunk, states)[:, :, :-1]
            Y_off = jnp.einsum('bclhn,bhcpn,bhcl->bhclp', Cc, new_states, jnp.exp(A_cum))
            Y = (Y_diag + Y_off).transpose(0, 2, 3, 1, 4).reshape(b, L, h, p)
            if pad_len > 0:
                Y = Y[:, :seqlen]
            return Y

        def rmsnorm_grouped(x, w, ngroups, eps=1e-05):
            gs = x.shape[-1] // ngroups
            xg = x.reshape(*x.shape[:-1], ngroups, gs)
            xg = xg * jax.lax.rsqrt(jnp.mean(xg * xg, axis=-1, keepdims=True) + eps)
            return xg.reshape(x.shape) * w
        B, L, _ = u.shape
        zxbcdt = u @ W_in.T
        z = zxbcdt[..., :D_INNER]
        xBC = zxbcdt[..., D_INNER:D_INNER + D_XBC]
        dt = zxbcdt[..., D_INNER + D_XBC:]
        xpad = jnp.pad(xBC, ((0, 0), (D_CONV - 1, 0), (0, 0)))
        conv = conv_b
        for k in range(D_CONV):
            conv = conv + conv_w[:, k] * xpad[:, k:k + L, :]
        xBC = jax.nn.silu(conv)
        x = xBC[..., :D_INNER].reshape(B, L, NHEADS, HEADDIM)
        B_ssm = xBC[..., D_INNER:D_INNER + NGROUPS * D_STATE].reshape(B, L, NGROUPS, D_STATE)
        C_ssm = xBC[..., D_INNER + NGROUPS * D_STATE:].reshape(B, L, NGROUPS, D_STATE)
        if NGROUPS < NHEADS:
            rep = NHEADS // NGROUPS
            B_ssm = jnp.repeat(B_ssm, rep, axis=2)
            C_ssm = jnp.repeat(C_ssm, rep, axis=2)
        dt = jax.nn.softplus(dt + dt_bias)
        A = -jnp.exp(A_log)
        y = ssd_scan(x * dt[..., None], A * dt, B_ssm, C_ssm, block_len=CHUNK)
        y = y + D_param[:, None] * x
        y = y.reshape(B, L, D_INNER)
        y = rmsnorm_grouped(y * jax.nn.silu(z), norm_w, NGROUPS)
        return y @ W_out.T

    def _L0_ffn_ref(hidden_states, W_q, keys, down_embed, up_embed, gate_w, up_w, down_w):
        import jax, jax.numpy as jnp
        import numpy as np
        HIDDEN = 256
        INTER = 1024
        RETRIEVAL = 128
        NUM_EXPERTS = 512
        NUM_KEYS = 64
        TOP_K = 8
        B, S = (4, 256)
        b, s, h = hidden_states.shape
        n = b * s
        queries = (hidden_states @ W_q).reshape(2, n, RETRIEVAL // 2)
        routing = jnp.einsum('tnd,tdk->tnk', queries, keys)
        scores2, idx2 = jax.lax.top_k(routing, TOP_K)
        sx, sy = (scores2[0], scores2[1])
        ix, iy = (idx2[0], idx2[1])
        all_scores = (sx[:, :, None] + sy[:, None, :]).reshape(n, TOP_K * TOP_K)
        all_idx = (ix[:, :, None] * NUM_KEYS + iy[:, None, :]).reshape(n, TOP_K * TOP_K)
        scores, pk = jax.lax.top_k(all_scores, TOP_K)
        indices = jnp.take_along_axis(all_idx, pk, axis=-1)
        de = down_embed[indices]
        ue = up_embed[indices]
        x = hidden_states.reshape(n, h)
        ew = jnp.einsum('nh,nkh->nk', x, de)
        ew = jax.nn.silu(ew) * jax.nn.softmax(scores, axis=-1)
        experts_states = jnp.einsum('nk,nkh->nh', ew, ue).reshape(b, s, h)
        mlp = jax.nn.silu(x @ gate_w) * (x @ up_w) @ down_w
        return mlp.reshape(b, s, h) + experts_states
    x = L0_attn_u
    x = x + 0.5 * _L0_ffn_ref(_layernorm(x, axis=-1), L0_ffn_W_q, L0_ffn_keys, L0_ffn_down_embed, L0_ffn_up_embed, L0_ffn_gate_w, L0_ffn_up_w, L0_ffn_down_w)
    x = x + _L0_attn_ref(_layernorm(x, axis=-1), L0_attn_W_in, L0_attn_conv_w, L0_attn_conv_b, L0_attn_dt_bias, L0_attn_A_log, L0_attn_D_param, L0_attn_norm_w, L0_attn_W_out)
    x = x + 0.5 * _L0_ffn_ref(_layernorm(x, axis=-1), L0_ffn_W_q, L0_ffn_keys, L0_ffn_down_embed, L0_ffn_up_embed, L0_ffn_gate_w, L0_ffn_up_w, L0_ffn_down_w)
    return x

_drawn_inputs = setup_inputs


def setup_inputs(seed=0):
    import zlib

    import numpy as np

    out = dict(_drawn_inputs(seed))
    spreads = {'L0_attn_conv_b': (0.0, 0.1), 'L0_attn_D_param': (1.0, 0.2), 'L0_attn_norm_w': (1.0, 0.2)}
    factors = {'L0_attn_dt_bias': 8.0,
     'L0_attn_A_log': 8.0,
     'L0_ffn_W_q': 8.0,
     'L0_ffn_keys': 8.0,
     'L0_ffn_down_embed': 8.0,
     'L0_ffn_up_embed': 8.0}
    for name, (base, spread) in spreads.items():
        noise = np.random.default_rng([zlib.crc32(name.encode()), seed]).standard_normal(out[name].shape)
        drawn = base * np.exp(spread * noise) if base else spread * noise
        out[name] = jnp.asarray(drawn.astype(out[name].dtype))
    for name, factor in factors.items():
        out[name] = (out[name] * factor).astype(out[name].dtype)
    return out
```

```python
import concourse.bass as bass
from concourse import mybir
from contextlib import ExitStack

SEQ, DM, P = 2048, 256, 128
TILES = SEQ // P
GT = 4
BLOCKS = TILES // GT
BT = GT * P
KD = DM // P
INTER = 1024
FC = INTER // P
NKEY, TOPK, NEXP = 64, 8, 512
EC = NEXP // P
XKEYS = NEXP // NKEY
DI, NH, HD, NS, TAPS = 512, 8, 64, 64, 4
CC = DI // P
XBC = DI + 2 * NS
CONVC = XBC // P
LN_EPS = 1e-5
RMS_EPS = 1e-5
RSQRT_MAGIC = float(0x5F3759DF)
CREDIT = 4
SERIES = 9


def program(nc, A):
    fp32, bf16 = mybir.dt.float32, mybir.dt.bfloat16
    i32, u32 = mybir.dt.int32, mybir.dt.uint32
    ALU, ACT, AX = mybir.AluOpType, mybir.ActivationFunctionType, mybir.AxisListType
    ds = bass.ds
    ctx = ExitStack()
    with ctx:
        def sb(name, shape, dt=fp32):
            return ctx.enter_context(nc.sbuf_tensor(name, shape, dt))

        def sem(name):
            return ctx.enter_context(nc.semaphore(name))

        WORK = 19456
        work = sb("work", [P, WORK])
        used = {"ffn": 0, "att": 0}

        def part(layer, *shape):
            n = 1
            for d in shape:
                n *= d
            at = used[layer]
            used[layer] += n
            assert used[layer] <= WORK
            v = work[:, at:at + n]
            names = "abc"[:len(shape)]
            if len(shape) == 1:
                return v
            return v.rearrange(f"p ({' '.join(names)}) -> p {' '.join(names)}", **dict(zip(names, shape)))

        x = sb("x", [P, TILES, DM])
        wq = sb("wq", [P, KD, P])
        wg = sb("wg", [P, KD, INTER])
        wu = sb("wu", [P, KD, INTER])
        wd = sb("wd", [P, FC, DM])
        de = sb("de", [P, KD, NEXP])
        ue = sb("ue", [P, EC, DM])
        keys = sb("keys", [P, P])
        win = sb("win", [P, KD, XBC])
        wz = sb("wz", [P, KD, DI])
        wdt = sb("wdt", [P, KD, NH])
        wo = sb("wo", [P, CC, DM])
        small = sb("small", [P, 53])
        convw = small[:, 0:20].rearrange("p (c k) -> p c k", k=TAPS)
        convb = small[:, 20:25]
        normw = small[:, 25:29]
        dtb, alog, dpar = small[:, 29:37], small[:, 37:45], small[:, 45:53]
        cst = sb("cst", [P, 4, P])
        ident, tri_incl, tri_after, ones = cst[:, 0, :], cst[:, 1, :], cst[:, 2, :], cst[:, 3, :]
        sel = sb("sel", [NKEY + XKEYS + 1, EC + 1, P])
        selb = sb("selb", [NKEY + XKEYS, EC, P], bf16)
        iota = sb("iota", [P, NKEY])
        iotab = sb("iotab", [P, NKEY], bf16)

        stats = sb("stats", [P, GT, 6])
        mv = sb("mv", [P, GT, 2])
        rs = sb("rs", [P, 4, GT])
        varc = sb("varc", [P, GT])
        rstd = sb("rstd", [P, GT])
        xn = sb("xn", [P, GT, DM])
        hT = part("ffn", KD, SEQ)
        qT = part("ffn", SEQ)

        rT = part("ffn", BT)
        rtok = part("ffn", GT, P)
        sxy = sb("sxy", [P, 2, GT, TOPK])
        ixy = sb("ixy", [P, 2, GT, TOPK], u32)
        ixyf = sb("ixyf", [P, 2, GT, TOPK])
        sums = sb("sums", [P, GT, 64])
        best = sb("best", [P, GT, TOPK])
        rest = sb("rest", [P, GT, 64])
        chosen = sb("chosen", [P, GT, 64])
        chosenw = sb("chosenw", [P, GT, 64])
        dxy = sb("dxy", [P, 2 * GT, TOPK])
        exy = sb("exy", [P, 2 * GT, TOPK])
        sxyv = sxy[:, :, :, :].rearrange("p s g k -> p (s g) k")
        exyv = exy[:, :, :].rearrange("p (s g) k -> p s g k", s=2)
        cnt = sb("cnt", [P, GT, TOPK])
        rowsum = sb("rowsum", [P, GT, TOPK])
        clamped = sb("clamped", [P, GT, TOPK])
        zsum = sb("zsum", [P, GT])
        zinv = sb("zinv", [P, 2, GT])
        eqx = sb("eqx", [P, GT, XKEYS, TOPK])
        onehot = sb("onehot", [P, 2, TOPK, NKEY], bf16)
        TT = sb("TT", [P, GT, 73])
        DD = sb("DD", [P, GT, 72])
        TTs = sb("TTs", [73, BT])
        DDs = sb("DDs", [72, BT], bf16)
        E = part("ffn", 2, BT)
        TP = part("ffn", 2, BT)
        SP = part("ffn", 2, BT)
        GE = part("ffn", 2, BT)
        coef = part("ffn", EC, BT)
        TG = part("ffn", 2, BT)
        SG = part("ffn", 2, BT)
        gu = part("ffn", FC, BT)

        hTb = part("att", KD, BT)
        U = sb("U", [P, CONVC, TAPS - 1 + BT])
        acc = part("att", 2, BT)
        TC = part("att", 2, BT)
        xc = part("att", CC, BT)
        BTt = part("att", BT)[0:NS, :]
        CTt = part("att", BT)[0:NS, :]
        negA = sb("negA", [P, NH])
        sp = sb("sp", [P, 6, GT * NH])
        dt = sb("dt", [P, GT, NH])
        a = sb("a", [P, GT, NH])
        decays = sb("decays", [P, 3, GT, NH])
        adiag = part("att", NH, P)
        xtok = part("att", DI)
        xdt = part("att", DI)
        xdd = part("att", DI)
        xD = part("att", DI)
        Btok = sb("Btok", [P, NS])
        Tz = part("att", DI)
        SZ = part("att", DI)
        Lx = part("att", NH, P)
        CBm = sb("CBm", [P, P])
        M = part("att", NH, P)
        state = sb("state", [NS, DI])
        y1 = part("att", DI)
        yg = part("att", DI)
        sq = part("att", DI)
        ss = sb("ss", [P, GT])
        ygT = part("att", CC, P)
        obuf = sb("obuf", [P, GT, DM])

        bank = [ctx.enter_context(nc.psum_tensor(f"bank{n}", [P, 512], fp32)) for n in range(8)]


        in_x = [sem(f"in_x{n}") for n in range(BLOCKS)]
        x_there = sem("x_there")
        in_c, in_f, in_a = sem("in_consts"), sem("in_ffn"), sem("in_attn")
        prep = sem("constants_prepared")
        out_sent = sem("out_sent")
        dve_done = sem("dve_done")
        passed = sem("passed")
        FFN_SEMS = {
            "pe": ("hps", "qps", "rps", "rtps", "ttps", "ddps", "pps", "lps", "dps", "rbps", "gps", "ups", "ops"),
            "act": ("h", "q", "rT", "rtok", "exy", "tts", "dds", "tp", "e", "tg"),
            "dve": ("xn", "dxy", "tt", "dd", "sg", "gu", "ge", "sp", "res", "out"),
            "pool": ("coef",)}
        ATT_SEMS = {
            "pe": ("hps", "pps", "dtps", "cums", "zps", "xps", "cbps", "segps", "ydps", "offps", "stps", "ytps", "ops"),
            "act": ("h", "u", "tc", "eu", "decays", "lx", "tz", "xt", "bt", "ss", "yt", "o"),
            "dve": ("xn", "conv", "xc", "raw", "ab", "a", "sz", "cbm", "m", "yoff", "yadd", "state", "yg", "x1"),
            "pool": ("hist", "ad", "xdt", "xdd", "xD")}
        ffn_s = [{n: sem(f"f{L}_{n}") for names in FFN_SEMS.values() for n in names} for L in range(2)]
        att_s = {n: sem(f"a_{n}") for names in ATT_SEMS.values() for n in names}

        def credit(eng, who):
            for S in ffn_s:
                for n in FFN_SEMS[who]:
                    eng.sem_inc(S[n], CREDIT)
            for n in ATT_SEMS[who]:
                eng.sem_inc(att_s[n], CREDIT)

        def nth(n):
            return n + CREDIT

        class Chain:

            def __init__(self, eng, s):
                self.eng, self.s, self.before, self.base, self.n = eng, s, 0, 0, 0

            def do(self, ins):
                ins.then_inc(self.s, 1)
                self.n += 1

            def wait(self):
                self.eng.wait_ge(self.s, self.base + self.n)

            def enter(self, i, per):
                self.before += self.n
                self.per, self.n = per, 0
                self.base = i * per + self.before

            def leave(self, trips):
                assert self.n == self.per, (self.n, self.per)
                self.before += trips * self.per
                self.base, self.n = self.before, 0

        block = ctx.enter_context(nc.Block())
        xv = A["u"].rearrange("o (t p) d -> p (o t) d", p=P)
        ov = A["out"].rearrange("o (t p) d -> p (o t) d", p=P)
        CONSTS = [("cst", cst), ("small", small), ("iota", iota), ("sel", sel)]
        FFNW = [("wq", wq), ("keys", keys), ("wg", wg), ("wu", wu), ("wd", wd), ("de", de), ("ue", ue)]
        ATTNW = [("win", win), ("wz", wz), ("wdt", wdt), ("wo", wo)]

        def full(t):
            return t[tuple(slice(None) for _ in t.shape)]

        def hb(t):
            return t.rearrange("p (h d) -> p h d", d=HD)

        def per_head(t, parts=P):
            return t.unsqueeze(2).to_broadcast([parts, NH, HD])

        @block.sync
        def _(sync):
            for n in range(BLOCKS):
                sync.dma_start(x[:, GT * n:GT * (n + 1), :], xv[:, GT * n:GT * (n + 1), :]).then_inc(in_x[n], 16)
                if n == 0:
                    for name, t in CONSTS:
                        sync.dma_start(full(t), A[name]).then_inc(in_c, 16)
            for name, t in FFNW:
                sync.dma_start(full(t), A[name]).then_inc(in_f, 16)
            for name, t in ATTNW:
                sync.dma_start(full(t), A[name]).then_inc(in_a, 16)
            for n in range(BLOCKS):
                sync.wait_ge(in_x[n], 16)
                sync.sem_inc(x_there, 1)
            with sync.Fori(0, BLOCKS) as i:
                sync.wait_ge(ffn_s[1]["out"], nth(i * GT + GT))
                sync.dma_start(ov[:, ds(i * GT, GT), :], x[:, ds(i * GT, GT), :]).then_inc(out_sent, 16)
            sync.wait_ge(out_sent, 16 * BLOCKS)

        @block.vector
        def _(dve):
            ch = Chain(dve, dve_done)
            v = nc.vector
            credit(dve, "dve")

            def alone():
                dve.sem_inc(passed, 1)

            def rsqrt(var, y, scale):
                vh, w, t, bits = (rs[:, n, :] for n in range(4))
                ch.do(v.tensor_scalar(vh, var, -0.5, None, ALU.mult))
                ch.do(v.tensor_scalar(bits.bitcast(i32), var.bitcast(i32), 1, None, ALU.logical_shift_right))
                ch.wait()
                ch.do(v.tensor_scalar(w.bitcast(i32), bits.bitcast(i32), -1.0, RSQRT_MAGIC, ALU.mult, ALU.add))
                for n in range(3):
                    ch.wait()
                    ch.do(v.tensor_tensor(t, w, w, ALU.mult))
                    ch.wait()
                    ch.do(v.tensor_tensor(t, t, vh, ALU.mult))
                    ch.wait()
                    ch.do(v.scalar_tensor_tensor(w, t, 1.5, w, ALU.add, ALU.mult))
                ch.wait()
                ch.do(v.tensor_scalar(y, w, scale, None, ALU.mult))
                ch.wait()
            RSQRT = 2 + 1 + 9 + 1

            def normalize(i, S):
                for g in range(GT):
                    ch.do(v.bn_stats(stats[:, g, :], x[:, i * GT + g, :]))
                ch.wait()
                alone()
                for g in range(GT):
                    ch.do(v.bn_aggr(mv[:, g, :], stats[:, g, :]))
                ch.wait()
                ch.do(v.tensor_scalar(varc[:, :], mv[:, :, 1], LN_EPS, None, ALU.add))
                ch.wait()
                rsqrt(varc[:, :], rstd[:, :], 1.0)
                dve.wait_ge(S["hps"], nth(i * KD))
                for g in range(GT):
                    v.tensor_scalar(xn[:, g, :], x[:, i * GT + g, :], mv[:, g, 0:1], rstd[:, g:g + 1],
                                    ALU.subtract, ALU.mult).then_inc(S["xn"], 1)
            NORM = GT + GT + 1 + RSQRT

            def sq8(t):
                return t.rearrange("p g (a b) -> p g a b", b=TOPK)

            def routing(i, S, part):
                rx, ry = rtok[:, :, 0:NKEY], rtok[:, :, NKEY:P]
                pairs = [P, GT, TOPK, TOPK]
                if part == 0:
                    dve.wait_ge(S["rtok"], nth(i + 1))
                    alone()
                    for s, r in ((0, rx), (1, ry)):
                        for g in range(GT):
                            ch.do(v.max(sxy[:, s, g, :], r[:, g, :]))
                elif part == 1:
                    ch.wait()
                    alone()
                    for s, r in ((0, rx), (1, ry)):
                        for g in range(GT):
                            ch.do(v.max_index(ixy[:, s, g, :], sxy[:, s, g, :], r[:, g, :]))
                    ch.do(v.tensor_tensor(sq8(sums[:, :, :]), sxy[:, 0, :, :].unsqueeze(3).to_broadcast(pairs),
                                          sxy[:, 1, :, :].unsqueeze(2).to_broadcast(pairs), ALU.add))
                    v.tensor_tensor(dxy[:, :, :], sxyv[:, :, :], sxyv[:, :, 0:1].to_broadcast([P, 2 * GT, TOPK]),
                                    ALU.subtract).then_inc(S["dxy"], 1)
                elif part == 2:
                    ch.wait()
                    alone()
                    for g in range(GT):
                        ch.do(v.max(best[:, g, :], sums[:, g, :]))
                    ch.do(v.tensor_copy(ixyf[:, :, :, :], ixy[:, :, :, :]))
                    ch.wait()
                    alone()
                    for g in range(GT):
                        ch.do(v.match_replace(rest[:, g, :], best[:, g, :], sums[:, g, :], -3.0e38))
                elif part == 3:
                    ch.wait()
                    ch.do(v.tensor_tensor(chosen[:, :, :], sums[:, :, :], rest[:, :, :], ALU.not_equal))
                    dve.wait_ge(S["ttps"], nth(i))
                    ch.do(v.tensor_tensor(TT[:, :, 0:NKEY], ry, sxy[:, 1, :, 0:1].to_broadcast([P, GT, NKEY]), ALU.subtract))
                    ch.do(v.tensor_tensor(TT[:, :, NKEY:NKEY + XKEYS], rx[:, :, 0:XKEYS],
                                          sxy[:, 0, :, 0:1].to_broadcast([P, GT, XKEYS]), ALU.subtract))
                    ch.wait()
                    ch.do(v.tensor_reduce(cnt[:, :, :], sq8(chosen[:, :, :]), AX.X, ALU.add))
                    dve.wait_ge(S["exy"], nth(i + 1))
                    ch.do(v.tensor_tensor(sq8(chosenw[:, :, :]), sq8(chosen[:, :, :]),
                                          exyv[:, 1, :, :].unsqueeze(2).to_broadcast(pairs), ALU.mult))
                elif part == 4:
                    ch.wait()
                    ch.do(v.tensor_reduce(rowsum[:, :, :], sq8(chosenw[:, :, :]), AX.X, ALU.add))
                    ch.wait()
                    ch.do(v.tensor_tensor(rowsum[:, :, :], rowsum[:, :, :], exyv[:, 0, :, :], ALU.mult))
                    ch.wait()
                    ch.do(v.tensor_reduce(zsum[:, :], rowsum[:, :, :], AX.X, ALU.add))
                    ch.do(v.scalar_tensor_tensor(clamped[:, :, :], ixyf[:, 0, :, :], float(XKEYS), rowsum[:, :, :],
                                                 ALU.is_ge, ALU.mult))
                    ch.wait()
                    ch.do(v.reciprocal(zinv[:, 0, :], zsum[:, :]))
                    v.tensor_reduce(TT[:, :, 72:73], clamped[:, :, :], AX.X, ALU.add).then_inc(S["tt"], 1)
                elif part == 5:
                    ch.wait()
                    ch.do(v.tensor_scalar(zinv[:, 1, :], zinv[:, 0, :], 0.25, None, ALU.mult))
                    ch.do(v.tensor_tensor(eqx[:, :, :, :], ixyf[:, 0, :, :].unsqueeze(2).to_broadcast([P, GT, XKEYS, TOPK]),
                                          iota[:, 0:XKEYS].unsqueeze(1).unsqueeze(3).to_broadcast([P, GT, XKEYS, TOPK]),
                                          ALU.is_equal))
                    ch.wait()
                    ch.do(v.tensor_tensor(eqx[:, :, :, :], eqx[:, :, :, :],
                                          cnt[:, :, :].unsqueeze(2).to_broadcast([P, GT, XKEYS, TOPK]), ALU.mult))
                    ch.wait()
                    dve.wait_ge(S["ddps"], nth(i))
                    ch.do(v.tensor_reduce(DD[:, :, NKEY:NKEY + XKEYS], eqx[:, :, :, :], AX.X, ALU.add))
                else:
                    for g in (0, 1) if part == 6 else (2, 3):
                        dve.wait_ge(S["dd"], nth(i * GT + (g - 1)))
                        for b in range(TOPK):
                            ch.do(v.tensor_scalar(onehot[:, g % 2, b, :], iotab[:, :], ixyf[:, 1, g, b:b + 1], float(TOPK - b),
                                                  ALU.is_equal, ALU.mult))
                        ch.wait()
                        v.tensor_reduce(DD[:, g, 0:NKEY], onehot[:, g % 2, :, :].rearrange("p b j -> p j b"), AX.X, ALU.add)\
                            .then_inc(S["dd"], 1)
            ROUTE = 2 * GT + 2 * GT + 1 + 2 * GT + 1 + 5 + 5 + 4 + GT * TOPK

            def ffn(L):
                S = ffn_s[L]
                with dve.Fori(0, BLOCKS) as i:
                    ch.enter(i, NORM)
                    if L == 0:
                        dve.wait_ge(x_there, i + 1)
                    normalize(i, S)
                    ch.leave(BLOCKS)
                with dve.Fori(0, BLOCKS) as i:
                    ch.enter(i, ROUTE)
                    for f in range(FC):
                        k = i * FC + (f + 1)
                        dve.wait_ge(S["tg"], nth(k))
                        v.scalar_tensor_tensor(SG[:, f % 2, :], TG[:, f % 2, :], 1.0, bank[2 * (f % 2)][:, :], ALU.add, ALU.mult)\
                            .then_inc(S["sg"], 1)
                        dve.wait_ge(S["sg"], nth(k))
                        dve.wait_ge(S["ups"], nth(k))
                        v.tensor_tensor(gu[:, f, :], SG[:, f % 2, :], bank[2 * (f % 2) + 1][:, :], ALU.mult).then_inc(S["gu"], 1)
                        routing(i, S, f)
                    for c in range(EC):
                        k = i * EC + (c + 1)
                        dve.wait_ge(S["dps"], nth(k))
                        dve.wait_ge(S["e"], nth(k))
                        dve.wait_ge(S["coef"], nth(k - 2))
                        v.scalar_tensor_tensor(GE[:, c % 2, :], bank[4 + c % 2][:, :], float(TOPK), E[:, c % 2, :],
                                               ALU.is_gt, ALU.mult).then_inc(S["ge"], 1)
                        if c == EC - 1:
                            dve.wait_ge(S["ge"], nth(i * (EC + 1) + EC))
                            dve.wait_ge(S["rbps"], nth(i + 1))
                            v.tensor_tensor(GE[:, c % 2, :], GE[:, c % 2, :], bank[6][:, :], ALU.add).then_inc(S["ge"], 1)
                        dve.wait_ge(S["tp"], nth(k))
                        v.scalar_tensor_tensor(SP[:, c % 2, :], TP[:, c % 2, :], 1.0, bank[2 * (c % 2)][:, :], ALU.add, ALU.mult)\
                            .then_inc(S["sp"], 1)
                    for g in range(GT):
                        t = i * GT + g
                        o = bank[4 + g % 2]
                        dve.wait_ge(S["ops"], nth(t + 1))
                        v.scalar_tensor_tensor(obuf[:, g, :], o[:, 0:DM], 0.25, x[:, t, :], ALU.mult, ALU.add).then_inc(S["res"], 1)
                        dve.wait_ge(S["res"], nth(t + 1))
                        v.scalar_tensor_tensor(x[:, t, :], o[:, DM:2 * DM], zinv[:, 1, g:g + 1], obuf[:, g, :], ALU.mult, ALU.add)\
                            .then_inc(S["out"], 1)
                    ch.leave(BLOCKS)

            dve.wait_ge(in_c, 16 * len(CONSTS))
            ch.do(v.tensor_copy(iotab[:, :], iota[:, :]))
            ch.do(v.tensor_scalar(small[:, 0:25], small[:, 0:25], 0.5, None, ALU.mult))
            ch.do(v.memset(U[:, :, 0:TAPS - 1], 0.0))
            v.memset(state[:, :], 0.0).then_inc(prep, 1)
            v.tensor_copy(selb[:, :, :], sel[0:72, 0:EC, :]).then_inc(prep, 1)
            dve.wait_ge(prep, 2)
            ch.wait()
            ffn(0)

            S = att_s
            dve.wait_ge(in_a, 16 * len(ATTNW))
            for k in range(CC):
                v.tensor_scalar(wo[:, k, :], wo[:, k, :], normw[:, k:k + 1], None, ALU.mult).then_inc(prep, 1)
            dve.wait_ge(S["eu"], nth(1))
            ch.do(v.tensor_scalar(negA[:, :], negA[:, :], -1.0, None, ALU.mult))
            ch.wait()
            dve.wait_ge(ffn_s[0]["out"], nth(TILES))
            ATT = NORM + CONVC * TAPS - CONVC + 5 + SERIES - 1 + 3 + 2 * GT + 1 + RSQRT
            with dve.Fori(0, BLOCKS) as i:
                ch.enter(i, ATT)
                normalize(i, S)

                def conv_silu(c):
                    dve.wait_ge(S["tc"], nth(i * CONVC + (c + 1)))
                    for h, dst in enumerate([xc[:, c, :]] if c < CC else [BTt[:, :], CTt[:, :]]):
                        r = slice(0, P) if c < CC else slice(NS * h, NS * (h + 1))
                        v.scalar_tensor_tensor(dst, TC[r, c % 2, :], 1.0, acc[r, c % 2, :], ALU.add, ALU.mult)\
                            .then_inc(S["xc"], 1)

                raw, ab, u1, s1, s2, pl = (sp[:, n, :] for n in range(6))
                for c in range(CONVC):
                    dve.wait_ge(S["u"], nth(i * CONVC + (c + 1)))
                    if c >= 2:
                        dve.wait_ge(S["xc"], nth(i * (CONVC + 1) + (c - 1)))
                    ch.do(v.tensor_scalar(acc[:, c % 2, :], U[:, c, 3:3 + BT], convw[:, c, 3:4], convb[:, c:c + 1], ALU.mult, ALU.add))
                    for k in (2, 1, 0):
                        ch.wait()
                        w = v.scalar_tensor_tensor(acc[:, c % 2, :], U[:, c, k:k + BT], convw[:, c, k:k + 1], acc[:, c % 2, :],
                                                   ALU.mult, ALU.add)
                        if k:
                            ch.do(w)
                        else:
                            w.then_inc(S["conv"], 1)
                    if c:
                        conv_silu(c - 1)
                    else:
                        dve.wait_ge(S["dtps"], nth(i + 1))
                        v.tensor_tensor(raw.rearrange("p (g h) -> p g h", h=NH),
                                        bank[7][:, 0:GT * NH].rearrange("p (g h) -> p g h", h=NH),
                                        dtb.unsqueeze(1).to_broadcast([P, GT, NH]), ALU.add).then_inc(S["raw"], 1)
                        dve.wait_ge(S["raw"], nth(i + 1))
                        v.scalar_tensor_tensor(ab, raw, -1.0, raw, ALU.mult, ALU.max).then_inc(S["ab"], 1)
                conv_silu(CONVC - 1)
                dve.wait_ge(S["eu"], nth(i + 2))
                ch.do(v.tensor_scalar(s1, u1, 2.0, None, ALU.add))
                ch.wait()
                ch.do(v.reciprocal(s1, s1))
                ch.wait()
                ch.do(v.tensor_tensor(s1, s1, u1, ALU.mult))
                ch.wait()
                ch.do(v.tensor_tensor(s2, s1, s1, ALU.mult))
                ch.wait()
                ch.do(v.tensor_scalar(pl, s2, 1.0 / (2 * SERIES + 1), None, ALU.mult))
                for n in range(SERIES - 1, 0, -1):
                    ch.wait()
                    ch.do(v.scalar_tensor_tensor(pl, pl, 1.0 / (2 * n + 1), s2, ALU.add, ALU.mult))
                ch.wait()
                ch.do(v.scalar_tensor_tensor(pl, pl, 1.0, s1, ALU.add, ALU.mult))
                ch.do(v.tensor_scalar(raw, raw, 0.0, None, ALU.max))
                ch.wait()
                ch.do(v.scalar_tensor_tensor(dt[:, :, :].rearrange("p g h -> p (g h)"), pl, 2.0, raw, ALU.mult, ALU.add))
                ch.wait()
                v.tensor_tensor(a[:, :, :], dt[:, :, :], negA[:, :].unsqueeze(1).to_broadcast([P, GT, NH]), ALU.mult)\
                    .then_inc(S["a"], 1)
                for g in range(GT):
                    k = i * GT + (g + 1)
                    dve.wait_ge(S["tz"], nth(k))
                    v.scalar_tensor_tensor(SZ[:, :], Tz[:, :], 1.0, bank[3][:, :], ALU.add, ALU.mult).then_inc(S["sz"], 1)
                    dve.wait_ge(S["cbps"], nth(k))
                    v.tensor_tensor(CBm[:, :], bank[7][:, 0:P], tri_incl, ALU.mult).then_inc(S["cbm"], 1)
                    dve.wait_ge(S["cbm"], nth(k))
                    dve.wait_ge(S["lx"], nth(i * (2 * GT) + (2 * g + 2)))
                    dve.wait_ge(S["ydps"], nth(k - 1))
                    v.tensor_tensor(M[:, :, :], Lx[:, :, :], CBm[:, :].unsqueeze(1).to_broadcast([P, NH, P]), ALU.mult)\
                        .then_inc(S["m"], 1)
                    dve.wait_ge(S["offps"], nth(k))
                    dve.wait_ge(S["decays"], nth(i + 1))
                    v.tensor_tensor(hb(y1[:, :]), hb(bank[4][:, :]), per_head(decays[:, 0, g, :]), ALU.mult)\
                        .then_inc(S["yoff"], 1)
                    ch.do(v.tensor_tensor(hb(state[:, :]), hb(state[:, :]), per_head(decays[0:NS, 2, g, :], NS), ALU.mult))
                    ch.wait()
                    dve.wait_ge(S["stps"], nth(k))
                    v.tensor_tensor(state[:, :], state[:, :], bank[5][0:NS, :], ALU.add).then_inc(S["state"], 1)
                    dve.wait_ge(S["ydps"], nth(k))
                    dve.wait_ge(S["yoff"], nth(k))
                    v.tensor_tensor(y1[:, :], y1[:, :], bank[6][:, :], ALU.add).then_inc(S["yadd"], 1)
                    dve.wait_ge(S["yadd"], nth(k))
                    dve.wait_ge(S["xD"], nth(k))
                    ch.do(v.tensor_tensor(y1[:, :], y1[:, :], xD[:, :], ALU.add))
                    ch.wait()
                    dve.wait_ge(S["sz"], nth(k))
                    dve.wait_ge(S["ss"], nth(k - 1))
                    dve.wait_ge(S["ytps"], nth(k - 1))
                    v.tensor_tensor(yg[:, :], y1[:, :], SZ[:, :], ALU.mult).then_inc(S["yg"], 1)
                dve.wait_ge(S["ss"], nth(i * GT + GT))
                ch.do(v.tensor_scalar(varc[:, :], ss[:, :], 0.25 / DI, RMS_EPS, ALU.mult, ALU.add))
                ch.wait()
                rsqrt(varc[:, :], rstd[:, :], 0.5)
                dve.wait_ge(S["o"], nth(i * GT + GT))
                for g in range(GT):
                    v.scalar_tensor_tensor(x[:, i * GT + g, :], obuf[:, g, :], rstd[:, g:g + 1], x[:, i * GT + g, :],
                                           ALU.mult, ALU.add).then_inc(S["x1"], 1)
                ch.leave(BLOCKS)
            dve.wait_ge(S["x1"], nth(TILES))
            ffn(1)

        @block.scalar
        def _(act):
            s = nc.scalar
            credit(act, "act")

            def ffn(L):
                S = ffn_s[L]
                for side in range(2):
                    with act.Fori(0, BLOCKS // 2) as j:
                        i = j + side * (BLOCKS // 2)
                        for k in range(KD):
                            act.wait_ge(S["hps"], nth(i * KD + (k + 1)))
                            s.activation(hT[:, k, ds(i * BT, BT)], bank[k][:, :], ACT.Copy).then_inc(S["h"], 1)
                        act.wait_ge(S["qps"], nth(i + 1))
                        qv = qT[NS * side:NS * (side + 1), :].rearrange("p (m two) -> p two m", two=2)
                        for half in range(2):
                            s.activation(qv[:, half, ds(j * BT, BT)], bank[2][NS * half:NS * (half + 1), :], ACT.Copy)\
                                .then_inc(S["q"], 1)
                with act.Fori(0, BLOCKS) as i:
                    act.wait_ge(S["rps"], nth(i + 1))
                    act.wait_ge(S["rtps"], nth(i))
                    s.activation(rT[:, :], bank[6][:, :], ACT.Copy).then_inc(S["rT"], 1)
                    act.wait_ge(S["rtps"], nth(i + 1))
                    act.wait_ge(S["tt"], nth(i))
                    s.activation(rtok[:, :, :].rearrange("p g k -> p (g k)"), bank[7][:, :], ACT.Copy).then_inc(S["rtok"], 1)
                    for f in range(FC):
                        k = i * FC + (f + 1)
                        act.wait_ge(S["gps"], nth(k))
                        act.wait_ge(S["sg"], nth(k - 2))
                        s.activation(TG[:, f % 2, :], bank[2 * (f % 2)][:, :], ACT.Tanh, scale=0.5).then_inc(S["tg"], 1)
                        if f == 2:
                            act.wait_ge(S["dxy"], nth(i + 1))
                            s.activation(exy[:, :, :], dxy[:, :, :], ACT.Exp).then_inc(S["exy"], 1)
                    act.wait_ge(S["ttps"], nth(i + 1))
                    act.wait_ge(S["rbps"], nth(i))
                    act.wait_ge(S["lps"], nth(i * EC))
                    s.activation(TTs[:, :], bank[6][0:73, :], ACT.Copy).then_inc(S["tts"], 1)
                    act.wait_ge(S["ddps"], nth(i + 1))
                    act.wait_ge(S["dps"], nth(i * EC))
                    s.activation(DDs[:, :], bank[7][0:72, :], ACT.Copy).then_inc(S["dds"], 1)
                    for c in range(EC):
                        k = i * EC + (c + 1)
                        act.wait_ge(S["pps"], nth(k))
                        act.wait_ge(S["sp"], nth(k - 2))
                        s.activation(TP[:, c % 2, :], bank[2 * (c % 2)][:, :], ACT.Tanh, scale=0.5).then_inc(S["tp"], 1)
                        act.wait_ge(S["lps"], nth(k))
                        act.wait_ge(S["ge"], nth(i * (EC + 1) + (c - 1 if c >= 2 else c - 2)))
                        s.activation(E[:, c % 2, :], bank[2 * (c % 2) + 1][:, :], ACT.Exp).then_inc(S["e"], 1)

            act.wait_ge(in_c, 16 * len(CONSTS))
            s.activation(negA[:, :], alog, ACT.Exp).then_inc(att_s["eu"], 1)
            ffn(0)
            S = att_s
            with act.Fori(0, BLOCKS) as i:
                for k in range(KD):
                    act.wait_ge(S["hps"], nth(i * KD + (k + 1)))
                    s.activation(hTb[:, k, :], bank[k][:, :], ACT.Copy).then_inc(S["h"], 1)
                act.wait_ge(S["hist"], nth(i))
                for c in range(CONVC):
                    act.wait_ge(S["pps"], nth(i * CONVC + (c + 1)))
                    s.activation(U[:, c, 3:3 + BT], bank[c % 2][:, :], ACT.Copy).then_inc(S["u"], 1)
                for c in range(CONVC):
                    act.wait_ge(S["conv"], nth(i * CONVC + (c + 1)))
                    s.activation(TC[:, c % 2, :], acc[:, c % 2, :], ACT.Tanh).then_inc(S["tc"], 1)
                    if c == 0:
                        act.wait_ge(S["ab"], nth(i + 1))
                        s.activation(sp[:, 2, :], sp[:, 1, :], ACT.Exp, scale=-1.0).then_inc(S["eu"], 1)
                act.wait_ge(S["cums"], nth(i + 1))
                s.activation(decays[:, :, :, :].rearrange("p w g h -> p (w g h)"), bank[7][:, 0:3 * GT * NH], ACT.Exp)\
                    .then_inc(S["decays"], 1)
                for g in range(GT):
                    k = i * GT + (g + 1)
                    act.wait_ge(S["zps"], nth(k))
                    act.wait_ge(S["sz"], nth(k - 1))
                    s.activation(Tz[:, :], bank[3][:, :], ACT.Tanh, scale=0.5).then_inc(S["tz"], 1)
                    act.wait_ge(S["xps"], nth(k))
                    act.wait_ge(S["xdt"], nth(k - 1))
                    act.wait_ge(S["xD"], nth(k - 1))
                    s.activation(xtok[:, :], bank[2][:, :], ACT.Copy).then_inc(S["xt"], 1)
                    act.wait_ge(S["cbps"], nth(k))
                    act.wait_ge(S["cbm"], nth(k))
                    act.wait_ge(S["stps"], nth(k - 1))
                    s.activation(Btok[:, :], bank[7][:, P:P + NS], ACT.Copy).then_inc(S["bt"], 1)
                    for n in range(2):
                        act.wait_ge(S["segps"], nth(i * (2 * GT) + (2 * g + n + 1)))
                        act.wait_ge(S["m"], nth(k - 1))
                        s.activation(Lx[:, 4 * n:4 * n + 4, :].rearrange("p h l -> p (h l)"), bank[4 + n][:, :], ACT.Exp)\
                            .then_inc(S["lx"], 1)
                    act.wait_ge(S["yg"], nth(k))
                    s.activation(sq[:, :], yg[:, :], ACT.Square, accum_out=ss[:, g:g + 1]).then_inc(S["ss"], 1)
                    act.wait_ge(S["ytps"], nth(k))
                    s.activation(ygT[:, :, :].rearrange("p c t -> p (c t)"), bank[2][:, :], ACT.Copy).then_inc(S["yt"], 1)
                    act.wait_ge(S["ops"], nth(k))
                    s.activation(obuf[:, g, :], bank[3][:, 0:DM], ACT.Copy).then_inc(S["o"], 1)
            ffn(1)

        @block.gpsimd
        def _(pool):
            gp = nc.gpsimd
            credit(pool, "pool")

            def ffn(L):
                S = ffn_s[L]
                with pool.Fori(0, BLOCKS) as i:
                    pool.wait_ge(S["out"], nth(i * GT))
                    for c in range(EC):
                        pool.wait_ge(S["ge"], nth(i * (EC + 1) + (c + 1 if c < EC - 1 else EC + 1)))
                        pool.wait_ge(S["sp"], nth(i * EC + (c + 1)))
                        gp.tensor_tensor(coef[:, c, :], SP[:, c % 2, :], GE[:, c % 2, :], ALU.mult).then_inc(S["coef"], 1)

            ffn(0)
            S = att_s
            with pool.Fori(0, BLOCKS) as i:
                pool.wait_ge(S["conv"], nth(i * CONVC + CONVC))
                pool.sem_inc(passed, 1)
                gp.tensor_copy(U[:, :, 0:TAPS - 1], U[:, :, BT:BT + TAPS - 1]).then_inc(S["hist"], 1)
                pool.wait_ge(S["a"], nth(i + 1))
                for g in range(GT):
                    k = i * GT + (g + 1)
                    pool.wait_ge(S["segps"], nth(i * (2 * GT) + 2 * g))
                    gp.tensor_tensor(adiag[:, :, :], tri_incl.unsqueeze(1).to_broadcast([P, NH, P]),
                                     a[:, g, :].unsqueeze(2).to_broadcast([P, NH, P]), ALU.mult).then_inc(S["ad"], 1)
                    pool.wait_ge(S["xt"], nth(k))
                    pool.wait_ge(S["ydps"], nth(k - 1))
                    gp.tensor_tensor(hb(xdt[:, :]), hb(xtok[:, :]), per_head(dt[:, g, :]), ALU.mult).then_inc(S["xdt"], 1)
                    pool.wait_ge(S["xdt"], nth(k))
                    pool.wait_ge(S["decays"], nth(i + 1))
                    pool.wait_ge(S["stps"], nth(k - 1))
                    gp.tensor_tensor(hb(xdd[:, :]), hb(xdt[:, :]), per_head(decays[:, 1, g, :]), ALU.mult).then_inc(S["xdd"], 1)
                    pool.wait_ge(S["yg"], nth(k - 1))
                    gp.tensor_tensor(hb(xD[:, :]), hb(xtok[:, :]), per_head(dpar), ALU.mult).then_inc(S["xD"], 1)
            ffn(1)

        @block.tensor
        def _(pe):
            credit(pe, "pe")

            def mm(out, pairs):
                for n, (lhsT, rhs) in enumerate(pairs):
                    last = nc.tensor.matmul(out, lhsT, rhs, start=n == 0, stop=n == len(pairs) - 1)
                return last

            def transposes(outs_ins):
                for o, t in outs_ins:
                    n = t.shape[0]
                    last = nc.tensor.transpose(o, t, ident[0:n, 0:n])
                return last

            def cols(t, g):
                return t[:, P * g:P * (g + 1)]

            def ffn(L):
                S = ffn_s[L]
                with pe.Fori(0, BLOCKS) as i:
                    pe.wait_ge(S["xn"], nth(i * GT + GT))
                    for k in range(KD):
                        pe.wait_ge(S["h"], nth(i * KD + (k - 1)))
                        transposes([(cols(bank[k], g), cols(xn[:, g, :], k)) for g in range(GT)]).then_inc(S["hps"], 1)
                    pe.wait_ge(S["h"], nth(i * KD + KD))
                    pe.wait_ge(S["q"], nth(i * 2))
                    mm(bank[2][:, :], [(wq[:, k, :], hT[:, k, ds(i * BT, BT)]) for k in range(KD)]).then_inc(S["qps"], 1)
                pe.wait_ge(S["q"], nth(2 * BLOCKS))
                with pe.Fori(0, BLOCKS) as i:
                    pe.wait_ge(S["ge"], nth(i * (EC + 1)))
                    mm(bank[6][:, :], [(keys[:, :], qT[:, ds(i * BT, BT)])]).then_inc(S["rps"], 1)
                    pe.wait_ge(S["rT"], nth(i + 1))
                    pe.wait_ge(S["dds"], nth(i))
                    transposes([(cols(bank[7], g), cols(rT, g)) for g in range(GT)]).then_inc(S["rtps"], 1)
                    hblk = [hT[:, k, ds(i * BT, BT)] for k in range(KD)]
                    for f in range(FC):
                        b = 2 * (f % 2)
                        if f < 2:
                            pe.wait_ge(S["sp"], nth(i * EC + (f - 1)))
                            pe.wait_ge(S["e"], nth(i * EC + (f - 1)))
                        else:
                            pe.wait_ge(S["gu"], nth(i * FC + (f - 1)))
                        mm(bank[b][:, :], [(cols(wg[:, k, :], f), hblk[k]) for k in range(KD)]).then_inc(S["gps"], 1)
                        mm(bank[b + 1][:, :], [(cols(wu[:, k, :], f), hblk[k]) for k in range(KD)]).then_inc(S["ups"], 1)
                    pe.wait_ge(S["tt"], nth(i + 1))
                    transposes([(cols(bank[6][0:73, :], g), TT[:, g, :]) for g in range(GT)]).then_inc(S["ttps"], 1)
                    pe.wait_ge(S["rtok"], nth(i + 1))
                    pe.wait_ge(S["dd"], nth(i * GT + GT))
                    transposes([(cols(bank[7][0:72, :], g), DD[:, g, :]) for g in range(GT)]).then_inc(S["ddps"], 1)
                    for c in range(EC):
                        b = 2 * (c % 2)
                        if c < 2:
                            pe.wait_ge(S["gu"], nth(i * FC + (FC - 1 + c)))
                            pe.wait_ge(S["out"], nth(i * GT + (c - 1)))
                        else:
                            pe.wait_ge(S["sp"], nth(i * EC + (c - 1)))
                            pe.wait_ge(S["e"], nth(i * EC + (c - 1)))
                            pe.wait_ge(S["ge"], nth(i * (EC + 1) + (c - 1)))
                        mm(bank[b][:, :], [(cols(de[:, k, :], c), hblk[k]) for k in range(KD)]).then_inc(S["pps"], 1)
                        if c == 0:
                            pe.wait_ge(S["tts"], nth(i + 1))
                            pe.wait_ge(S["dds"], nth(i + 1))
                        mm(bank[b + 1][:, :], [(sel[:, c, :], TTs[:, :])]).then_inc(S["lps"], 1)
                        mm(bank[4 + c % 2][:, :], [(selb[:, c, :], DDs[:, :])]).then_inc(S["dps"], 1)
                    mm(bank[6][:, :], [(sel[:, EC, :], TTs[:, :])]).then_inc(S["rbps"], 1)
                    pe.wait_ge(S["gu"], nth(i * FC + FC))
                    for g in range(GT):
                        o = bank[4 + g % 2]
                        if g < 2:
                            pe.wait_ge(S["ge"], nth(i * (EC + 1) + (g + 3)))
                        else:
                            pe.wait_ge(S["out"], nth(i * GT + (g - 1)))
                        mm(o[:, 0:DM], [(cols(gu[:, f, :], g), wd[:, f, :]) for f in range(FC)])
                        pe.wait_ge(S["coef"], nth(i * EC + EC))
                        mm(o[:, DM:2 * DM], [(cols(coef[:, c, :], g), ue[:, c, :]) for c in range(EC)]).then_inc(S["ops"], 1)

            pe.wait_ge(in_c, 16 * len(CONSTS))
            pe.wait_ge(in_f, 16 * len(FFNW))
            pe.wait_ge(prep, 2)
            ffn(0)

            S = att_s
            pe.wait_ge(in_a, 16 * len(ATTNW))
            pe.wait_ge(prep, 2 + CC)
            with pe.Fori(0, BLOCKS) as i:
                pe.wait_ge(S["xn"], nth(i * GT + GT))
                pe.wait_ge(S["u"], nth(i * CONVC))
                for k in range(KD):
                    transposes([(cols(bank[k], g), cols(xn[:, g, :], k)) for g in range(GT)]).then_inc(S["hps"], 1)
                pe.wait_ge(S["h"], nth(i * KD + KD))
                for c in range(CONVC):
                    if c >= 2:
                        pe.wait_ge(S["u"], nth(i * CONVC + (c - 1)))
                    mm(bank[c % 2][:, :], [(cols(win[:, k, :], c), hTb[:, k, :]) for k in range(KD)]).then_inc(S["pps"], 1)
                pe.wait_ge(S["cbm"], nth(i * GT))
                pe.wait_ge(S["bt"], nth(i * GT))
                for g in range(GT):
                    last = mm(bank[7][:, NH * g:NH * (g + 1)], [(cols(hTb[:, k, :], g), wdt[:, k, :]) for k in range(KD)])
                last.then_inc(S["dtps"], 1)
                pe.wait_ge(S["a"], nth(i + 1))
                arow = a[:, :, :].rearrange("p g h -> p (g h)")
                for n, w in enumerate((tri_incl, tri_after, ones)):
                    last = mm(bank[7][:, GT * NH * n:GT * NH * (n + 1)], [(w, arow)])
                last.then_inc(S["cums"], 1)
                for g in range(GT):
                    k = i * GT + (g + 1)
                    pe.wait_ge(S["o"], nth(k - 1))
                    mm(bank[3][:, :], [(cols(hTb[:, m, :], g), wz[:, m, :]) for m in range(KD)]).then_inc(S["zps"], 1)
                    if g == 0:
                        pe.wait_ge(S["xc"], nth(i * (CONVC + 1) + CONVC + 1))
                        pe.wait_ge(S["decays"], nth(i + 1))
                    else:
                        pe.wait_ge(S["cbm"], nth(k - 1))
                        pe.wait_ge(S["bt"], nth(k - 1))
                    pe.wait_ge(S["yt"], nth(k - 1))
                    transposes([(cols(bank[2], c), cols(xc[:, c, :], g)) for c in range(CC)]).then_inc(S["xps"], 1)
                    mm(bank[7][:, 0:P], [(cols(BTt, g), cols(CTt, g))])
                    transposes([(bank[7][:, P:P + NS], cols(BTt, g))]).then_inc(S["cbps"], 1)
                    pe.wait_ge(S["ad"], nth(k))
                    pe.wait_ge(S["yoff"], nth(k - 1))
                    pe.wait_ge(S["state"], nth(k - 1))
                    for n in range(2):
                        mm(bank[4 + n][:, :], [(tri_after, adiag[:, 4 * n:4 * n + 4, :].rearrange("p h l -> p (h l)"))])\
                            .then_inc(S["segps"], 1)
                    pe.wait_ge(S["lx"], nth(i * (2 * GT) + (2 * g + 1)))
                    mm(bank[4][:, :], [(cols(CTt, g), state[:, :])]).then_inc(S["offps"], 1)
                    pe.wait_ge(S["lx"], nth(i * (2 * GT) + (2 * g + 2)))
                    pe.wait_ge(S["bt"], nth(k))
                    pe.wait_ge(S["xdd"], nth(k))
                    mm(bank[5][0:NS, :], [(Btok[:, :], xdd[:, :])]).then_inc(S["stps"], 1)
                    pe.wait_ge(S["m"], nth(k))
                    pe.wait_ge(S["xdt"], nth(k))
                    pe.wait_ge(S["yadd"], nth(k - 1))
                    for h in range(NH):
                        last = mm(bank[6][:, HD * h:HD * (h + 1)], [(M[:, h, :], xdt[:, HD * h:HD * (h + 1)])])
                    last.then_inc(S["ydps"], 1)
                    pe.wait_ge(S["yg"], nth(k))
                    pe.wait_ge(S["xt"], nth(k))
                    transposes([(cols(bank[2], c), cols(yg, c)) for c in range(CC)]).then_inc(S["ytps"], 1)
                    pe.wait_ge(S["yt"], nth(k))
                    pe.wait_ge(S["sz"], nth(k))
                    mm(bank[3][:, 0:DM], [(ygT[:, c, :], wo[:, c, :]) for c in range(CC)]).then_inc(S["ops"], 1)
            ffn(1)


def kernel(**inputs):
    import numpy as np
    import concourse.bacc as bacc
    from concourse.bass_utils import run_bass_kernel_spmd

    pre = "L0_attn_"
    w = {k: np.asarray(v) for k, v in inputs.items()}
    f32 = np.float32

    def rows(a, n):
        return np.ascontiguousarray(a.reshape(n, P, -1).transpose(1, 0, 2))

    w_inT = w[pre + "W_in"].T
    k = w["L0_ffn_keys"]
    keys = np.zeros((P, P), f32)
    keys[:NKEY, :NKEY], keys[NKEY:, NKEY:] = k[0], k[1]
    small = np.concatenate([
        w[pre + "conv_w"].reshape(CONVC, P, TAPS).transpose(1, 0, 2).reshape(P, CONVC * TAPS),
        w[pre + "conv_b"].reshape(CONVC, P).T, w[pre + "norm_w"].reshape(CC, P).T,
        np.broadcast_to(w[pre + "dt_bias"], (P, NH)), np.broadcast_to(w[pre + "A_log"], (P, NH)),
        np.broadcast_to(w[pre + "D_param"], (P, NH))], axis=1)
    r = np.arange(P)
    cst = np.stack([r[:, None] == r, r[:, None] <= r, r[:, None] > r, np.ones((P, P), bool)], axis=1).astype(f32)
    sel = np.zeros((NKEY + XKEYS + 1, EC + 1, P), f32)
    for c in range(EC):
        sel[r % NKEY, c, r] = 1
        sel[NKEY + 2 * c + r // NKEY, c, r] = 1
    sel[NKEY + XKEYS, EC, P - 1] = 1
    arrays = {
        "u": w[pre + "u"], "wq": rows(w["L0_ffn_W_q"], KD), "keys": keys,
        "wg": rows(w["L0_ffn_gate_w"], KD), "wu": rows(w["L0_ffn_up_w"], KD), "wd": rows(w["L0_ffn_down_w"], FC),
        "de": rows(w["L0_ffn_down_embed"].T, KD), "ue": rows(w["L0_ffn_up_embed"], EC),
        "win": rows(w_inT[:, DI:DI + XBC], KD), "wz": rows(w_inT[:, :DI], KD), "wdt": rows(w_inT[:, DI + XBC:], KD),
        "wo": rows(w[pre + "W_out"].T, CC), "small": small, "cst": cst, "sel": sel,
        "iota": np.broadcast_to(np.arange(NKEY, dtype=f32), (P, NKEY)),
    }
    arrays = {n: np.ascontiguousarray(a) for n, a in arrays.items()}
    nc = bacc.Bacc("TRN2", target_bir_lowering=False, num_devices=1)
    A = {n: nc.dram_tensor(f"in_{n}", a.shape, mybir.dt.from_np(a.dtype), kind="ExternalInput").ap()
         for n, a in arrays.items()}
    A["out"] = nc.dram_tensor("out", (1, SEQ, DM), mybir.dt.float32, kind="ExternalOutput").ap()
    program(nc, A)
    res = run_bass_kernel_spmd(nc, [{f"in_{n}": a for n, a in arrays.items()}], core_ids=[0])
    return res.results[0]["out"]
```

```python
import concourse.bass as bass
from concourse import mybir
from contextlib import ExitStack

SEQ, DM, P = 2048, 256, 128
TILES = SEQ // P
GT = 4
BLOCKS = TILES // GT
BT = GT * P
AG = 2
GROUPS = TILES // AG
AT = AG * P
KD = DM // P
INTER = 1024
FC = INTER // P
NKEY, TOPK, NEXP = 64, 8, 512
EC = NEXP // P
XKEYS = NEXP // NKEY
DI, NH, HD, NS, TAPS = 512, 8, 64, 64, 4
CC = DI // P
XBC = DI + 2 * NS
CONVC = XBC // P
CORDER = (CONVC - 1, *range(CONVC - 1))
LN_EPS = 1e-5
RMS_EPS = 1e-5
RSQRT_MAGIC = float(0x5F3759DF)
CREDIT = 4
SERIES = 9


def program(nc, A):
    fp32, bf16, f32r = mybir.dt.float32, mybir.dt.bfloat16, mybir.dt.float32r
    i32, u32 = mybir.dt.int32, mybir.dt.uint32
    HI, LO = 0, 1
    ALU, ACT, AX = mybir.AluOpType, mybir.ActivationFunctionType, mybir.AxisListType
    ds = bass.ds
    ctx = ExitStack()
    with ctx:
        def sb(name, shape, dt=fp32):
            return ctx.enter_context(nc.sbuf_tensor(name, shape, dt))

        def sem(name):
            return ctx.enter_context(nc.semaphore(name))

        WORK = {"work": 13820, "workr": 13312}
        work = sb("work", [P, WORK["work"]])
        workr = sb("workr", [P, WORK["workr"]], f32r)
        used = {}

        def part(layer, *shape, split=False):
            pool = "workr" if split else "work"
            n = 1
            for d in shape:
                n *= d
            at = used.get((layer, pool), 0)
            used[layer, pool] = at + n
            assert at + n <= WORK[pool], (layer, pool, at + n)
            v = (workr if split else work)[:, at:at + n]
            names = "abcd"[:len(shape)]
            if len(shape) == 1:
                return v
            return v.rearrange(f"p ({' '.join(names)}) -> p {' '.join(names)}", **dict(zip(names, shape)))

        x = sb("x", [P, TILES, DM])
        wq = sb("wq", [P, 2, KD, P], f32r)
        wg = sb("wg", [P, 2, KD, INTER], f32r)
        wu = sb("wu", [P, 2, KD, INTER], f32r)
        wd = sb("wd", [P, 2, FC, DM], f32r)
        de = sb("de", [P, 2, KD, NEXP], f32r)
        ue = sb("ue", [P, 2, EC, DM], f32r)
        keys = sb("keys", [P, P])
        win = part("att", 2, KD, XBC, split=True)
        wz = part("att", 2, KD, DI, split=True)
        wdt = part("att", 2, KD, NH, split=True)
        wo = sb("wo", [P, CC, DM])
        small = sb("small", [P, 49])
        convw = small[:, 0:20].rearrange("p (c k) -> p c k", k=TAPS)
        convb = small[:, 20:25]
        normw = small[:, 25:29]
        dtb, alog, dcol = small[:, 29:37], small[:, 37:45], small[:, 45:49]
        cst = sb("cst", [P, 4, P])
        ident, tri_incl, tri_after, ones = cst[:, 0, :], cst[:, 1, :], cst[:, 2, :], cst[:, 3, :]
        after_hi = sb("after_hi", [P, P], f32r)
        NSEL = NKEY + XKEYS + 1
        sel = sb("sel", [NSEL, EC + 1, P], f32r)
        selb = sb("selb", [NKEY + XKEYS, EC, P], bf16)
        iota = sb("iota", [P, NKEY])
        iotab = sb("iotab", [P, NKEY], bf16)
        negA = sb("negA", [P, NH])

        xn = part("ffn", 2, GT, DM)
        qT = part("ffn", SEQ)
        stats = sb("stats", [P, TILES, 6])
        mv = sb("mv", [P, TILES, 2])
        rs = sb("rs", [P, 4, TILES])
        varc = sb("varc", [P, TILES])
        rstd = sb("rstd", [P, TILES])
        hT = part("ffn", 2, KD, SEQ, split=True)
        after_norm = used["ffn", "work"]

        TG = part("ffn", 2, BT)
        gu = part("ffn", 2, BT)
        rT = part("ffn", BT)
        rtok = part("ffn", GT, P)
        sxy = sb("sxy", [P, 2, GT, TOPK])
        ixy = sb("ixy", [P, 2, GT, TOPK], u32)
        ixyf = sb("ixyf", [P, 2, GT, TOPK])
        sums = part("ffn", GT, 64)
        best = part("ffn", GT, TOPK)
        rest = part("ffn", GT, 64)
        chosen = part("ffn", GT, 64)
        chosenw = part("ffn", GT, 64)
        dxy = part("ffn", 2 * GT, TOPK)
        exy = part("ffn", 2 * GT, TOPK)
        sxyv = sxy[:, :, :, :].rearrange("p s g k -> p (s g) k")
        exyv = exy[:, :, :].rearrange("p (s g) k -> p s g k", s=2)
        cnt = part("ffn", GT, TOPK)
        rowsum = part("ffn", GT, TOPK)
        clamped = part("ffn", GT, TOPK)
        zsum = part("ffn", GT)
        zinv = part("ffn", GT)
        zlog = part("ffn", GT)
        csum = part("ffn", GT)
        eqx = part("ffn", GT, XKEYS, TOPK)
        onehot = sb("onehot", [P, 2, TOPK, NKEY], bf16)
        TT = part("ffn", GT, NSEL)
        DD = part("ffn", GT, NSEL - 1)
        TTs = part("ffn", 2, BT, split=True)[0:NSEL, :, :]
        DDs = sb("DDs", [NSEL - 1, BT], bf16)

        E = part("ffn", 2, BT)
        TP = part("ffn", 2, BT)
        coef = part("ffn", 2, BT)
        coefs = part("ffn", 2, 2, BT, split=True)
        gus = part("ffn", 2, 2, BT, split=True)

        diagD = sb("diagD", [P, CC, P])
        hTb = part("att", 2, 2, KD * AT, split=True)
        asplit = part("att", 2, 2, AG * NH, split=True)
        adiag = part("att", 2, 2, NH * P, split=True)
        xn_a = part("att", AG, DM)
        U = part("att", 2, TAPS - 1 + AT)
        hist = sb("hist", [P, CONVC, TAPS - 1])
        TC = part("att", 2, AT)
        xc = part("att", 2, CC, AT)
        xB = part("att", AT)
        BTt = part("att", 2, AT)[0:NS, :, :]
        CTt = part("att", 2, AT)[0:NS, :, :]
        sp = part("att", 6, AG * NH)
        dt = part("att", 2, AG, NH)
        a = part("att", 2, AG, NH)
        decays = part("att", 2, 3, AG, NH)
        xtok = part("att", DI)
        xdt = part("att", 2, DI)
        xdd = part("att", DI)
        Btok = part("att", NS)
        Tz = part("att", 2, DI)
        CBm = part("att", P)
        y1 = part("att", 2, DI)
        ss = part("att", 2, AG)
        ygT = part("att", CC, P)
        Lx = part("att", 2, NH, P)
        obuf = part("att", AG, DM)
        state = sb("state", [NS, DI])

        stage, at = {}, after_norm
        for name, t in (("wq", wq), ("sel", sel), ("wu", wu), ("wg", wg), ("wd", wd), ("de", de), ("ue", ue)):
            n = KD * P if name == "wq" else (EC + 1) * P if name == "sel" else t.shape[2] * t.shape[3]
            stage[name] = work[0:t.shape[0], at:at + n]
            at += n
        stage["win"] = work[:, 0:KD * XBC]
        assert KD * XBC <= 2 * GT * DM
        at = WORK["work"] - KD * (DI + NH)
        assert at >= used["ffn", "work"]
        for name, t in (("wz", wz), ("wdt", wdt)):
            n = t.shape[2] * t.shape[3]
            stage[name] = work[:, at:at + n]
            at += n

        bank = [ctx.enter_context(nc.psum_tensor(f"bank{n}", [P, 512], fp32)) for n in range(8)]


        in_x = [sem(f"in_x{n}") for n in range(BLOCKS)]
        in_w = {n: sem(f"in_{n}") for n in stage}
        x_there = sem("x_there")
        in_c, in_k, in_o = sem("in_consts"), sem("in_keys"), sem("in_wo")
        w_hi = sem("weights_hi")
        w_lo = {"v": sem("weights_lo_dve"), "p": sem("weights_lo_pool")}
        prep = sem("constants_prepared")
        out_sent = sem("out_sent")
        dve_done = sem("dve_done")
        passed = sem("passed")
        FFN_SEMS = {
            "pe": ("hps", "qps", "rps", "rtps", "ttps", "ddps", "pps", "lps", "dps", "rbps", "gps", "ups", "ecol", "gcol"),
            "act": ("h", "q", "rT", "rtok", "exy", "zlog", "tts", "dds", "tp", "e", "tg", "guh", "coh"),
            "dve": ("xn", "hl", "dxy", "zs", "tt", "dd", "ttl", "sg", "gu", "ge", "sp", "out"),
            "pool": ("coef", "gul", "col")}
        ATT_SEMS = {
            "pe": ("hps", "pps", "dtps", "cums", "zps", "xps", "cbps", "segps", "ydps", "offps", "stps", "ytps", "ops"),
            "act": ("h", "hist", "u", "tc", "eu", "decays", "lx", "tz", "xt", "bt", "ss", "yt", "o", "ahi"),
            "dve": ("xn", "conv", "xc", "raw", "ab", "a", "alo", "sz", "cbm", "m", "yoff", "yadd", "state", "yg", "x1", "hl"),
            "pool": ("ad", "xdt", "xdd", "dec")}
        ffn_s = [{n: sem(f"f{L}_{n}") for names in FFN_SEMS.values() for n in names} for L in range(2)]
        att_s = {n: sem(f"a_{n}") for names in ATT_SEMS.values() for n in names}

        def credit(eng, who):
            for S in ffn_s:
                for n in FFN_SEMS[who]:
                    eng.sem_inc(S[n], CREDIT)
            for n in ATT_SEMS[who]:
                eng.sem_inc(att_s[n], CREDIT)

        def nth(n):
            return n + CREDIT

        class Chain:

            def __init__(self, eng, s):
                self.eng, self.s, self.before, self.base, self.n = eng, s, 0, 0, 0

            def do(self, ins):
                ins.then_inc(self.s, 1)
                self.n += 1
                return self.n

            def wait(self, n=None):
                self.eng.wait_ge(self.s, self.base + (self.n if n is None else n))

            def enter(self, i, per):
                self.before += self.n
                self.per, self.n = per, 0
                self.base = i * per + self.before

            def leave(self, trips):
                assert self.n == self.per, (self.n, self.per)
                self.before += trips * self.per
                self.base, self.n = self.before, 0

        block = ctx.enter_context(nc.Block())
        xv = A["u"].rearrange("o (t p) d -> p (o t) d", p=P)
        ov = A["out"].rearrange("o (t p) d -> p (o t) d", p=P)
        CONSTS = [("cst", cst), ("small", small), ("iota", iota)]
        SPLITS = [("wq", wq, "v"), ("wu", wu, "p"), ("wg", wg, "v"), ("wd", wd, "p"), ("de", de, "v"), ("ue", ue, "p")]
        SPLITS_A = [("win", win, "v"), ("wz", wz, "v"), ("wdt", wdt, "v")]
        UNITS = [("F", n) for n in range(7)] + [("E", 0), ("F", 7), ("E", 1), ("E", 2), ("E", 3)]
        NU = len(UNITS)
        LAG = 2
        QUERIES = 16
        START = 6
        NORDER = (0, 2, 1, 3)

        def unit(u, i):
            return (*UNITS[u % NU], i + 1 if u >= NU else i)

        def flat(t, w):
            return t[:, w].rearrange("p a b -> p (a b)")

        def full(t):
            return t[tuple(slice(None) for _ in t.shape)]

        def hb(t):
            return t.rearrange("p (h d) -> p h d", d=HD)

        def per_head(t, parts=P):
            return t.unsqueeze(2).to_broadcast([parts, NH, HD])

        def pair(kind, n):
            return 2 * (UNITS.index((kind, n)) % 2)

        def split_lo(eng, unit, who, weights, done):
            for n, (name, t, by) in enumerate(weights):
                if by == who:
                    eng.wait_ge(w_hi, done + n + 1)
                    unit.tensor_tensor(flat(t, LO), stage[name], flat(t, HI).bitcast(fp32), ALU.subtract).then_inc(w_lo[by], 1)

        def wait_split(eng, weights):
            for by, s in w_lo.items():
                eng.wait_ge(s, len([w for w in weights if w[2] == by]))

        @block.sync
        def _(sync):
            for n in range(BLOCKS):
                sync.dma_start(x[:, GT * n:GT * (n + 1), :], xv[:, GT * n:GT * (n + 1), :]).then_inc(in_x[n], 16)
            for name, t in CONSTS:
                sync.dma_start(full(t), A[name]).then_inc(in_c, 16)
            sync.dma_start(keys[:, :], A["keys"]).then_inc(in_k, 16)
            for name, dst in stage.items():
                if name not in ("win", "wz", "wdt"):
                    sync.dma_start(dst, A[name].rearrange("p a b -> p (a b)")).then_inc(in_w[name], 16)
            sync.dma_start(wo[:, :, :], A["wo"]).then_inc(in_o, 16)
            for n in range(BLOCKS):
                sync.wait_ge(in_x[n], 16)
                sync.sem_inc(x_there, 1)
            sync.wait_ge(w_hi, len(SPLITS))
            wait_split(sync, SPLITS)
            sync.wait_ge(ffn_s[0]["hps"], nth(BLOCKS * KD))
            for name in ("win", "wz", "wdt"):
                sync.dma_start(stage[name], A[name].rearrange("p a b -> p (a b)")).then_inc(in_w[name], 16)
            with sync.Fori(0, BLOCKS) as i:
                sync.wait_ge(ffn_s[1]["out"], nth(i * GT + GT))
                sync.dma_start(ov[:, ds(i * GT, GT), :], x[:, ds(i * GT, GT), :]).then_inc(out_sent, 16)
            sync.wait_ge(out_sent, 16 * BLOCKS)

        @block.vector
        def _(dve):
            ch = Chain(dve, dve_done)
            v = nc.vector
            credit(dve, "dve")

            def alone():
                dve.sem_inc(passed, 1)

            def rsqrt(step, var, y, scale):
                vh, w, t, bits = (rs[:, n, 0:var.shape[1]] for n in range(4))
                if step == 0:
                    ch.do(v.tensor_scalar(vh, var, -0.5, None, ALU.mult))
                    return ch.do(v.tensor_scalar(bits.bitcast(i32), var.bitcast(i32), 1, None, ALU.logical_shift_right))
                if step == 1:
                    return ch.do(v.tensor_scalar(w.bitcast(i32), bits.bitcast(i32), -1.0, RSQRT_MAGIC, ALU.mult, ALU.add))
                if step == RSQRT - 1:
                    return ch.do(v.tensor_scalar(y, w, scale, None, ALU.mult))
                if step % 3 == 2:
                    return ch.do(v.tensor_tensor(t, w, w, ALU.mult))
                if step % 3 == 0:
                    return ch.do(v.tensor_tensor(t, t, vh, ALU.mult))
                return ch.do(v.scalar_tensor_tensor(w, t, 1.5, w, ALU.add, ALU.mult))
            RSQRT = 2 + 3 * 3 + 1

            def layer_stats(first):
                if first:
                    for t in range(TILES):
                        if t % GT == 0:
                            dve.wait_ge(x_there, t // GT + 1)
                        ch.do(v.bn_stats(stats[:, t, :], x[:, t, :]))
                ch.wait()
                for t in range(TILES):
                    ch.do(v.bn_aggr(mv[:, t, :], stats[:, t, :]))
                ch.wait()
                ch.do(v.tensor_scalar(varc[:, :], mv[:, :, 1], LN_EPS, None, ALU.add))
                for step in range(RSQRT):
                    ch.wait()
                    rsqrt(step, varc[:, :], rstd[:, :], 1.0)
                ch.wait()

            def normalized(t, xn, tiles, done):
                for g in range(tiles):
                    v.tensor_scalar(xn[:, g, :], x[:, ds(t + g, 1), :].rearrange("p a d -> p (a d)"),
                                    mv[:, ds(t + g, 1), 0:1].rearrange("p a b -> p (a b)"), rstd[:, ds(t + g, 1)],
                                    ALU.subtract, ALU.mult).then_inc(done, 1)

            def sums_of(t, tiles, done):
                dve.wait_ge(done, nth(t + tiles))
                alone()
                for g in range(tiles):
                    ch.do(v.bn_stats(stats[:, t + g, :], x[:, t + g, :]))

            def sq8(t):
                return t.rearrange("p g (a b) -> p g a b", b=TOPK)

            def routing(i, S, part):
                rx, ry = rtok[:, :, 0:NKEY], rtok[:, :, NKEY:P]
                pairs = [P, GT, TOPK, TOPK]
                if part == 0:
                    dve.wait_ge(S["rtok"], nth(i + 1))
                    alone()
                    for s, r in ((0, rx), (1, ry)):
                        for g in range(GT):
                            ch.do(v.max(sxy[:, s, g, :], r[:, g, :]))
                elif part == 1:
                    ch.wait()
                    alone()
                    for s, r in ((0, rx), (1, ry)):
                        for g in range(GT):
                            ch.do(v.max_index(ixy[:, s, g, :], sxy[:, s, g, :], r[:, g, :]))
                    ch.do(v.tensor_tensor(sq8(sums[:, :, :]), sxy[:, 0, :, :].unsqueeze(3).to_broadcast(pairs),
                                          sxy[:, 1, :, :].unsqueeze(2).to_broadcast(pairs), ALU.add))
                    v.tensor_tensor(dxy[:, :, :], sxyv[:, :, :], sxyv[:, :, 0:1].to_broadcast([P, 2 * GT, TOPK]),
                                    ALU.subtract).then_inc(S["dxy"], 1)
                elif part == 2:
                    ch.wait()
                    alone()
                    for g in range(GT):
                        ch.do(v.max(best[:, g, :], sums[:, g, :]))
                    ch.do(v.tensor_copy(ixyf[:, :, :, :], ixy[:, :, :, :]))
                    ch.wait()
                    alone()
                    for g in range(GT):
                        ch.do(v.match_replace(rest[:, g, :], best[:, g, :], sums[:, g, :], -3.0e38))
                elif part == 3:
                    ch.wait()
                    ch.do(v.tensor_tensor(chosen[:, :, :], sums[:, :, :], rest[:, :, :], ALU.not_equal))
                    dve.wait_ge(S["ttps"], nth(i))
                    ch.do(v.tensor_tensor(TT[:, :, 0:NKEY], ry, sxy[:, 1, :, 0:1].to_broadcast([P, GT, NKEY]), ALU.subtract))
                    ch.wait()
                    ch.do(v.tensor_reduce(cnt[:, :, :], sq8(chosen[:, :, :]), AX.X, ALU.add))
                    dve.wait_ge(S["exy"], nth(i + 1))
                    ch.do(v.tensor_tensor(sq8(chosenw[:, :, :]), sq8(chosen[:, :, :]),
                                          exyv[:, 1, :, :].unsqueeze(2).to_broadcast(pairs), ALU.mult))
                elif part == 4:
                    ch.wait()
                    ch.do(v.tensor_reduce(rowsum[:, :, :], sq8(chosenw[:, :, :]), AX.X, ALU.add))
                    ch.wait()
                    ch.do(v.tensor_tensor(rowsum[:, :, :], rowsum[:, :, :], exyv[:, 0, :, :], ALU.mult))
                    ch.wait()
                    v.tensor_reduce(zsum[:, :], rowsum[:, :, :], AX.X, ALU.add).then_inc(S["zs"], 1)
                    ch.do(v.scalar_tensor_tensor(clamped[:, :, :], ixyf[:, 0, :, :], float(XKEYS), rowsum[:, :, :],
                                                 ALU.is_ge, ALU.mult))
                    ch.wait()
                    dve.wait_ge(S["zs"], nth(i + 1))
                    ch.do(v.reciprocal(zinv[:, :], zsum[:, :]))
                    ch.do(v.tensor_reduce(csum[:, :], clamped[:, :, :], AX.X, ALU.add))
                elif part == 5:
                    ch.wait()
                    ch.do(v.tensor_tensor(TT[:, :, NSEL - 1], csum[:, :], zinv[:, :], ALU.mult))
                    ch.do(v.tensor_tensor(eqx[:, :, :, :], ixyf[:, 0, :, :].unsqueeze(2).to_broadcast([P, GT, XKEYS, TOPK]),
                                          iota[:, 0:XKEYS].unsqueeze(1).unsqueeze(3).to_broadcast([P, GT, XKEYS, TOPK]),
                                          ALU.is_equal))
                    ch.wait()
                    ch.do(v.tensor_tensor(eqx[:, :, :, :], eqx[:, :, :, :],
                                          cnt[:, :, :].unsqueeze(2).to_broadcast([P, GT, XKEYS, TOPK]), ALU.mult))
                    ch.wait()
                    dve.wait_ge(S["ddps"], nth(i))
                    ch.do(v.tensor_reduce(DD[:, :, NKEY:NKEY + XKEYS], eqx[:, :, :, :], AX.X, ALU.add))
                    dve.wait_ge(S["zlog"], nth(i + 1))
                    ch.do(v.tensor_tensor(zlog[:, :], zlog[:, :], sxy[:, 0, :, 0], ALU.add))
                    ch.wait()
                    v.tensor_tensor(TT[:, :, NKEY:NKEY + XKEYS], rx[:, :, 0:XKEYS],
                                    zlog[:, :].unsqueeze(2).to_broadcast([P, GT, XKEYS]), ALU.subtract).then_inc(S["tt"], 1)
                else:
                    g = part - 6
                    dve.wait_ge(S["ddps"], nth(i))
                    dve.wait_ge(S["dd"], nth(i * GT + (g - 1)))
                    for b in range(TOPK):
                        ch.do(v.tensor_scalar(onehot[:, g % 2, b, :], iotab[:, :], ixyf[:, 1, g, b:b + 1], float(TOPK - b),
                                              ALU.is_equal, ALU.mult))
                    ch.wait()
                    v.tensor_reduce(DD[:, g, 0:NKEY], onehot[:, g % 2, :, :].rearrange("p b j -> p j b"), AX.X, ALU.add)\
                        .then_inc(S["dd"], 1)
            ROUTE = 2 * GT + 2 * GT + 1 + 2 * GT + 1 + 4 + 5 + 5 + GT * TOPK

            def hidden(i, S, f):
                k = i * FC + (f + 1)
                dve.wait_ge(S["tg"], nth(k))
                v.scalar_tensor_tensor(TG[:, f % 2, :], TG[:, f % 2, :], 1.0, bank[pair("F", f)][:, :], ALU.add, ALU.mult)\
                    .then_inc(S["sg"], 1)
                dve.wait_ge(S["sg"], nth(k))
                dve.wait_ge(S["ups"], nth(k))
                dve.wait_ge(S["gul"], nth(k - 2))
                v.tensor_tensor(gu[:, f % 2, :], TG[:, f % 2, :], bank[pair("F", f) + 1][:, :], ALU.mult).then_inc(S["gu"], 1)

            def experts(i, S, c):
                k = i * EC + (c + 1)
                dve.wait_ge(S["dps"], nth(k))
                dve.wait_ge(S["e"], nth(k))
                v.scalar_tensor_tensor(E[:, c % 2, :], bank[6 + c % 2][:, :], float(TOPK), E[:, c % 2, :],
                                       ALU.is_gt, ALU.mult).then_inc(S["ge"], 1)
                if c == EC - 1:
                    dve.wait_ge(S["ge"], nth(i * (EC + 1) + EC))
                    dve.wait_ge(S["rbps"], nth(i + 1))
                    v.tensor_tensor(E[:, c % 2, :], E[:, c % 2, :], bank[6][:, :], ALU.add).then_inc(S["ge"], 1)
                dve.wait_ge(S["tp"], nth(k))
                v.scalar_tensor_tensor(TP[:, c % 2, :], TP[:, c % 2, :], 1.0, bank[pair("E", c)][:, :], ALU.add, ALU.mult)\
                    .then_inc(S["sp"], 1)

            def query_lo(i, S):
                dve.wait_ge(S["tts"], nth(i + 1))
                v.tensor_tensor(TTs[:, LO, :], bank[6][0:NSEL, :], TTs[:, HI, :].bitcast(fp32), ALU.subtract).then_inc(S["ttl"], 1)

            def step(u, i, S):
                kind, n, j = unit(u, i)
                (hidden if kind == "F" else experts)(j, S, n)

            PARTS = {6: (0,), 7: (1,), 8: (2,), 9: (3,), 10: (4,), 11: (6,), 12: (5,), 13: (7,), 14: (8,), 15: (9,)}
            PARTS0 = {0: (2,), 1: (3,), 2: (4, 6), 3: (5, 7), 4: (8,), 5: (9,)}

            def ffn_block(i, S, more, L):
                for u in range(START, NU + START * more):
                    step(u, i, S)
                    if u == NU + LAG - 1:
                        finished(i, S, L)
                    if more:
                        for part in PARTS.get(u, ()):
                            routing(i + 1, S, part)
                        if u == QUERIES:
                            query_lo(i + 1, S)
                if not more:
                    finished(i, S, L)

            def finished(i, S, L):
                for g in range(GT):
                    t = i * GT + g
                    if g == 0:
                        dve.wait_ge(S["ecol"], nth(i * EC + EC))
                    v.scalar_tensor_tensor(x[:, t, :], bank[4 + g // 2][:, DM * (g % 2):DM * (g % 2 + 1)], 0.25, x[:, t, :],
                                           ALU.mult, ALU.add).then_inc(S["out"], 1)
                if L == 0:
                    sums_of(i * GT, GT, S["out"])

            def constants():
                dve.wait_ge(in_c, 16 * len(CONSTS))
                ch.do(v.tensor_copy(iotab[:, :], iota[:, :]))
                ch.do(v.tensor_scalar(small[:, 0:25], small[:, 0:25], 0.5, None, ALU.mult))
                for c in range(CC):
                    ch.do(v.tensor_scalar(diagD[:, c, :], ident, dcol[:, c:c + 1], None, ALU.mult))
                v.tensor_copy(after_hi[:, :], tri_after).then_inc(prep, 1)
                v.memset(hist[:, :, :], 0.0).then_inc(prep, 1)
                v.memset(state[:, :], 0.0).then_inc(prep, 1)
                dve.wait_ge(in_w["sel"], 16)
                selw = stage["sel"].rearrange("p (c q) -> p c q", q=P)
                v.tensor_copy(selb[:, :, :], selw[0:NSEL - 1, 0:EC, :]).then_inc(prep, 1)
                v.tensor_copy(sel[:, :, :], selw).then_inc(prep, 1)
                dve.wait_ge(prep, 5)
                ch.wait()
                split_lo(dve, v, "v", SPLITS[:1], 0)

            def ffn(L):
                S = ffn_s[L]
                layer_stats(L == 0)
                if L == 0:
                    constants()
                for n, i in enumerate(NORDER):
                    dve.wait_ge(S["hps"], nth((n - 1) * KD))
                    normalized(i * GT, xn[:, n % 2, :, :], GT, S["xn"])
                    if n % 2:
                        for m in (n - 1, n):
                            for k in range(KD):
                                dve.wait_ge(S["h"], nth(m * KD + k + 1))
                                v.tensor_tensor(hT[:, LO, k, BT * NORDER[m]:BT * (NORDER[m] + 1)], bank[2 * (m % 2) + k][:, :],
                                                hT[:, HI, k, BT * NORDER[m]:BT * (NORDER[m] + 1)].bitcast(fp32), ALU.subtract)\
                                    .then_inc(S["hl"], 1)
                if L == 0:
                    split_lo(dve, v, "v", SPLITS[1:], 1)
                    wait_split(dve, SPLITS)
                for part in (0, 1):
                    routing(0, S, part)
                for u in range(START):
                    step(u, 0, S)
                    for part in PARTS0[u]:
                        routing(0, S, part)
                query_lo(0, S)
                with dve.Fori(0, BLOCKS - 1) as i:
                    ch.enter(i, ROUTE + (GT if L == 0 else 0))
                    ffn_block(i, S, True, L)
                    ch.leave(BLOCKS - 1)
                ffn_block(BLOCKS - 1, S, False, L)

            ffn(0)

            S = att_s
            dve.wait_ge(ffn_s[0]["out"], nth(TILES))
            split_lo(dve, v, "v", SPLITS_A, len(SPLITS))
            dve.wait_ge(in_o, 16)
            for k in range(CC):
                v.tensor_scalar(wo[:, k, :], wo[:, k, :], normw[:, k:k + 1], None, ALU.mult).then_inc(prep, 1)
            dve.wait_ge(S["eu"], nth(1))
            ch.do(v.tensor_scalar(negA[:, :], negA[:, :], -1.0, None, ALU.mult))
            ch.wait()
            layer_stats(False)

            raw, ab, u1, s1, s2, pl = (sp[:, n, :] for n in range(6))
            SOFTPLUS = 5 + (SERIES - 1) + 3

            def softplus(step, f, q):
                if step == 0:
                    dve.wait_ge(S["eu"], nth(f + 2))
                    return ch.do(v.tensor_scalar(s1, u1, 2.0, None, ALU.add))
                if step == 1:
                    return ch.do(v.reciprocal(s1, s1))
                if step == 2:
                    return ch.do(v.tensor_tensor(s1, s1, u1, ALU.mult))
                if step == 3:
                    return ch.do(v.tensor_tensor(s2, s1, s1, ALU.mult))
                if step == 4:
                    return ch.do(v.tensor_scalar(pl, s2, 1.0 / (2 * SERIES + 1), None, ALU.mult))
                if step < 4 + SERIES:
                    return ch.do(v.scalar_tensor_tensor(pl, pl, 1.0 / (2 * (4 + SERIES - step) + 1), s2, ALU.add, ALU.mult))
                if step == 4 + SERIES:
                    return ch.do(v.scalar_tensor_tensor(pl, pl, 1.0, s1, ALU.add, ALU.mult))
                if step == 5 + SERIES:
                    return ch.do(v.tensor_scalar(raw, raw, 0.0, None, ALU.max))
                return ch.do(v.scalar_tensor_tensor(dt[:, q, :, :].rearrange("p g h -> p (g h)"), pl, 2.0, raw, ALU.mult, ALU.add))

            def conv(f, q, p, between=None):
                c = CORDER[p]
                dst = xB[:, :] if c == CC else xc[:, q, c, :]
                dve.wait_ge(S["u"], nth(f * CONVC + (p + 1)))
                for k in range(TAPS - 2, -1, -1):
                    if k < TAPS - 2:
                        ch.wait(last)
                    w = v.scalar_tensor_tensor(dst, U[:, p % 2, k:k + AT], convw[:, c, k:k + 1], dst, ALU.mult, ALU.add)
                    if k:
                        last = ch.do(w)
                    else:
                        w.then_inc(S["conv"], 1)
                    if between:
                        between()

            def conv_silu(f, q, p):
                c = CORDER[p]
                dve.wait_ge(S["tc"], nth(f * CONVC + (p + 1)))
                if c < CC:
                    v.scalar_tensor_tensor(xc[:, q, c, :], TC[:, p % 2, :], 1.0, xc[:, q, c, :], ALU.add, ALU.mult).then_inc(S["xc"], 1)
                    return
                ch.do(v.scalar_tensor_tensor(BTt[:, q, :], TC[0:NS, p % 2, :], 1.0, xB[0:NS, :], ALU.add, ALU.mult))
                v.scalar_tensor_tensor(CTt[:, q, :], TC[NS:P, p % 2, :], 1.0, xB[NS:P, :], ALU.add, ALU.mult).then_inc(S["xc"], 1)

            class Steps:

                def __init__(self, step, count, *args):
                    self.step, self.count, self.args, self.n, self.last = step, count, args, 0, None

                def __call__(self):
                    if self.n < self.count:
                        if self.last is not None:
                            ch.wait(self.last)
                        self.last = self.step(self.n, *self.args)
                        self.n += 1

            def lo_of(f, q):
                dve.wait_ge(S["h"], nth(f + 1))
                v.tensor_tensor(hTb[:, q, LO, :], bank[0][:, :], hTb[:, q, HI, :].bitcast(fp32), ALU.subtract).then_inc(S["hl"], 1)

            def scan_in(k):
                dve.wait_ge(S["cbps"], nth(k))
                dve.wait_ge(S["m"], nth(k - 1))
                v.tensor_tensor(CBm[:, :], bank[7][:, 0:P], tri_incl, ALU.mult).then_inc(S["cbm"], 1)

            def gate(k, g):
                dve.wait_ge(S["tz"], nth(k))
                v.scalar_tensor_tensor(Tz[:, g, :], Tz[:, g, :], 1.0, bank[1][:, :], ALU.add, ALU.mult).then_inc(S["sz"], 1)

            def weights_of(k, g):
                dve.wait_ge(S["cbm"], nth(k))
                dve.wait_ge(S["lx"], nth(2 * k))
                v.tensor_tensor(Lx[:, g, :, :], Lx[:, g, :, :], CBm[:, :].unsqueeze(1).to_broadcast([P, NH, P]), ALU.mult)\
                    .then_inc(S["m"], 1)

            def from_before(k, b, q, g, between):
                dve.wait_ge(S["offps"], nth(k))
                dve.wait_ge(S["decays"], nth(b + 1))
                dve.wait_ge(S["ss"], nth(k - 2))
                dve.wait_ge(S["ytps"], nth(k - 2))
                v.tensor_tensor(hb(y1[:, g, :]), hb(bank[4][:, :]), per_head(decays[:, q, 0, g, :]), ALU.mult)\
                    .then_inc(S["yoff"], 1)
                between()
                dve.wait_ge(S["dec"], nth(k))
                dve.wait_ge(S["stps"], nth(k))
                v.tensor_tensor(state[:, :], state[:, :], bank[5][0:NS, :], ALU.add).then_inc(S["state"], 1)

            def gated(k, g):
                dve.wait_ge(S["ydps"], nth(k))
                dve.wait_ge(S["yoff"], nth(k))
                v.tensor_tensor(y1[:, g, :], y1[:, g, :], bank[6][:, :], ALU.add).then_inc(S["yadd"], 1)
                dve.wait_ge(S["yadd"], nth(k))
                dve.wait_ge(S["sz"], nth(k))
                v.tensor_tensor(y1[:, g, :], y1[:, g, :], Tz[:, g, :], ALU.mult).then_inc(S["yg"], 1)

            def raw_dt(f):
                dve.wait_ge(S["dtps"], nth(f + 1))
                v.tensor_tensor(raw.rearrange("p (g h) -> p g h", h=NH),
                                bank[3][:, 0:AG * NH].rearrange("p (g h) -> p g h", h=NH),
                                dtb.unsqueeze(1).to_broadcast([P, AG, NH]), ALU.add).then_inc(S["raw"], 1)
                dve.wait_ge(S["raw"], nth(f + 1))
                v.scalar_tensor_tensor(ab, raw, -1.0, raw, ALU.mult, ALU.max).then_inc(S["ab"], 1)

            def step_sizes(f, q):
                v.tensor_tensor(a[:, q, :, :], dt[:, q, :, :], negA[:, :].unsqueeze(1).to_broadcast([P, AG, NH]), ALU.mult)\
                    .then_inc(S["a"], 1)

            def step_sizes_lo(f, q):
                dve.wait_ge(S["ahi"], nth(f + 1))
                v.tensor_tensor(asplit[:, q, LO, :], a[:, q, :, :].rearrange("p g h -> p (g h)"),
                                asplit[:, q, HI, :].bitcast(fp32), ALU.subtract).then_inc(S["alo"], 1)

            def variance(step, q):
                if step == 0:
                    return ch.do(v.tensor_scalar(varc[:, 0:AG], ss[:, q, :], 0.25 / DI, RMS_EPS, ALU.mult, ALU.add))
                return rsqrt(step - 1, varc[:, 0:AG], varc[:, AG:2 * AG], 0.5)

            def residual(b, between=None):
                dve.wait_ge(S["o"], nth(b * AG + AG))
                for g in range(AG):
                    v.scalar_tensor_tensor(x[:, b * AG + g, :], obuf[:, g, :], varc[:, AG + g:AG + g + 1], x[:, b * AG + g, :],
                                           ALU.mult, ALU.add).then_inc(S["x1"], 1)
                    if between:
                        between()
                sums_of(b * AG, AG, S["x1"])

            def group(b, q, front, prev):
                k, f, r = b * AG + 1, b + 1, 1 - q
                if prev:
                    dve.wait_ge(S["ss"], nth(b * AG))
                norm = Steps(variance, RSQRT + 1 if prev else 0, r)
                sizes = Steps(softplus, SOFTPLUS if front else 0, f, r)

                def chains():
                    for _ in range(2):
                        sizes()
                        norm()

                if front:
                    dve.wait_ge(S["hps"], nth(f))
                    normalized(f * AG, xn_a, AG, S["xn"])
                    norm()
                weights_of(k, 0)
                norm()
                gate(k, 0)
                norm()
                from_before(k, b, q, 0, norm)
                norm()
                if front:
                    lo_of(f, r)
                    norm()
                scan_in(k + 1)
                if front:
                    raw_dt(f)
                    conv(f, r, 0, chains)
                weights_of(k + 1, 1)
                norm()
                gated(k, 0)
                norm()
                gate(k + 1, 1)
                while norm.n < norm.count:
                    chains()
                if prev:
                    ch.wait(norm.last)
                    residual(b - 1, sizes)
                sizes()
                from_before(k + 1, b, q, 1, sizes)
                if front:
                    conv(f, r, 1, chains)
                    while sizes.n < sizes.count:
                        sizes()
                    ch.wait(sizes.last)
                    step_sizes(f, r)
                    conv_silu(f, r, 0)
                    step_sizes_lo(f, r)
                    conv(f, r, 2)
                gated(k + 1, 1)
                if front:
                    rest_of_front(f, r)
                    scan_in(k + 2)

            def rest_of_front(f, q):
                conv_silu(f, q, 1)
                for p in (3, 4):
                    conv(f, q, p)
                    conv_silu(f, q, p - 1)
                conv_silu(f, q, 4)

            FRONT = CONVC * (TAPS - 2) + SOFTPLUS + 1
            PREV = 1 + RSQRT + 1 + AG
            normalized(0, xn_a, AG, S["xn"])
            lo_of(0, 0)
            raw_dt(0)
            sizes = Steps(softplus, SOFTPLUS, 0, 0)
            conv(0, 0, 0, sizes)
            conv(0, 0, 1, sizes)
            conv_silu(0, 0, 0)
            while sizes.n < sizes.count:
                sizes()
            ch.wait(sizes.last)
            step_sizes(0, 0)
            step_sizes_lo(0, 0)
            conv(0, 0, 2)
            rest_of_front(0, 0)
            scan_in(1)
            group(0, 0, True, False)
            with dve.Fori(0, GROUPS // 2 - 1) as j:
                ch.enter(j, 2 * (FRONT + PREV))
                group(j * 2 + 1, 1, True, True)
                group(j * 2 + 2, 0, True, True)
                ch.leave(GROUPS // 2 - 1)
            group(GROUPS - 1, 1, False, True)
            dve.wait_ge(S["ss"], nth(TILES))
            norm = Steps(variance, RSQRT + 1, 1)
            while norm.n < norm.count:
                norm()
            ch.wait()
            residual(GROUPS - 1)
            dve.wait_ge(S["x1"], nth(TILES))
            ffn(1)

        @block.scalar
        def _(act):
            s = nc.scalar
            credit(act, "act")

            def hidden(i, S, f):
                k = i * FC + (f + 1)
                act.wait_ge(S["gps"], nth(k))
                act.wait_ge(S["gu"], nth(k - 2))
                s.activation(TG[:, f % 2, :], bank[pair("F", f)][:, :], ACT.Tanh, scale=0.5).then_inc(S["tg"], 1)

            def hidden_hi(i, S, f):
                k = i * FC + (f + 1)
                act.wait_ge(S["gu"], nth(k))
                act.wait_ge(S["gcol"], nth(k - 2))
                s.activation(gus[:, HI, f % 2, :], gu[:, f % 2, :], ACT.Copy).then_inc(S["guh"], 1)

            def experts(i, S, c):
                k = i * EC + (c + 1)
                act.wait_ge(S["lps"], nth(k))
                act.wait_ge(S["coef"], nth(k - 2))
                s.activation(E[:, c % 2, :], bank[pair("E", c) + 1][:, :], ACT.Exp).then_inc(S["e"], 1)
                act.wait_ge(S["pps"], nth(k))
                s.activation(TP[:, c % 2, :], bank[pair("E", c)][:, :], ACT.Tanh, scale=0.5).then_inc(S["tp"], 1)

            def experts_hi(i, S, c):
                k = i * EC + (c + 1)
                act.wait_ge(S["coef"], nth(k))
                act.wait_ge(S["ecol"], nth(k - 2))
                s.activation(coefs[:, HI, c % 2, :], coef[:, c % 2, :], ACT.Copy).then_inc(S["coh"], 1)

            def scores(i, S, part):
                if part == 0:
                    act.wait_ge(S["rps"], nth(i + 1))
                    act.wait_ge(S["rtps"], nth(i))
                    s.activation(rT[:, :], bank[6][:, :], ACT.Copy).then_inc(S["rT"], 1)
                elif part == 1:
                    act.wait_ge(S["rtps"], nth(i + 1))
                    act.wait_ge(S["tt"], nth(i))
                    s.activation(rtok[:, :, :].rearrange("p g k -> p (g k)"), bank[7][:, :], ACT.Copy).then_inc(S["rtok"], 1)
                elif part == 2:
                    act.wait_ge(S["dxy"], nth(i + 1))
                    s.activation(exy[:, :, :], dxy[:, :, :], ACT.Exp).then_inc(S["exy"], 1)
                elif part == 3:
                    act.wait_ge(S["zs"], nth(i + 1))
                    s.activation(zlog[:, :], zsum[:, :], ACT.Ln).then_inc(S["zlog"], 1)
                else:
                    act.wait_ge(S["ttps"], nth(i + 1))
                    act.wait_ge(S["rbps"], nth(i))
                    s.activation(TTs[:, HI, :], bank[6][0:NSEL, :], ACT.Copy).then_inc(S["tts"], 1)
                    act.wait_ge(S["ddps"], nth(i + 1))
                    act.wait_ge(S["dps"], nth(i * EC))
                    s.activation(DDs[:, :], bank[7][0:NSEL - 1, :], ACT.Copy).then_inc(S["dds"], 1)
            SCORES = {6: (1,), 8: (2,), 11: (3,), QUERIES: (4,)}
            SCORES0 = {0: (2,), 3: (3,), 5: (4,)}

            def step(u, i, S):
                kind, n, j = unit(u, i)
                before = unit(u - 1, i) if u else None
                if before and before[0] == "F":
                    hidden_hi(before[2], S, before[1])
                (hidden if kind == "F" else experts)(j, S, n)
                if before and before[0] == "E":
                    experts_hi(before[2], S, before[1])

            def ffn_block(i, S, more):
                if more:
                    scores(i + 1, S, 0)
                for u in range(START, NU + START * more):
                    step(u, i, S)
                    if more:
                        for part in SCORES.get(u, ()):
                            scores(i + 1, S, part)
                if not more:
                    experts_hi(i, S, EC - 1)

            def ffn(L):
                S = ffn_s[L]
                if L == 0:
                    split_hi(SPLITS[:1])
                for n in range(0, BLOCKS, 2):
                    for m in (n, n + 1):
                        for k in range(KD):
                            act.wait_ge(S["hps"], nth(m * KD + k + 1))
                            s.activation(hT[:, HI, k, BT * NORDER[m]:BT * (NORDER[m] + 1)], bank[2 * (m % 2) + k][:, :], ACT.Copy)\
                                .then_inc(S["h"], 1)
                    if n and L == 0:
                        split_hi(SPLITS[1:])
                    for m in (n, n + 1):
                        side, at = NORDER[m] // (BLOCKS // 2), BT * (NORDER[m] % (BLOCKS // 2))
                        act.wait_ge(S["qps"], nth(m + 1))
                        qv = qT[NS * side:NS * (side + 1), :].rearrange("p (m two) -> p two m", two=2)
                        for half in range(2):
                            s.activation(qv[:, half, at:at + BT], bank[4 + m % 2][NS * half:NS * (half + 1), :], ACT.Copy)\
                                .then_inc(S["q"], 1)
                if L == 0:
                    wait_split(act, SPLITS)
                for part in (0, 1):
                    scores(0, S, part)
                for u in range(START):
                    step(u, 0, S)
                    for part in SCORES0.get(u, ()):
                        scores(0, S, part)
                with act.Fori(0, BLOCKS - 1) as i:
                    ffn_block(i, S, True)
                ffn_block(BLOCKS - 1, S, False)

            def split_hi(weights):
                for name, t, _ in weights:
                    act.wait_ge(in_w[name], 16)
                    s.activation(flat(t, HI), stage[name], ACT.Copy).then_inc(w_hi, 1)

            act.wait_ge(in_c, 16 * len(CONSTS))
            s.activation(negA[:, :], alog, ACT.Exp).then_inc(att_s["eu"], 1)
            ffn(0)
            act.wait_ge(ffn_s[0]["out"], nth(TILES))
            split_hi(SPLITS_A)
            S = att_s

            def hi_of(f, q):
                act.wait_ge(S["hps"], nth(f + 1))
                s.activation(hTb[:, q, HI, :], bank[0][:, :], ACT.Copy).then_inc(S["h"], 1)

            def conv_in(f, q, p):
                c = CORDER[p]
                act.wait_ge(S["conv"], nth(f * CONVC + (p - 1)))
                s.activation(U[:, p % 2, 0:TAPS - 1], hist[:, c, :], ACT.Copy).then_inc(S["hist"], 1)
                act.wait_ge(S["pps"], nth(f * CONVC + (p + 1)))
                s.activation(U[:, p % 2, TAPS - 1:], bank[p % 2][:, 0:AT], ACT.Copy).then_inc(S["hist"], 1)
                act.wait_ge(S["ydps"], nth((f - 1) * AG))
                s.activation(xB[:, :] if c == CC else xc[:, q, c, :], bank[p % 2][:, 0:AT], ACT.Identity,
                             bias=convb[:, c:c + 1], scale=convw[:, c, TAPS - 1:TAPS]).then_inc(S["hist"], 1)
                act.wait_ge(S["hist"], nth(f * (3 * CONVC) + (3 * p + 1)))
                s.activation(hist[:, c, :], bank[p % 2][:, AT - TAPS + 1:AT], ACT.Copy).then_inc(S["u"], 1)

            def conv_tanh(f, q, p):
                c = CORDER[p]
                act.wait_ge(S["conv"], nth(f * CONVC + (p + 1)))
                act.wait_ge(S["xc"], nth(f * CONVC + (p - 1)))
                s.activation(TC[:, p % 2, :], xB[:, :] if c == CC else xc[:, q, c, :], ACT.Tanh).then_inc(S["tc"], 1)

            def gate(k, g):
                act.wait_ge(S["zps"], nth(k))
                act.wait_ge(S["yg"], nth(k - 2))
                s.activation(Tz[:, g, :], bank[1][:, :], ACT.Tanh, scale=0.5).then_inc(S["tz"], 1)

            def exponents(k, g):
                for n in range(2):
                    act.wait_ge(S["segps"], nth(2 * k + (n - 1)))
                    act.wait_ge(S["ydps"], nth(k - 2))
                    s.activation(Lx[:, g, 4 * n:4 * n + 4, :].rearrange("p h l -> p (h l)"), bank[4 + n][:, :], ACT.Exp)\
                        .then_inc(S["lx"], 1)

            def tokens(k):
                act.wait_ge(S["xps"], nth(k))
                act.wait_ge(S["xdt"], nth(k - 1))
                s.activation(xtok[:, :], bank[2][:, :], ACT.Copy).then_inc(S["xt"], 1)
                act.wait_ge(S["cbm"], nth(k))
                act.wait_ge(S["stps"], nth(k - 1))
                s.activation(Btok[:, :], bank[7][:, P:P + NS], ACT.Copy).then_inc(S["bt"], 1)

            def gated_t(k):
                act.wait_ge(S["ytps"], nth(k))
                act.wait_ge(S["ss"], nth(k))
                s.activation(ygT[:, :, :].rearrange("p c t -> p (c t)"), bank[2][:, :], ACT.Copy).then_inc(S["yt"], 1)

            def output(k, b, g):
                act.wait_ge(S["ops"], nth(k))
                act.wait_ge(S["x1"], nth(b * AG))
                s.activation(obuf[:, g, :], bank[3][:, 0:DM], ACT.Copy).then_inc(S["o"], 1)

            def squares(k, q, g):
                act.wait_ge(S["yg"], nth(k))
                s.activation(ygT[:, :, :].rearrange("p c t -> p (c t)"), y1[:, g, :], ACT.Square, accum_out=ss[:, q, g:g + 1])\
                    .then_inc(S["ss"], 1)

            def sizes(f):
                act.wait_ge(S["ab"], nth(f + 1))
                s.activation(sp[:, 2, :], sp[:, 1, :], ACT.Exp, scale=-1.0).then_inc(S["eu"], 1)

            def sizes_hi(f, q):
                act.wait_ge(S["a"], nth(f + 1))
                s.activation(asplit[:, q, HI, :], a[:, q, :, :].rearrange("p g h -> p (g h)"), ACT.Copy).then_inc(S["ahi"], 1)

            def chunk_decays(f, q):
                act.wait_ge(S["cums"], nth(f + 1))
                s.activation(decays[:, q, :, :, :].rearrange("p w g h -> p (w g h)"), bank[3][:, 0:3 * AG * NH], ACT.Exp)\
                    .then_inc(S["decays"], 1)

            def group(b, q, front, prev):
                k, f, r = b * AG + 1, b + 1, 1 - q
                if front:
                    hi_of(f, r)
                tokens(k + 1)
                if front:
                    sizes(f)
                    conv_in(f, r, 0)
                exponents(k + 1, 1)
                gate(k + 1, 1)
                if front:
                    conv_tanh(f, r, 0)
                    conv_in(f, r, 1)
                squares(k, q, 0)
                if front:
                    conv_in(f, r, 2)
                gated_t(k)
                if front:
                    sizes_hi(f, r)
                output(k, b, 0)
                if front:
                    rest_of_front(f, r)
                squares(k + 1, q, 1)
                if front:
                    next_gate(f, r, k + 2)
                gated_t(k + 1)
                if front:
                    conv_tanh(f, r, 4)
                    exponents(k + 2, 0)
                    tokens(k + 2)
                output(k + 1, b, 1)

            def rest_of_front(f, q):
                conv_tanh(f, q, 1)
                chunk_decays(f, q)
                conv_in(f, q, 3)
                conv_tanh(f, q, 2)

            def next_gate(f, q, k):
                conv_in(f, q, 4)
                gate(k, 0)
                conv_tanh(f, q, 3)

            hi_of(0, 0)
            sizes(0)
            conv_in(0, 0, 0)
            conv_in(0, 0, 1)
            conv_tanh(0, 0, 0)
            conv_in(0, 0, 2)
            sizes_hi(0, 0)
            rest_of_front(0, 0)
            next_gate(0, 0, 1)
            conv_tanh(0, 0, 4)
            exponents(1, 0)
            tokens(1)
            group(0, 0, True, False)
            with act.Fori(0, GROUPS // 2 - 1) as j:
                group(j * 2 + 1, 1, True, True)
                group(j * 2 + 2, 0, True, True)
            group(GROUPS - 1, 1, False, True)
            ffn(1)

        @block.gpsimd
        def _(pool):
            gp = nc.gpsimd
            credit(pool, "pool")

            def lo(u, i, S):
                kind, n, j = unit(u, i)
                if kind == "F":
                    pool.wait_ge(S["guh"], nth(j * FC + (n + 1)))
                    gp.tensor_tensor(gus[:, LO, n % 2, :], gu[:, n % 2, :], gus[:, HI, n % 2, :].bitcast(fp32), ALU.subtract)\
                        .then_inc(S["gul"], 1)
                else:
                    pool.wait_ge(S["coh"], nth(j * EC + (n + 1)))
                    gp.tensor_tensor(coefs[:, LO, n % 2, :], coef[:, n % 2, :], coefs[:, HI, n % 2, :].bitcast(fp32), ALU.subtract)\
                        .then_inc(S["col"], 1)

            def coefficients(i, S, c):
                pool.wait_ge(S["ge"], nth(i * (EC + 1) + (c + 1 if c < EC - 1 else EC + 1)))
                pool.wait_ge(S["sp"], nth(i * EC + (c + 1)))
                pool.wait_ge(S["col"], nth(i * EC + (c - 1)))
                gp.tensor_tensor(coef[:, c % 2, :], TP[:, c % 2, :], E[:, c % 2, :], ALU.mult).then_inc(S["coef"], 1)

            def ffn_block(i, S):
                for u, (kind, n) in enumerate(UNITS):
                    if u:
                        lo(u - 1, i, S)
                    if kind == "E":
                        coefficients(i, S, n)
                lo(NU - 1, i, S)

            def ffn(L):
                if L == 0:
                    split_lo(pool, gp, "p", SPLITS, 0)
                with pool.Fori(0, BLOCKS) as i:
                    ffn_block(i, ffn_s[L])

            ffn(0)
            S = att_s

            def scan_in(b, q):
                pool.wait_ge(S["alo"], nth(b + 1))
                for g in range(AG):
                    pool.wait_ge(S["segps"], nth(2 * (b * AG + g - 1)))
                    for w in (HI, LO):
                        m = gp.tensor_tensor(adiag[:, g, w, :].rearrange("p (h l) -> p h l", h=NH),
                                             tri_incl.unsqueeze(1).to_broadcast([P, NH, P]),
                                             asplit[:, q, w, NH * g:NH * (g + 1)].bitcast(fp32).unsqueeze(2).to_broadcast([P, NH, P]),
                                             ALU.mult)
                    m.then_inc(S["ad"], 1)

            def inputs(k, b, q, g):
                pool.wait_ge(S["xt"], nth(k))
                pool.wait_ge(S["ydps"], nth(k - 2))
                gp.tensor_tensor(hb(xdt[:, g, :]), hb(xtok[:, :]), per_head(dt[:, q, g, :]), ALU.mult).then_inc(S["xdt"], 1)
                pool.wait_ge(S["xdt"], nth(k))
                pool.wait_ge(S["decays"], nth(b + 1))
                pool.wait_ge(S["stps"], nth(k - 1))
                gp.tensor_tensor(hb(xdd[:, :]), hb(xdt[:, g, :]), per_head(decays[:, q, 1, g, :]), ALU.mult).then_inc(S["xdd"], 1)

            def decayed(k, q, g):
                pool.wait_ge(S["offps"], nth(k))
                pool.wait_ge(S["state"], nth(k - 1))
                gp.tensor_tensor(hb(state[:, :]), hb(state[:, :]), per_head(decays[0:NS, q, 2, g, :], NS), ALU.mult).then_inc(S["dec"], 1)

            def group(b, q, front, prev):
                k = b * AG + 1
                decayed(k, q, 0)
                inputs(k + 1, b, q, 1)
                decayed(k + 1, q, 1)
                if front:
                    scan_in(b + 1, 1 - q)
                    inputs(k + 2, b + 1, 1 - q, 0)

            scan_in(0, 0)
            inputs(1, 0, 0, 0)
            group(0, 0, True, False)
            with pool.Fori(0, GROUPS // 2 - 1) as j:
                group(j * 2 + 1, 1, True, True)
                group(j * 2 + 2, 0, True, True)
            group(GROUPS - 1, 1, False, True)
            ffn(1)

        @block.tensor
        def _(pe):
            credit(pe, "pe")

            def mm(out, pairs):
                for n, (lhsT, rhs) in enumerate(pairs):
                    last = nc.tensor.matmul(out, lhsT, rhs, start=n == 0, stop=n == len(pairs) - 1)
                return last

            def transposes(outs_ins):
                for o, t in outs_ins:
                    n = t.shape[0]
                    last = nc.tensor.transpose(o, t, ident[0:n, 0:n])
                return last

            def split3(lhsT, rhs):
                return [(lhsT(a), rhs(b)) for a, b in ((HI, HI), (HI, LO), (LO, HI))]

            def cols(t, g):
                return t[:, P * g:P * (g + 1)]

            def ffn(L):
                S = ffn_s[L]
                for n in range(0, BLOCKS, 2):
                    for m in (n, n + 1):
                        pe.wait_ge(S["xn"], nth((m + 1) * GT))
                        for k in range(KD):
                            pe.wait_ge(S["hl"], nth((m - 2) * KD + k + 1))
                            transposes([(cols(bank[2 * (m % 2) + k], g), cols(xn[:, m % 2, g, :], k)) for g in range(GT)])\
                                .then_inc(S["hps"], 1)
                    for m in (n, n + 1):
                        if m == 0 and L == 0:
                            pe.wait_ge(w_lo["v"], 1)
                        pe.wait_ge(S["hl"], nth(m * KD + KD))
                        pe.wait_ge(S["q"], nth((m - 1) * 2))
                        mm(bank[4 + m % 2][:, :], [p for k in range(KD) for p in split3(
                            lambda w: wq[:, w, k, :], lambda w: hT[:, w, k, BT * NORDER[m]:BT * (NORDER[m] + 1)])]).then_inc(S["qps"], 1)
                if L == 0:
                    pe.wait_ge(in_k, 16)
                    wait_split(pe, SPLITS)
                pe.wait_ge(S["q"], nth(2 * BLOCKS))
                raw_scores(0, S)
                token_scores(0, S)
                for u in range(START):
                    products(u, 0, S, True)
                    if u >= LAG:
                        accumulate(u - LAG, 0, S)
                queries(0, S)
                with pe.Fori(0, BLOCKS - 1) as i:
                    ffn_block(i, S, True)
                ffn_block(BLOCKS - 1, S, False)

            def raw_scores(i, S):
                pe.wait_ge(S["dds"], nth(i))
                pe.wait_ge(S["ttl"], nth(i))
                mm(bank[6][:, :], [(keys[:, :], qT[:, ds(i * BT, BT)])]).then_inc(S["rps"], 1)

            def token_scores(i, S):
                pe.wait_ge(S["rT"], nth(i + 1))
                transposes([(cols(bank[7], g), cols(rT, g)) for g in range(GT)]).then_inc(S["rtps"], 1)

            def queries(i, S):
                pe.wait_ge(S["tt"], nth(i + 1))
                pe.wait_ge(S["ge"], nth(i * (EC + 1)))
                pe.wait_ge(S["rtok"], nth(i + 1))
                transposes([(cols(bank[6][0:NSEL, :], g), TT[:, g, :]) for g in range(GT)]).then_inc(S["ttps"], 1)
                pe.wait_ge(S["dd"], nth(i * GT + GT))
                transposes([(cols(bank[7][0:NSEL - 1, :], g), DD[:, g, :]) for g in range(GT)]).then_inc(S["ddps"], 1)

            def accumulate(u, i, S):
                kind, n, j = unit(u, i)
                if kind == "F":
                    pe.wait_ge(S["gul"], nth(j * FC + (n + 1)))
                    lhs, w, s = gus, wd, S["gcol"]
                else:
                    pe.wait_ge(S["col"], nth(j * EC + (n + 1)))
                    lhs, w, s = coefs, ue, S["ecol"]
                if u % NU == 0:
                    pe.wait_ge(S["out"], nth(j * GT))
                for g in range(GT):
                    o = bank[4 + g // 2][:, DM * (g % 2):DM * (g % 2 + 1)]
                    for m, (lhsT, rhs) in enumerate(split3(lambda a: cols(lhs[:, a, n % 2, :], g), lambda b: w[:, b, n, :])):
                        last = nc.tensor.matmul(o, lhsT, rhs, start=u % NU == 0 and m == 0 and g % 2 == 0,
                                                stop=u == NU - 1 and m == 2, skip_group_check=True)
                last.then_inc(s, 1)

            def products(u, i, S, more):
                kind, n, j = unit(u, i)
                b = pair(kind, n)
                before, m = UNITS[(u - 2) % NU]
                back = j - 1 if u % NU < 2 else j
                if before == "F":
                    pe.wait_ge(S["gu"], nth(back * FC + (m + 1)))
                else:
                    pe.wait_ge(S["sp"], nth(back * EC + (m + 1)))

                def h(w, k):
                    return hT[:, w, k, ds(j * BT, BT)]

                if kind == "F":
                    for w, o, s in ((wg, b, "gps"), (wu, b + 1, "ups")):
                        mm(bank[o][:, :], [p for k in range(KD) for p in split3(
                            lambda q: cols(w[:, q, k, :], n), lambda q: h(q, k))]).then_inc(S[s], 1)
                    return
                if n == 0:
                    pe.wait_ge(S["ttl"], nth(j + 1))
                    pe.wait_ge(S["dds"], nth(j + 1))
                    if more:
                        pe.wait_ge(S["rtok"], nth(j + 2))
                mm(bank[b + 1][:, :], [(sel[:, n, :], TTs[:, w, :]) for w in (HI, LO)]).then_inc(S["lps"], 1)
                if n >= 2:
                    pe.wait_ge(S["ge"], nth(j * (EC + 1) + (n - 1)))
                mm(bank[6 + n % 2][:, :], [(selb[:, n, :], DDs[:, :])]).then_inc(S["dps"], 1)
                mm(bank[b][:, :], [p for k in range(KD) for p in split3(
                    lambda q: cols(de[:, q, k, :], n), lambda q: h(q, k))]).then_inc(S["pps"], 1)
                if n == EC - 1:
                    pe.wait_ge(S["ge"], nth(j * (EC + 1) + n))
                    mm(bank[6][:, :], [(sel[:, EC, :], TTs[:, w, :]) for w in (HI, LO)]).then_inc(S["rbps"], 1)

            def ffn_block(i, S, more):
                if more:
                    raw_scores(i + 1, S)
                for u in range(START, NU + START * more):
                    products(u, i, S, more)
                    if more and u == START:
                        token_scores(i + 1, S)
                    accumulate(u - LAG, i, S)
                    if more and u == QUERIES:
                        queries(i + 1, S)
                if not more:
                    for u in range(NU - LAG, NU):
                        accumulate(u, i, S)

            pe.wait_ge(in_c, 16 * len(CONSTS))
            pe.wait_ge(prep, 5)
            ffn(0)

            S = att_s
            wait_split(pe, SPLITS + SPLITS_A)
            pe.wait_ge(prep, 5 + CC)

            def hk(q, w, k, g=None):
                return hTb[:, q, w, AT * k:AT * (k + 1)] if g is None else hTb[:, q, w, AT * k + P * g:AT * k + P * (g + 1)]

            def transposed(f):
                pe.wait_ge(S["xn"], nth(f * AG + AG))
                pe.wait_ge(S["u"], nth(f * CONVC))
                transposes([(cols(bank[0], AG * k + g), cols(xn_a[:, g, :], k)) for k in range(KD) for g in range(AG)])\
                    .then_inc(S["hps"], 1)

            def raw_dt(f, q):
                pe.wait_ge(S["hl"], nth(f + 1))
                pe.wait_ge(S["o"], nth((f - 1) * AG))
                for g in range(AG):
                    last = mm(bank[3][:, NH * g:NH * (g + 1)], [p for k in range(KD) for p in split3(
                        lambda w: hk(q, w, k, g), lambda w: wdt[:, w, k, :])])
                last.then_inc(S["dtps"], 1)

            def project(f, q, p):
                pe.wait_ge(S["u"], nth(f * CONVC + (p - 1)))
                if p == 1:
                    pe.wait_ge(S["sz"], nth(f * AG))
                mm(bank[p % 2][:, 0:AT], [m for k in range(KD) for m in split3(
                    lambda w: cols(win[:, w, k, :], CORDER[p]), lambda w: hk(q, w, k))]).then_inc(S["pps"], 1)

            def sums(f, q):
                pe.wait_ge(S["a"], nth(f + 1))
                pe.wait_ge(S["o"], nth((f - 1) * AG + 1))
                arow = a[:, q, :, :].rearrange("p g h -> p (g h)")
                for n, w in enumerate((tri_incl, tri_after, ones)):
                    last = mm(bank[3][:, AG * NH * n:AG * NH * (n + 1)], [(w, arow)])
                last.then_inc(S["cums"], 1)

            def gate(k, q, g):
                pe.wait_ge(S["sz"], nth(k - 1))
                mm(bank[1][:, :], [p for m in range(KD) for p in split3(
                    lambda w: hk(q, w, m, g), lambda w: wz[:, w, m, :])]).then_inc(S["zps"], 1)

            def decay_sums(k, g):
                pe.wait_ge(S["ad"], nth(k))
                pe.wait_ge(S["yoff"], nth(k - 1))
                pe.wait_ge(S["state"], nth(k - 1))
                for n in range(2):
                    mm(bank[4 + n][:, :], [(after_hi[:, :], adiag[:, g, w, 512 * n:512 * (n + 1)])
                                           for w in (HI, LO)]).then_inc(S["segps"], 1)

            def tokens(k, b, q, g):
                pe.wait_ge(S["xc"], nth(b * CONVC + CONVC))
                if g:
                    pe.wait_ge(S["xt"], nth(k - 1))
                else:
                    pe.wait_ge(S["yt"], nth(k - 2))
                transposes([(cols(bank[2], c), cols(xc[:, q, c, :], g)) for c in range(CC)]).then_inc(S["xps"], 1)
                pe.wait_ge(S["bt"], nth(k - 1))
                mm(bank[7][:, 0:P], [(cols(BTt[:, q, :], g), cols(CTt[:, q, :], g))])
                transposes([(bank[7][:, P:P + NS], cols(BTt[:, q, :], g))]).then_inc(S["cbps"], 1)

            def from_before(k, q, g):
                pe.wait_ge(S["state"], nth(k - 1))
                pe.wait_ge(S["lx"], nth(2 * k - 1))
                mm(bank[4][:, :], [(cols(CTt[:, q, :], g), state[:, :])]).then_inc(S["offps"], 1)

            def to_after(k):
                pe.wait_ge(S["lx"], nth(2 * k))
                pe.wait_ge(S["bt"], nth(k))
                pe.wait_ge(S["xdd"], nth(k))
                mm(bank[5][0:NS, :], [(Btok[:, :], xdd[:, :])]).then_inc(S["stps"], 1)

            def within(k, q, g):
                pe.wait_ge(S["m"], nth(k))
                pe.wait_ge(S["xdt"], nth(k))
                pe.wait_ge(S["yadd"], nth(k - 1))
                for c in range(CC):
                    nc.tensor.matmul(cols(bank[6], c), cols(xc[:, q, c, :], g), diagD[:, c, :],
                                     start=c == 0, stop=False, skip_group_check=True)
                for h in range(NH):
                    last = nc.tensor.matmul(bank[6][:, HD * h:HD * (h + 1)], Lx[:, g, h, :], xdt[:, g, HD * h:HD * (h + 1)],
                                            start=False, stop=h == NH - 1, skip_group_check=True)
                last.then_inc(S["ydps"], 1)

            def gated_t(k, g):
                pe.wait_ge(S["yg"], nth(k))
                pe.wait_ge(S["xt"], nth(k + 1 - g))
                pe.wait_ge(S["yt"], nth(k - 1))
                transposes([(cols(bank[2], c), cols(y1[:, g, :], c)) for c in range(CC)]).then_inc(S["ytps"], 1)

            def output(k):
                pe.wait_ge(S["yt"], nth(k))
                pe.wait_ge(S["o"], nth(k - 1))
                mm(bank[3][:, 0:DM], [(ygT[:, c, :], wo[:, c, :]) for c in range(CC)]).then_inc(S["ops"], 1)

            def group(b, q, front, prev):
                k, f, r = b * AG + 1, b + 1, 1 - q
                from_before(k, q, 0)
                if front:
                    transposed(f)
                to_after(k)
                tokens(k + 1, b, q, 1)
                if front:
                    raw_dt(f, r)
                    project(f, r, 0)
                decay_sums(k + 1, 1)
                within(k, q, 0)
                gate(k + 1, q, 1)
                from_before(k + 1, q, 1)
                to_after(k + 1)
                gated_t(k, 0)
                if front:
                    project(f, r, 1)
                    project(f, r, 2)
                within(k + 1, q, 1)
                if front:
                    pe.wait_ge(S["raw"], nth(f + 1))
                output(k)
                if front:
                    rest_of_front(f, r)
                gated_t(k + 1, 1)
                if front:
                    decay_sums(k + 2, 0)
                    tokens(k + 2, f, r, 0)
                    pe.wait_ge(S["decays"], nth(f + 1))
                output(k + 1)

            def rest_of_front(f, q):
                sums(f, q)
                project(f, q, 3)
                project(f, q, 4)
                pe.wait_ge(S["u"], nth(f * CONVC + 4))
                gate(f * AG + 1, q, 0)

            transposed(0)
            raw_dt(0, 0)
            project(0, 0, 0)
            project(0, 0, 1)
            project(0, 0, 2)
            pe.wait_ge(S["raw"], nth(1))
            rest_of_front(0, 0)
            decay_sums(1, 0)
            tokens(1, 0, 0, 0)
            group(0, 0, True, False)
            with pe.Fori(0, GROUPS // 2 - 1) as j:
                group(j * 2 + 1, 1, True, True)
                group(j * 2 + 2, 0, True, True)
            group(GROUPS - 1, 1, False, True)
            ffn(1)


def kernel(**inputs):
    import numpy as np
    import concourse.bacc as bacc
    from concourse.bass_utils import run_bass_kernel_spmd

    pre = "L0_attn_"
    w = {k: np.asarray(v) for k, v in inputs.items()}
    f32 = np.float32

    def rows(a, n):
        return np.ascontiguousarray(a.reshape(n, P, -1).transpose(1, 0, 2))

    w_inT = w[pre + "W_in"].T
    k = w["L0_ffn_keys"]
    keys = np.zeros((P, P), f32)
    keys[:NKEY, :NKEY], keys[NKEY:, NKEY:] = k[0], k[1]
    small = np.concatenate([
        w[pre + "conv_w"].reshape(CONVC, P, TAPS).transpose(1, 0, 2).reshape(P, CONVC * TAPS),
        w[pre + "conv_b"].reshape(CONVC, P).T, w[pre + "norm_w"].reshape(CC, P).T,
        np.broadcast_to(w[pre + "dt_bias"], (P, NH)), np.broadcast_to(w[pre + "A_log"], (P, NH)),
        np.repeat(w[pre + "D_param"], HD).reshape(CC, P).T], axis=1)
    r = np.arange(P)
    cst = np.stack([r[:, None] == r, r[:, None] <= r, r[:, None] > r, np.ones((P, P), bool)], axis=1).astype(f32)
    sel = np.zeros((NKEY + XKEYS + 1, EC + 1, P), f32)
    for c in range(EC):
        sel[r % NKEY, c, r] = 1
        sel[NKEY + 2 * c + r // NKEY, c, r] = 1
    sel[NKEY + XKEYS, EC, P - 1] = 1
    arrays = {
        "u": w[pre + "u"], "wq": rows(w["L0_ffn_W_q"], KD), "keys": keys,
        "wg": rows(w["L0_ffn_gate_w"], KD), "wu": rows(w["L0_ffn_up_w"], KD), "wd": rows(w["L0_ffn_down_w"], FC),
        "de": rows(w["L0_ffn_down_embed"].T, KD), "ue": rows(w["L0_ffn_up_embed"], EC),
        "win": rows(w_inT[:, DI:DI + XBC], KD), "wz": rows(w_inT[:, :DI], KD), "wdt": rows(w_inT[:, DI + XBC:], KD),
        "wo": rows(w[pre + "W_out"].T, CC), "small": small, "cst": cst, "sel": sel,
        "iota": np.broadcast_to(np.arange(NKEY, dtype=f32), (P, NKEY)),
    }
    arrays = {n: np.ascontiguousarray(a) for n, a in arrays.items()}
    nc = bacc.Bacc("TRN2", target_bir_lowering=False, num_devices=1)
    A = {n: nc.dram_tensor(f"in_{n}", a.shape, mybir.dt.from_np(a.dtype), kind="ExternalInput").ap()
         for n, a in arrays.items()}
    A["out"] = nc.dram_tensor("out", (1, SEQ, DM), mybir.dt.float32, kind="ExternalOutput").ap()
    program(nc, A)
    res = run_bass_kernel_spmd(nc, [{f"in_{n}": a for n, a in arrays.items()}], core_ids=[0])
    return res.results[0]["out"]
```

```python
import concourse.bass as bass
from concourse import mybir
from contextlib import ExitStack

SEQ, DM, P = 2048, 256, 128
TILES = SEQ // P
GT = 4
BLOCKS = TILES // GT
BT = GT * P
AG = 2
GROUPS = TILES // AG
AT = AG * P
KD = DM // P
INTER = 1024
FC = INTER // P
NKEY, TOPK, NEXP = 64, 8, 512
EC = NEXP // P
XKEYS = NEXP // NKEY
DI, NH, HD, NS, TAPS = 512, 8, 64, 64, 4
CC = DI // P
XBC = DI + 2 * NS
CONVC = XBC // P
CORDER = (CONVC - 1, *range(CONVC - 1))
LN_EPS = 1e-5
RMS_EPS = 1e-5
RSQRT_MAGIC = float(0x5F3759DF)
CREDIT = 4
SERIES = 9


def program(nc, A):
    fp32, bf16, f32r = mybir.dt.float32, mybir.dt.bfloat16, mybir.dt.float32r
    i32, u32 = mybir.dt.int32, mybir.dt.uint32
    HI, LO = 0, 1
    ALU, ACT, AX = mybir.AluOpType, mybir.ActivationFunctionType, mybir.AxisListType
    ds = bass.ds
    ctx = ExitStack()
    with ctx:
        def sb(name, shape, dt=fp32):
            return ctx.enter_context(nc.sbuf_tensor(name, shape, dt))

        def sem(name):
            return ctx.enter_context(nc.semaphore(name))

        WORK = {"work": 13704, "workr": 13312}
        work = sb("work", [P, WORK["work"]])
        workr = sb("workr", [P, WORK["workr"]], f32r)
        used = {}

        def part(layer, *shape, split=False):
            pool = "workr" if split else "work"
            n = 1
            for d in shape:
                n *= d
            at = used.get((layer, pool), 0)
            used[layer, pool] = at + n
            assert at + n <= WORK[pool], (layer, pool, at + n)
            v = (workr if split else work)[:, at:at + n]
            names = "abcd"[:len(shape)]
            if len(shape) == 1:
                return v
            return v.rearrange(f"p ({' '.join(names)}) -> p {' '.join(names)}", **dict(zip(names, shape)))

        x = sb("x", [P, TILES, DM])
        wq = sb("wq", [P, 2, KD, P], f32r)
        wg = sb("wg", [P, 2, KD, INTER], f32r)
        wu = sb("wu", [P, 2, KD, INTER], f32r)
        wd = sb("wd", [P, 2, FC, DM], f32r)
        de = sb("de", [P, 2, KD, NEXP], f32r)
        ue = sb("ue", [P, 2, EC, DM], f32r)
        keys = sb("keys", [P, P])
        win = part("att", 2, KD, XBC, split=True)
        wz = part("att", 2, KD, DI, split=True)
        wdt = part("att", 2, KD, NH, split=True)
        wo = sb("wo", [P, CC, DM])
        small = sb("small", [P, 49])
        convw = small[:, 0:20].rearrange("p (c k) -> p c k", k=TAPS)
        convb = small[:, 20:25]
        normw = small[:, 25:29]
        dtb, alog, dcol = small[:, 29:37], small[:, 37:45], small[:, 45:49]
        cst = sb("cst", [P, 4, P])
        ident, tri_incl, tri_after, ones = cst[:, 0, :], cst[:, 1, :], cst[:, 2, :], cst[:, 3, :]
        after_hi = sb("after_hi", [P, P], f32r)
        NSEL = NKEY + XKEYS + 1
        sel = sb("sel", [NSEL, EC + 1, P], f32r)
        selb = sb("selb", [NKEY + XKEYS, EC, P], bf16)
        iota = sb("iota", [P, NKEY])
        iotab = sb("iotab", [P, NKEY], bf16)
        negA = sb("negA", [P, NH])

        xn = part("ffn", 2, GT, DM)
        qT = part("ffn", SEQ)
        stats = sb("stats", [P, TILES, 6])
        mv = sb("mv", [P, TILES, 2])
        rs = sb("rs", [P, 2, 4, TILES])
        varc = sb("varc", [P, 2, 2 * TILES])
        rstd = sb("rstd", [P, TILES])
        hT = part("ffn", BLOCKS, 2, KD, BT, split=True)
        after_norm = used["ffn", "work"]

        TG = part("ffn", 2, BT)
        gu = part("ffn", 2, BT)
        rT = part("ffn", BT)
        rtok = part("ffn", GT, P)
        sxy = sb("sxy", [P, 2, GT, TOPK])
        ixy = sb("ixy", [P, 2, GT, TOPK], u32)
        ixyf = sb("ixyf", [P, 2, GT, TOPK])
        sums = part("ffn", GT, 64)
        best = part("ffn", GT, TOPK)
        rest = part("ffn", GT, 64)
        chosen = part("ffn", GT, 64)
        chosenw = part("ffn", GT, 64)
        dxy = part("ffn", 2 * GT, TOPK)
        exy = part("ffn", 2 * GT, TOPK)
        sxyv = sxy[:, :, :, :].rearrange("p s g k -> p (s g) k")
        exyv = exy[:, :, :].rearrange("p (s g) k -> p s g k", s=2)
        cnt = part("ffn", GT, TOPK)
        rowsum = part("ffn", GT, TOPK)
        clamped = part("ffn", GT, TOPK)
        zsum = part("ffn", GT)
        zinv = part("ffn", GT)
        zlog = part("ffn", GT)
        csum = part("ffn", GT)
        eqx = part("ffn", GT, XKEYS, TOPK)
        onehot = sb("onehot", [P, 2, TOPK, NKEY], bf16)
        TT = part("ffn", GT, NSEL)
        DD = part("ffn", GT, NSEL - 1)
        TTs = part("ffn", 2, BT, split=True)[0:NSEL, :, :]
        DDs = sb("DDs", [NSEL - 1, BT], bf16)

        after_routing = used["ffn", "work"]

        E = part("ffn", 2, BT)
        TP = part("ffn", 2, BT)
        coef = part("ffn", 2, BT)
        coefs = part("ffn", 2, 2, BT, split=True)
        gus = part("ffn", 2, 2, BT, split=True)

        diagD = sb("diagD", [P, CC, P])
        hTb = part("att", 2, 2, KD * AT, split=True)
        asplit = part("att", 2, 2, AG * NH, split=True)
        adiag = part("att", 2, 2, NH * P, split=True)
        xn_a = part("att", AG, DM)
        U = part("att", 2, TAPS - 1 + AT)
        hist = sb("hist", [P, CONVC, TAPS - 1])
        TC = part("att", 2, AT)
        xc = part("att", 2, CC, AT)
        xB = part("att", AT)
        BTt = part("att", 2, AT)[0:NS, :, :]
        CTt = part("att", 2, AT)[0:NS, :, :]
        sp = part("att", 6, AG * NH)
        dt = part("att", 2, AG, NH)
        a = part("att", 2, AG, NH)
        decays = part("att", 2, 3, AG, NH)
        xtok = part("att", DI)
        xdt = part("att", 2, DI)
        xdd = part("att", DI)
        Btok = part("att", NS)
        Tz = part("att", 2, DI)
        CBm = part("att", P)
        y1 = part("att", 2, DI)
        ss = part("att", 2, AG)
        ygT = part("att", CC, P)
        Lx = part("att", 2, NH, P)
        obuf = part("att", AG, DM)
        state = sb("state", [NS, DI])

        stage, at = {}, after_norm
        for name, t in (("wq", wq), ("sel", sel), ("wu", wu), ("wg", wg), ("wd", wd), ("de", de), ("ue", ue)):
            n = KD * P if name == "wq" else (EC + 1) * P if name == "sel" else t.shape[2] * t.shape[3]
            if name == "wd":
                assert at <= after_routing
                at = after_routing
            stage[name] = work[0:t.shape[0], at:at + n]
            at += n
        assert at <= WORK["work"]
        stage["win"] = work[:, 0:KD * XBC]
        assert KD * XBC <= 2 * GT * DM
        at = WORK["work"] - KD * (DI + NH)
        assert at >= used["ffn", "work"]
        for name, t in (("wz", wz), ("wdt", wdt)):
            n = t.shape[2] * t.shape[3]
            stage[name] = work[:, at:at + n]
            at += n

        bank = [ctx.enter_context(nc.psum_tensor(f"bank{n}", [P, 512], fp32)) for n in range(8)]


        in_x = [sem(f"in_x{n}") for n in range(BLOCKS)]
        in_w = {n: sem(f"in_{n}") for n in stage}
        x_there = sem("x_there")
        in_c, in_k, in_o = sem("in_consts"), sem("in_keys"), sem("in_wo")
        w_hi = sem("weights_hi")
        w_lo = {"v": sem("weights_lo_dve"), "p": sem("weights_lo_pool")}
        prep = sem("constants_prepared")
        out_sent = sem("out_sent")
        dve_done = sem("dve_done")
        passed = sem("passed")
        FFN_SEMS = {
            "pe": ("hps", "qps", "rps", "rtps", "ttps", "ddps", "pps", "lps", "dps", "rbps", "gps", "ups", "ecol", "gcol"),
            "act": ("h", "q", "rT", "rtok", "exy", "zlog", "tts", "dds", "tp", "e", "tg", "guh", "coh"),
            "dve": ("xn", "hl", "dxy", "zs", "tt", "dd", "ttl", "sg", "gu", "ge", "sp", "out"),
            "pool": ("coef", "gul", "col")}
        ATT_SEMS = {
            "pe": ("hps", "pps", "dtps", "cums", "zps", "xps", "cbps", "segps", "ydps", "offps", "stps", "ytps", "ops"),
            "act": ("h", "hist", "u", "tc", "eu", "decays", "lx", "tz", "xt", "bt", "ss", "yt", "o", "ahi"),
            "dve": ("xn", "conv", "xc", "raw", "ab", "a", "alo", "sz", "cbm", "m", "yoff", "yadd", "state", "yg", "x1", "hl"),
            "pool": ("ad", "xdt", "xdd", "dec")}
        ffn_s = [{n: sem(f"f{L}_{n}") for names in FFN_SEMS.values() for n in names} for L in range(2)]
        att_s = {n: sem(f"a_{n}") for names in ATT_SEMS.values() for n in names}

        def credit(eng, who):
            for S in ffn_s:
                for n in FFN_SEMS[who]:
                    eng.sem_inc(S[n], CREDIT)
            for n in ATT_SEMS[who]:
                eng.sem_inc(att_s[n], CREDIT)

        def nth(n):
            return n + CREDIT

        class Chain:

            def __init__(self, eng, s):
                self.eng, self.s, self.before, self.base, self.n = eng, s, 0, 0, 0

            def do(self, ins):
                ins.then_inc(self.s, 1)
                self.n += 1
                return self.n

            def wait(self, n=None):
                self.eng.wait_ge(self.s, self.base + (self.n if n is None else n))

            def enter(self, i, per):
                self.before += self.n
                self.per, self.n = per, 0
                self.base = i * per + self.before

            def leave(self, trips):
                assert self.n == self.per, (self.n, self.per)
                self.before += trips * self.per
                self.base, self.n = self.before, 0

        block = ctx.enter_context(nc.Block())
        xv = A["u"].rearrange("o (t p) d -> p (o t) d", p=P)
        ov = A["out"].rearrange("o (t p) d -> p (o t) d", p=P)
        CONSTS = [("cst", cst), ("small", small), ("iota", iota)]
        SPLITS = [("wq", wq, "v"), ("wu", wu, "p"), ("wg", wg, "p"), ("wd", wd, "p"), ("de", de, "p"), ("ue", ue, "p")]
        SPLITS_A = [("win", win, "v"), ("wz", wz, "v"), ("wdt", wdt, "v")]
        UNITS = [("F", n) for n in range(7)] + [("E", 0), ("F", 7), ("E", 1), ("E", 2), ("E", 3)]
        NU = len(UNITS)
        LAG = 2
        PREPARED = CC + 5
        QUERIES = 16
        START = 6
        NORDER = (0, 2, 1, 3)

        def unit(u, i):
            return (*UNITS[u % NU], i + 1 if u >= NU else i)

        def flat(t, w):
            return t[:, w].rearrange("p a b -> p (a b)")

        def full(t):
            return t[tuple(slice(None) for _ in t.shape)]

        def hb(t):
            return t.rearrange("p (h d) -> p h d", d=HD)

        def per_head(t, parts=P):
            return t.unsqueeze(2).to_broadcast([parts, NH, HD])

        NBANK = (6, 2, 6, 6)
        QBANK = (4, 5, 6, 6)

        def pair(kind, n):
            return 2 * (UNITS.index((kind, n)) % 2)

        def split_lo(eng, unit, who, weights, done):
            for n, (name, t, by) in enumerate(weights):
                if by == who:
                    eng.wait_ge(w_hi, done + n + 1)
                    unit.tensor_tensor(flat(t, LO), stage[name], flat(t, HI).bitcast(fp32), ALU.subtract).then_inc(w_lo[by], 1)

        def wait_split(eng, weights):
            for by, s in w_lo.items():
                eng.wait_ge(s, len([w for w in weights if w[2] == by]))

        @block.sync
        def _(sync):
            def load(name):
                sync.dma_start(stage[name], A[name].rearrange("p a b -> p (a b)")).then_inc(in_w[name], 16)

            def load_x(n):
                sync.dma_start(x[:, GT * n:GT * (n + 1), :], xv[:, GT * n:GT * (n + 1), :]).then_inc(in_x[n], 16)

            load_x(NORDER[0])
            load_x(NORDER[1])
            for name, t in CONSTS:
                sync.dma_start(full(t), A[name]).then_inc(in_c, 16)
            sync.dma_start(keys[:, :], A["keys"]).then_inc(in_k, 16)
            for name in ("wq", "sel", "wu", "wg"):
                load(name)
            load_x(NORDER[2])
            load_x(NORDER[3])
            for name in ("wd", "de", "ue"):
                load(name)
            sync.dma_start(wo[:, :, :], A["wo"]).then_inc(in_o, 16)
            for n in NORDER:
                sync.wait_ge(in_x[n], 16)
                sync.sem_inc(x_there, 1)
            sync.wait_ge(w_hi, len(SPLITS))
            wait_split(sync, SPLITS)
            sync.wait_ge(ffn_s[0]["hps"], nth(BLOCKS * KD))
            for name in ("win", "wz", "wdt"):
                load(name)
            with sync.Fori(0, BLOCKS) as i:
                sync.wait_ge(ffn_s[1]["out"], nth(i * GT + GT))
                sync.dma_start(ov[:, ds(i * GT, GT), :], x[:, ds(i * GT, GT), :]).then_inc(out_sent, 16)
            sync.wait_ge(out_sent, 16 * BLOCKS)

        @block.vector
        def _(dve):
            ch = Chain(dve, dve_done)
            v = nc.vector
            credit(dve, "dve")

            def alone():
                dve.sem_inc(passed, 1)

            class Steps:

                def __init__(self, step, count, *args):
                    self.step, self.count, self.args, self.n, self.last = step, count, args, 0, None

                def __call__(self):
                    if self.n < self.count:
                        if self.last is not None:
                            ch.wait(self.last)
                        self.last = self.step(self.n, *self.args)
                        self.n += 1

            def rsqrt(step, which, var, y, scale):
                vh, w, t, bits = (rs[:, which, n, 0:var.shape[1]] for n in range(4))
                if step == 0:
                    ch.do(v.tensor_scalar(vh, var, -0.5, None, ALU.mult))
                    return ch.do(v.tensor_scalar(bits.bitcast(i32), var.bitcast(i32), 1, None, ALU.logical_shift_right))
                if step == 1:
                    return ch.do(v.tensor_scalar(w.bitcast(i32), bits.bitcast(i32), -1.0, RSQRT_MAGIC, ALU.mult, ALU.add))
                if step == RSQRT - 1:
                    return ch.do(v.tensor_scalar(y, w, scale, None, ALU.mult))
                if step % 3 == 2:
                    return ch.do(v.tensor_tensor(t, w, w, ALU.mult))
                if step % 3 == 0:
                    return ch.do(v.tensor_tensor(t, t, vh, ALU.mult))
                return ch.do(v.scalar_tensor_tensor(w, t, 1.5, w, ALU.add, ALU.mult))
            RSQRT = 2 + 3 * 3 + 1

            TSETS = {"even": [0, 1, 2, 3, 8, 9, 10, 11], "odd": [4, 5, 6, 7, 12, 13, 14, 15],
                     "most": list(range(12)), "last": list(range(12, 16))}

            def pick(t, tset):
                if tset in ("even", "odd"):
                    return t.rearrange("p (s b g) -> p b s g", b=2, g=GT)[:, int(tset == "odd"), :, :]
                tiles = TSETS[tset]
                return t[:, tiles[0]:tiles[-1] + 1].rearrange("p (s g) -> p s g", g=GT)

            FACTOR = RSQRT + 3

            def factor(step, tset):
                n = len(TSETS[tset])
                if step == 0:
                    for t in TSETS[tset]:
                        last = ch.do(v.bn_aggr(mv[:, t, :], stats[:, t, :]))
                    return last
                if step == 1:
                    return ch.do(v.tensor_scalar(varc[:, 0, 0:n].rearrange("p (s g) -> p s g", g=GT), pick(mv[:, :, 1], tset),
                                                 LN_EPS, None, ALU.add))
                if step < FACTOR - 1:
                    return rsqrt(step - 2, 0, varc[:, 0, 0:n], varc[:, 0, TILES:TILES + n], 1.0)
                return ch.do(v.tensor_copy(pick(rstd[:, :], tset), varc[:, 0, TILES:TILES + n].rearrange("p (s g) -> p s g", g=GT)))

            def factors(tset):
                ch.wait()
                for step in range(FACTOR):
                    factor(step, tset)
                    ch.wait()

            def first_sums(n):
                dve.wait_ge(x_there, n + 1)
                for g in range(GT):
                    ch.do(v.bn_stats(stats[:, GT * NORDER[n] + g, :], x[:, GT * NORDER[n] + g, :]))

            def normalized(t, xn, tiles, done, between=None):
                for g in range(tiles):
                    v.tensor_scalar(xn[:, g, :], x[:, ds(t + g, 1), :].rearrange("p a d -> p (a d)"),
                                    mv[:, ds(t + g, 1), 0:1].rearrange("p a b -> p (a b)"), rstd[:, ds(t + g, 1)],
                                    ALU.subtract, ALU.mult).then_inc(done, 1)
                    if between:
                        between()

            def sums_of(t, tiles, done):
                dve.wait_ge(done, nth(t + tiles))
                alone()
                for g in range(tiles):
                    ch.do(v.bn_stats(stats[:, t + g, :], x[:, t + g, :]))

            def sq8(t):
                return t.rearrange("p g (a b) -> p g a b", b=TOPK)

            def routing(i, S, part):
                rx, ry = rtok[:, :, 0:NKEY], rtok[:, :, NKEY:P]
                pairs = [P, GT, TOPK, TOPK]
                if part == 0:
                    dve.wait_ge(S["rtok"], nth(i + 1))
                    alone()
                    for s, r in ((0, rx), (1, ry)):
                        for g in range(GT):
                            ch.do(v.max(sxy[:, s, g, :], r[:, g, :]))
                elif part == 1:
                    ch.wait()
                    alone()
                    for s, r in ((0, rx), (1, ry)):
                        for g in range(GT):
                            ch.do(v.max_index(ixy[:, s, g, :], sxy[:, s, g, :], r[:, g, :]))
                    ch.do(v.tensor_tensor(sq8(sums[:, :, :]), sxy[:, 0, :, :].unsqueeze(3).to_broadcast(pairs),
                                          sxy[:, 1, :, :].unsqueeze(2).to_broadcast(pairs), ALU.add))
                    v.tensor_tensor(dxy[:, :, :], sxyv[:, :, :], sxyv[:, :, 0:1].to_broadcast([P, 2 * GT, TOPK]),
                                    ALU.subtract).then_inc(S["dxy"], 1)
                elif part == 2:
                    ch.wait()
                    alone()
                    for g in range(GT):
                        ch.do(v.max(best[:, g, :], sums[:, g, :]))
                    ch.do(v.tensor_copy(ixyf[:, :, :, :], ixy[:, :, :, :]))
                    ch.wait()
                    alone()
                    for g in range(GT):
                        ch.do(v.match_replace(rest[:, g, :], best[:, g, :], sums[:, g, :], -3.0e38))
                elif part == 3:
                    ch.wait()
                    ch.do(v.tensor_tensor(chosen[:, :, :], sums[:, :, :], rest[:, :, :], ALU.not_equal))
                    dve.wait_ge(S["ttps"], nth(i))
                    ch.do(v.tensor_tensor(TT[:, :, 0:NKEY], ry, sxy[:, 1, :, 0:1].to_broadcast([P, GT, NKEY]), ALU.subtract))
                    ch.wait()
                    ch.do(v.tensor_reduce(cnt[:, :, :], sq8(chosen[:, :, :]), AX.X, ALU.add))
                    dve.wait_ge(S["exy"], nth(i + 1))
                    ch.do(v.tensor_tensor(sq8(chosenw[:, :, :]), sq8(chosen[:, :, :]),
                                          exyv[:, 1, :, :].unsqueeze(2).to_broadcast(pairs), ALU.mult))
                elif part == 4:
                    ch.wait()
                    ch.do(v.tensor_reduce(rowsum[:, :, :], sq8(chosenw[:, :, :]), AX.X, ALU.add))
                    ch.wait()
                    ch.do(v.tensor_tensor(rowsum[:, :, :], rowsum[:, :, :], exyv[:, 0, :, :], ALU.mult))
                    ch.wait()
                    v.tensor_reduce(zsum[:, :], rowsum[:, :, :], AX.X, ALU.add).then_inc(S["zs"], 1)
                    ch.do(v.scalar_tensor_tensor(clamped[:, :, :], ixyf[:, 0, :, :], float(XKEYS), rowsum[:, :, :],
                                                 ALU.is_ge, ALU.mult))
                    ch.wait()
                    dve.wait_ge(S["zs"], nth(i + 1))
                    ch.do(v.reciprocal(zinv[:, :], zsum[:, :]))
                    ch.do(v.tensor_reduce(csum[:, :], clamped[:, :, :], AX.X, ALU.add))
                elif part == 5:
                    ch.wait()
                    ch.do(v.tensor_tensor(TT[:, :, NSEL - 1], csum[:, :], zinv[:, :], ALU.mult))
                    ch.do(v.tensor_tensor(eqx[:, :, :, :], ixyf[:, 0, :, :].unsqueeze(2).to_broadcast([P, GT, XKEYS, TOPK]),
                                          iota[:, 0:XKEYS].unsqueeze(1).unsqueeze(3).to_broadcast([P, GT, XKEYS, TOPK]),
                                          ALU.is_equal))
                    ch.wait()
                    ch.do(v.tensor_tensor(eqx[:, :, :, :], eqx[:, :, :, :],
                                          cnt[:, :, :].unsqueeze(2).to_broadcast([P, GT, XKEYS, TOPK]), ALU.mult))
                    ch.wait()
                    dve.wait_ge(S["ddps"], nth(i))
                    ch.do(v.tensor_reduce(DD[:, :, NKEY:NKEY + XKEYS], eqx[:, :, :, :], AX.X, ALU.add))
                    dve.wait_ge(S["zlog"], nth(i + 1))
                    ch.do(v.tensor_tensor(zlog[:, :], zlog[:, :], sxy[:, 0, :, 0], ALU.add))
                    ch.wait()
                    v.tensor_tensor(TT[:, :, NKEY:NKEY + XKEYS], rx[:, :, 0:XKEYS],
                                    zlog[:, :].unsqueeze(2).to_broadcast([P, GT, XKEYS]), ALU.subtract).then_inc(S["tt"], 1)
                else:
                    g = part - 6
                    dve.wait_ge(S["ddps"], nth(i))
                    dve.wait_ge(S["dd"], nth(i * GT + (g - 1)))
                    for b in range(TOPK):
                        ch.do(v.tensor_scalar(onehot[:, g % 2, b, :], iotab[:, :], ixyf[:, 1, g, b:b + 1], float(TOPK - b),
                                              ALU.is_equal, ALU.mult))
                    ch.wait()
                    v.tensor_reduce(DD[:, g, 0:NKEY], onehot[:, g % 2, :, :].rearrange("p b j -> p j b"), AX.X, ALU.add)\
                        .then_inc(S["dd"], 1)
            ROUTE = 2 * GT + 2 * GT + 1 + 2 * GT + 1 + 4 + 5 + 5 + GT * TOPK

            def hidden(i, S, f):
                k = i * FC + (f + 1)
                dve.wait_ge(S["tg"], nth(k))
                v.scalar_tensor_tensor(TG[:, f % 2, :], TG[:, f % 2, :], 1.0, bank[pair("F", f)][:, :], ALU.add, ALU.mult)\
                    .then_inc(S["sg"], 1)
                dve.wait_ge(S["sg"], nth(k))
                dve.wait_ge(S["ups"], nth(k))
                dve.wait_ge(S["gul"], nth(k - 2))
                v.tensor_tensor(gu[:, f % 2, :], TG[:, f % 2, :], bank[pair("F", f) + 1][:, :], ALU.mult).then_inc(S["gu"], 1)

            def experts(i, S, c):
                k = i * EC + (c + 1)
                dve.wait_ge(S["dps"], nth(k))
                dve.wait_ge(S["e"], nth(k))
                v.scalar_tensor_tensor(E[:, c % 2, :], bank[6 + c % 2][:, :], float(TOPK), E[:, c % 2, :],
                                       ALU.is_gt, ALU.mult).then_inc(S["ge"], 1)
                if c == EC - 1:
                    dve.wait_ge(S["ge"], nth(i * (EC + 1) + EC))
                    dve.wait_ge(S["rbps"], nth(i + 1))
                    v.tensor_tensor(E[:, c % 2, :], E[:, c % 2, :], bank[6][:, :], ALU.add).then_inc(S["ge"], 1)
                dve.wait_ge(S["tp"], nth(k))
                v.scalar_tensor_tensor(TP[:, c % 2, :], TP[:, c % 2, :], 1.0, bank[pair("E", c)][:, :], ALU.add, ALU.mult)\
                    .then_inc(S["sp"], 1)

            def query_lo(i, S):
                dve.wait_ge(S["tts"], nth(i + 1))
                v.tensor_tensor(TTs[:, LO, :], bank[6][0:NSEL, :], TTs[:, HI, :].bitcast(fp32), ALU.subtract).then_inc(S["ttl"], 1)

            def step(u, i, S):
                kind, n, j = unit(u, i)
                (hidden if kind == "F" else experts)(j, S, n)

            PARTS = {6: (0,), 7: (1,), 8: (2,), 9: (3,), 10: (4,), 11: (6,), 12: (5,), 13: (7,), 14: (8,), 15: (9,)}

            def ffn_block(i, S, more, L):
                if L == 0 and not more:
                    ch.wait()
                    most = Steps(factor, FACTOR, "most")
                for u in range(START, NU + START * more):
                    step(u, i, S)
                    if L == 0 and not more:
                        next_layer(u, most)
                    if u == NU + LAG - 1:
                        finished(i, S, L)
                    if more:
                        for part in PARTS.get(u, ()):
                            routing(i + 1, S, part)
                        if u == QUERIES:
                            query_lo(i + 1, S)
                if not more:
                    finished(i, S, L)

            def finished(i, S, L):
                for g in range(GT):
                    t = i * GT + g
                    if g == 0:
                        dve.wait_ge(S["ecol"], nth(i * EC + EC))
                    v.scalar_tensor_tensor(x[:, t, :], bank[4 + g // 2][:, DM * (g % 2):DM * (g % 2 + 1)], 0.25, x[:, t, :],
                                           ALU.mult, ALU.add).then_inc(S["out"], 1)
                if L == 0:
                    sums_of(i * GT, GT, S["out"])

            def next_layer(u, most):
                if u == START + 1:
                    split_lo(dve, v, "v", SPLITS_A[:1], len(SPLITS))
                elif u == START + 2:
                    split_lo(dve, v, "v", SPLITS_A[1:], len(SPLITS) + 1)
                for _ in range(3):
                    most()
                if u == NU - 1:
                    wait_split(dve, SPLITS + SPLITS_A)
                    ch.wait()
                    normalized(0, xn_a, AG, att_s["xn"])

            def start(L, between=None):
                if L == 0:
                    first_sums(0)
                    first_sums(1)
                    factors("even")
                for n in (0, 1):
                    normalized(NORDER[n] * GT, xn[:, n, :, :], GT, ffn_s[L]["xn"], between)

            def transposed_lo(S, n):
                for k in range(KD):
                    dve.wait_ge(S["h"], nth(n * KD + k + 1))
                    v.tensor_tensor(hT[:, NORDER[n], LO, k, :], bank[NBANK[n] + k][:, :],
                                    hT[:, NORDER[n], HI, k, :].bitcast(fp32), ALU.subtract).then_inc(S["hl"], 1)

            def constants():
                dve.wait_ge(in_c, 16 * len(CONSTS))
                ch.do(v.tensor_copy(iotab[:, :], iota[:, :]))
                ch.do(v.tensor_scalar(small[:, 0:25], small[:, 0:25], 0.5, None, ALU.mult))
                dve.wait_ge(att_s["eu"], nth(1))
                ch.do(v.tensor_scalar(negA[:, :], negA[:, :], -1.0, None, ALU.mult))
                ch.wait()

            def ffn(L):
                S = ffn_s[L]
                if L == 0:
                    start(0)
                    split_lo(dve, v, "v", SPLITS[:1], 0)
                    constants()
                transposed_lo(S, 0)
                transposed_lo(S, 1)
                if L == 0:
                    for n in (2, 3):
                        first_sums(n)
                factors("odd")
                if L == 0:
                    wait_split(dve, SPLITS[:3])
                    dve.wait_ge(prep, PREPARED)
                step(0, 0, S)
                for n in (2, 3):
                    dve.wait_ge(S["hps"], nth((n - 1) * KD))
                    normalized(NORDER[n] * GT, xn[:, n % 2, :, :], GT, S["xn"])
                step(1, 0, S)
                routing(0, S, 0)
                routing(0, S, 1)
                step(2, 0, S)
                routing(0, S, 2)
                transposed_lo(S, 2)
                step(3, 0, S)
                routing(0, S, 3)
                routing(0, S, 4)
                step(4, 0, S)
                routing(0, S, 6)
                transposed_lo(S, 3)
                routing(0, S, 5)
                routing(0, S, 7)
                routing(0, S, 8)
                routing(0, S, 9)
                step(5, 0, S)
                query_lo(0, S)
                if L == 0:
                    wait_split(dve, SPLITS)
                with dve.Fori(0, BLOCKS - 1) as i:
                    ch.enter(i, ROUTE + (GT if L == 0 else 0))
                    ffn_block(i, S, True, L)
                    ch.leave(BLOCKS - 1)
                ffn_block(BLOCKS - 1, S, False, L)

            ffn(0)

            S = att_s
            raw, ab, u1, s1, s2, pl = (sp[:, n, :] for n in range(6))
            SOFTPLUS = 5 + (SERIES - 1) + 3

            def softplus(step, f, q):
                if step == 0:
                    dve.wait_ge(S["eu"], nth(f + 2))
                    return ch.do(v.tensor_scalar(s1, u1, 2.0, None, ALU.add))
                if step == 1:
                    return ch.do(v.reciprocal(s1, s1))
                if step == 2:
                    return ch.do(v.tensor_tensor(s1, s1, u1, ALU.mult))
                if step == 3:
                    return ch.do(v.tensor_tensor(s2, s1, s1, ALU.mult))
                if step == 4:
                    return ch.do(v.tensor_scalar(pl, s2, 1.0 / (2 * SERIES + 1), None, ALU.mult))
                if step < 4 + SERIES:
                    return ch.do(v.scalar_tensor_tensor(pl, pl, 1.0 / (2 * (4 + SERIES - step) + 1), s2, ALU.add, ALU.mult))
                if step == 4 + SERIES:
                    return ch.do(v.scalar_tensor_tensor(pl, pl, 1.0, s1, ALU.add, ALU.mult))
                if step == 5 + SERIES:
                    return ch.do(v.tensor_scalar(raw, raw, 0.0, None, ALU.max))
                return ch.do(v.scalar_tensor_tensor(dt[:, q, :, :].rearrange("p g h -> p (g h)"), pl, 2.0, raw, ALU.mult, ALU.add))

            def conv(f, q, p, between=None):
                c = CORDER[p]
                dst = xB[:, :] if c == CC else xc[:, q, c, :]
                dve.wait_ge(S["u"], nth(f * CONVC + (p + 1)))
                for k in range(TAPS - 2, -1, -1):
                    if k < TAPS - 2:
                        ch.wait(last)
                    w = v.scalar_tensor_tensor(dst, U[:, p % 2, k:k + AT], convw[:, c, k:k + 1], dst, ALU.mult, ALU.add)
                    if k:
                        last = ch.do(w)
                    else:
                        w.then_inc(S["conv"], 1)
                    if between:
                        between()

            def conv_silu(f, q, p):
                c = CORDER[p]
                dve.wait_ge(S["tc"], nth(f * CONVC + (p + 1)))
                if c < CC:
                    v.scalar_tensor_tensor(xc[:, q, c, :], TC[:, p % 2, :], 1.0, xc[:, q, c, :], ALU.add, ALU.mult).then_inc(S["xc"], 1)
                    return
                ch.do(v.scalar_tensor_tensor(BTt[:, q, :], TC[0:NS, p % 2, :], 1.0, xB[0:NS, :], ALU.add, ALU.mult))
                v.scalar_tensor_tensor(CTt[:, q, :], TC[NS:P, p % 2, :], 1.0, xB[NS:P, :], ALU.add, ALU.mult).then_inc(S["xc"], 1)

            def lo_of(f, q):
                dve.wait_ge(S["h"], nth(f + 1))
                v.tensor_tensor(hTb[:, q, LO, :], bank[0][:, :], hTb[:, q, HI, :].bitcast(fp32), ALU.subtract).then_inc(S["hl"], 1)

            def scan_in(k):
                dve.wait_ge(S["cbps"], nth(k))
                dve.wait_ge(S["m"], nth(k - 1))
                v.tensor_tensor(CBm[:, :], bank[7][:, 0:P], tri_incl, ALU.mult).then_inc(S["cbm"], 1)

            def gate(k, g):
                dve.wait_ge(S["tz"], nth(k))
                v.scalar_tensor_tensor(Tz[:, g, :], Tz[:, g, :], 1.0, bank[1][:, :], ALU.add, ALU.mult).then_inc(S["sz"], 1)

            def weights_of(k, g):
                dve.wait_ge(S["cbm"], nth(k))
                dve.wait_ge(S["lx"], nth(2 * k))
                v.tensor_tensor(Lx[:, g, :, :], Lx[:, g, :, :], CBm[:, :].unsqueeze(1).to_broadcast([P, NH, P]), ALU.mult)\
                    .then_inc(S["m"], 1)

            def from_before(k, b, q, g, between):
                dve.wait_ge(S["offps"], nth(k))
                dve.wait_ge(S["decays"], nth(b + 1))
                dve.wait_ge(S["ss"], nth(k - 2))
                dve.wait_ge(S["ytps"], nth(k - 2))
                v.tensor_tensor(hb(y1[:, g, :]), hb(bank[4][:, :]), per_head(decays[:, q, 0, g, :]), ALU.mult)\
                    .then_inc(S["yoff"], 1)
                between()
                dve.wait_ge(S["dec"], nth(k))
                dve.wait_ge(S["stps"], nth(k))
                v.tensor_tensor(state[:, :], state[:, :], bank[5][0:NS, :], ALU.add).then_inc(S["state"], 1)

            def gated(k, g):
                dve.wait_ge(S["ydps"], nth(k))
                dve.wait_ge(S["yoff"], nth(k))
                v.tensor_tensor(y1[:, g, :], y1[:, g, :], bank[6][:, :], ALU.add).then_inc(S["yadd"], 1)
                dve.wait_ge(S["yadd"], nth(k))
                dve.wait_ge(S["sz"], nth(k))
                v.tensor_tensor(y1[:, g, :], y1[:, g, :], Tz[:, g, :], ALU.mult).then_inc(S["yg"], 1)

            def raw_dt(f):
                dve.wait_ge(S["dtps"], nth(f + 1))
                v.tensor_tensor(raw.rearrange("p (g h) -> p g h", h=NH),
                                bank[3][:, 0:AG * NH].rearrange("p (g h) -> p g h", h=NH),
                                dtb.unsqueeze(1).to_broadcast([P, AG, NH]), ALU.add).then_inc(S["raw"], 1)
                dve.wait_ge(S["raw"], nth(f + 1))
                v.scalar_tensor_tensor(ab, raw, -1.0, raw, ALU.mult, ALU.max).then_inc(S["ab"], 1)

            def step_sizes(f, q):
                v.tensor_tensor(a[:, q, :, :], dt[:, q, :, :], negA[:, :].unsqueeze(1).to_broadcast([P, AG, NH]), ALU.mult)\
                    .then_inc(S["a"], 1)

            def step_sizes_lo(f, q):
                dve.wait_ge(S["ahi"], nth(f + 1))
                v.tensor_tensor(asplit[:, q, LO, :], a[:, q, :, :].rearrange("p g h -> p (g h)"),
                                asplit[:, q, HI, :].bitcast(fp32), ALU.subtract).then_inc(S["alo"], 1)

            def variance(step, q):
                if step == 0:
                    return ch.do(v.tensor_scalar(varc[:, 1, 0:AG], ss[:, q, :], 0.25 / DI, RMS_EPS, ALU.mult, ALU.add))
                return rsqrt(step - 1, 1, varc[:, 1, 0:AG], varc[:, 1, AG:2 * AG], 0.5)

            def residual(b, between=None):
                dve.wait_ge(S["o"], nth(b * AG + AG))
                for g in range(AG):
                    v.scalar_tensor_tensor(x[:, b * AG + g, :], obuf[:, g, :], varc[:, 1, AG + g:AG + g + 1], x[:, b * AG + g, :],
                                           ALU.mult, ALU.add).then_inc(S["x1"], 1)
                    if between:
                        between()
                sums_of(b * AG, AG, S["x1"])

            def group(b, q, front, prev):
                k, f, r = b * AG + 1, b + 1, 1 - q
                if prev:
                    dve.wait_ge(S["ss"], nth(b * AG))
                norm = Steps(variance, RSQRT + 1 if prev else 0, r)
                sizes = Steps(softplus, SOFTPLUS, f, r) if front else Steps(factor, FACTOR, "even")

                def chains():
                    for _ in range(2):
                        sizes()
                        norm()

                if front:
                    dve.wait_ge(S["hps"], nth(f))
                    normalized(f * AG, xn_a, AG, S["xn"])
                    norm()
                weights_of(k, 0)
                norm()
                gate(k, 0)
                norm()
                from_before(k, b, q, 0, norm)
                norm()
                if front:
                    lo_of(f, r)
                    norm()
                scan_in(k + 1)
                if front:
                    raw_dt(f)
                    conv(f, r, 0, chains)
                weights_of(k + 1, 1)
                norm()
                gated(k, 0)
                norm()
                gate(k + 1, 1)
                while norm.n < norm.count:
                    chains()
                if prev:
                    ch.wait(norm.last)
                    residual(b - 1, sizes)
                sizes()
                from_before(k + 1, b, q, 1, sizes)
                if front:
                    conv(f, r, 1, chains)
                    while sizes.n < sizes.count:
                        sizes()
                    ch.wait(sizes.last)
                    step_sizes(f, r)
                    conv_silu(f, r, 0)
                    step_sizes_lo(f, r)
                    conv(f, r, 2)
                gated(k + 1, 1)
                if front:
                    rest_of_front(f, r)
                    scan_in(k + 2)
                while sizes.n < sizes.count:
                    sizes()

            def rest_of_front(f, q, between=None):
                conv_silu(f, q, 1)
                for p in (3, 4):
                    conv(f, q, p, between)
                    conv_silu(f, q, p - 1)
                conv_silu(f, q, 4)

            FRONT = CONVC * (TAPS - 2) + SOFTPLUS + 1
            PREV = 1 + RSQRT + 1 + AG
            lo_of(0, 0)
            raw_dt(0)
            sizes = Steps(softplus, SOFTPLUS, 0, 0)
            conv(0, 0, 0, sizes)
            conv(0, 0, 1, sizes)
            conv_silu(0, 0, 0)
            while sizes.n < sizes.count:
                sizes()
            ch.wait(sizes.last)
            step_sizes(0, 0)
            step_sizes_lo(0, 0)
            conv(0, 0, 2)
            last_factors = Steps(factor, FACTOR, "last")
            rest_of_front(0, 0, last_factors)
            while last_factors.n < FACTOR:
                last_factors()
            scan_in(1)
            group(0, 0, True, False)
            with dve.Fori(0, GROUPS // 2 - 1) as j:
                ch.enter(j, 2 * (FRONT + PREV))
                group(j * 2 + 1, 1, True, True)
                group(j * 2 + 2, 0, True, True)
                ch.leave(GROUPS // 2 - 1)
            group(GROUPS - 1, 1, False, True)
            dve.wait_ge(S["ss"], nth(TILES))
            norm = Steps(variance, RSQRT + 1, 1)
            ch.wait()
            start(1, norm)
            while norm.n < norm.count:
                norm()
            ch.wait()
            residual(GROUPS - 1)
            dve.wait_ge(S["x1"], nth(TILES))
            ffn(1)

        @block.scalar
        def _(act):
            s = nc.scalar
            credit(act, "act")

            def hidden(i, S, f):
                k = i * FC + (f + 1)
                act.wait_ge(S["gps"], nth(k))
                act.wait_ge(S["gu"], nth(k - 2))
                s.activation(TG[:, f % 2, :], bank[pair("F", f)][:, :], ACT.Tanh, scale=0.5).then_inc(S["tg"], 1)

            def hidden_hi(i, S, f):
                k = i * FC + (f + 1)
                act.wait_ge(S["gu"], nth(k))
                act.wait_ge(S["gcol"], nth(k - 2))
                s.activation(gus[:, HI, f % 2, :], gu[:, f % 2, :], ACT.Copy).then_inc(S["guh"], 1)

            def experts(i, S, c):
                k = i * EC + (c + 1)
                act.wait_ge(S["lps"], nth(k))
                act.wait_ge(S["coef"], nth(k - 2))
                s.activation(E[:, c % 2, :], bank[pair("E", c) + 1][:, :], ACT.Exp).then_inc(S["e"], 1)
                act.wait_ge(S["pps"], nth(k))
                s.activation(TP[:, c % 2, :], bank[pair("E", c)][:, :], ACT.Tanh, scale=0.5).then_inc(S["tp"], 1)

            def experts_hi(i, S, c):
                k = i * EC + (c + 1)
                act.wait_ge(S["coef"], nth(k))
                act.wait_ge(S["ecol"], nth(k - 2))
                s.activation(coefs[:, HI, c % 2, :], coef[:, c % 2, :], ACT.Copy).then_inc(S["coh"], 1)

            def scores(i, S, part):
                if part == 0:
                    act.wait_ge(S["rps"], nth(i + 1))
                    act.wait_ge(S["rtps"], nth(i))
                    s.activation(rT[:, :], bank[6][:, :], ACT.Copy).then_inc(S["rT"], 1)
                elif part == 1:
                    act.wait_ge(S["rtps"], nth(i + 1))
                    act.wait_ge(S["tt"], nth(i))
                    s.activation(rtok[:, :, :].rearrange("p g k -> p (g k)"), bank[7][:, :], ACT.Copy).then_inc(S["rtok"], 1)
                elif part == 2:
                    act.wait_ge(S["dxy"], nth(i + 1))
                    s.activation(exy[:, :, :], dxy[:, :, :], ACT.Exp).then_inc(S["exy"], 1)
                elif part == 3:
                    act.wait_ge(S["zs"], nth(i + 1))
                    s.activation(zlog[:, :], zsum[:, :], ACT.Ln).then_inc(S["zlog"], 1)
                else:
                    act.wait_ge(S["ttps"], nth(i + 1))
                    act.wait_ge(S["rbps"], nth(i))
                    s.activation(TTs[:, HI, :], bank[6][0:NSEL, :], ACT.Copy).then_inc(S["tts"], 1)
                    act.wait_ge(S["ddps"], nth(i + 1))
                    act.wait_ge(S["dps"], nth(i * EC))
                    s.activation(DDs[:, :], bank[7][0:NSEL - 1, :], ACT.Copy).then_inc(S["dds"], 1)
            SCORES = {6: (1,), 8: (2,), 11: (3,), QUERIES: (4,)}

            def step(u, i, S):
                kind, n, j = unit(u, i)
                before = unit(u - 1, i) if u else None
                if before and before[0] == "F":
                    hidden_hi(before[2], S, before[1])
                (hidden if kind == "F" else experts)(j, S, n)
                if before and before[0] == "E":
                    experts_hi(before[2], S, before[1])

            def ffn_block(i, S, more, L):
                if more:
                    scores(i + 1, S, 0)
                for u in range(START, NU + START * more):
                    step(u, i, S)
                    if L == 0 and not more and u == START:
                        act.wait_ge(S["pps"], nth(i * EC))
                        split_hi(SPLITS_A)
                    if more:
                        for part in SCORES.get(u, ()):
                            scores(i + 1, S, part)
                if not more:
                    experts_hi(i, S, EC - 1)

            def ffn(L):
                S = ffn_s[L]
                def transposed_hi(n):
                    for k in range(KD):
                        act.wait_ge(S["hps"], nth(n * KD + k + 1))
                        s.activation(hT[:, NORDER[n], HI, k, :], bank[NBANK[n] + k][:, :], ACT.Copy).then_inc(S["h"], 1)

                def query(n):
                    side, at = NORDER[n] // (BLOCKS // 2), BT * (NORDER[n] % (BLOCKS // 2))
                    act.wait_ge(S["qps"], nth(n + 1))
                    qv = qT[NS * side:NS * (side + 1), :].rearrange("p (m two) -> p two m", two=2)
                    for half in range(2):
                        s.activation(qv[:, half, at:at + BT], bank[QBANK[n]][NS * half:NS * (half + 1), :], ACT.Copy).then_inc(S["q"], 1)

                if L == 0:
                    split_hi(SPLITS[:3])
                    selectors()
                transposed_hi(0)
                transposed_hi(1)
                query(0)
                query(1)
                if L == 0:
                    split_hi(SPLITS[3:])
                    wait_split(act, SPLITS[:3])
                step(0, 0, S)
                scores(0, S, 0)
                step(1, 0, S)
                scores(0, S, 1)
                step(2, 0, S)
                scores(0, S, 2)
                transposed_hi(2)
                step(3, 0, S)
                query(2)
                step(4, 0, S)
                transposed_hi(3)
                scores(0, S, 3)
                query(3)
                step(5, 0, S)
                scores(0, S, 4)
                if L == 0:
                    wait_split(act, SPLITS)
                with act.Fori(0, BLOCKS - 1) as i:
                    ffn_block(i, S, True, L)
                ffn_block(BLOCKS - 1, S, False, L)

            def selectors():
                act.wait_ge(in_w["sel"], 16)
                selw = stage["sel"].rearrange("p (c q) -> p c q", q=P)
                s.activation(selb[:, :, :], selw[0:NSEL - 1, 0:EC, :], ACT.Copy).then_inc(prep, 1)
                s.activation(sel[:, :, :], selw, ACT.Copy).then_inc(prep, 1)

            def split_hi(weights):
                for name, t, _ in weights:
                    act.wait_ge(in_w[name], 16)
                    s.activation(flat(t, HI), stage[name], ACT.Copy).then_inc(w_hi, 1)

            act.wait_ge(in_c, 16 * len(CONSTS))
            s.activation(negA[:, :], alog, ACT.Exp).then_inc(att_s["eu"], 1)
            ffn(0)
            S = att_s

            def hi_of(f, q):
                act.wait_ge(S["hps"], nth(f + 1))
                s.activation(hTb[:, q, HI, :], bank[0][:, :], ACT.Copy).then_inc(S["h"], 1)

            def conv_in(f, q, p):
                c = CORDER[p]
                act.wait_ge(S["conv"], nth(f * CONVC + (p - 1)))
                s.activation(U[:, p % 2, 0:TAPS - 1], hist[:, c, :], ACT.Copy).then_inc(S["hist"], 1)
                act.wait_ge(S["pps"], nth(f * CONVC + (p + 1)))
                s.activation(U[:, p % 2, TAPS - 1:], bank[p % 2][:, 0:AT], ACT.Copy).then_inc(S["hist"], 1)
                act.wait_ge(S["ydps"], nth((f - 1) * AG))
                s.activation(xB[:, :] if c == CC else xc[:, q, c, :], bank[p % 2][:, 0:AT], ACT.Identity,
                             bias=convb[:, c:c + 1], scale=convw[:, c, TAPS - 1:TAPS]).then_inc(S["hist"], 1)
                act.wait_ge(S["hist"], nth(f * (3 * CONVC) + (3 * p + 1)))
                s.activation(hist[:, c, :], bank[p % 2][:, AT - TAPS + 1:AT], ACT.Copy).then_inc(S["u"], 1)

            def conv_tanh(f, q, p):
                c = CORDER[p]
                act.wait_ge(S["conv"], nth(f * CONVC + (p + 1)))
                act.wait_ge(S["xc"], nth(f * CONVC + (p - 1)))
                s.activation(TC[:, p % 2, :], xB[:, :] if c == CC else xc[:, q, c, :], ACT.Tanh).then_inc(S["tc"], 1)

            def gate(k, g):
                act.wait_ge(S["zps"], nth(k))
                act.wait_ge(S["yg"], nth(k - 2))
                s.activation(Tz[:, g, :], bank[1][:, :], ACT.Tanh, scale=0.5).then_inc(S["tz"], 1)

            def exponents(k, g):
                for n in range(2):
                    act.wait_ge(S["segps"], nth(2 * k + (n - 1)))
                    act.wait_ge(S["ydps"], nth(k - 2))
                    s.activation(Lx[:, g, 4 * n:4 * n + 4, :].rearrange("p h l -> p (h l)"), bank[4 + n][:, :], ACT.Exp)\
                        .then_inc(S["lx"], 1)

            def tokens(k):
                act.wait_ge(S["xps"], nth(k))
                act.wait_ge(S["xdt"], nth(k - 1))
                s.activation(xtok[:, :], bank[2][:, :], ACT.Copy).then_inc(S["xt"], 1)
                act.wait_ge(S["cbm"], nth(k))
                act.wait_ge(S["stps"], nth(k - 1))
                s.activation(Btok[:, :], bank[7][:, P:P + NS], ACT.Copy).then_inc(S["bt"], 1)

            def gated_t(k):
                act.wait_ge(S["ytps"], nth(k))
                act.wait_ge(S["ss"], nth(k))
                s.activation(ygT[:, :, :].rearrange("p c t -> p (c t)"), bank[2][:, :], ACT.Copy).then_inc(S["yt"], 1)

            def output(k, b, g):
                act.wait_ge(S["ops"], nth(k))
                act.wait_ge(S["x1"], nth(b * AG))
                s.activation(obuf[:, g, :], bank[3][:, 0:DM], ACT.Copy).then_inc(S["o"], 1)

            def squares(k, q, g):
                act.wait_ge(S["yg"], nth(k))
                s.activation(ygT[:, :, :].rearrange("p c t -> p (c t)"), y1[:, g, :], ACT.Square, accum_out=ss[:, q, g:g + 1])\
                    .then_inc(S["ss"], 1)

            def sizes(f):
                act.wait_ge(S["ab"], nth(f + 1))
                s.activation(sp[:, 2, :], sp[:, 1, :], ACT.Exp, scale=-1.0).then_inc(S["eu"], 1)

            def sizes_hi(f, q):
                act.wait_ge(S["a"], nth(f + 1))
                s.activation(asplit[:, q, HI, :], a[:, q, :, :].rearrange("p g h -> p (g h)"), ACT.Copy).then_inc(S["ahi"], 1)

            def chunk_decays(f, q):
                act.wait_ge(S["cums"], nth(f + 1))
                s.activation(decays[:, q, :, :, :].rearrange("p w g h -> p (w g h)"), bank[3][:, 0:3 * AG * NH], ACT.Exp)\
                    .then_inc(S["decays"], 1)

            def group(b, q, front, prev):
                k, f, r = b * AG + 1, b + 1, 1 - q
                if front:
                    hi_of(f, r)
                tokens(k + 1)
                if front:
                    sizes(f)
                    conv_in(f, r, 0)
                exponents(k + 1, 1)
                gate(k + 1, 1)
                if front:
                    conv_tanh(f, r, 0)
                    conv_in(f, r, 1)
                squares(k, q, 0)
                if front:
                    conv_in(f, r, 2)
                gated_t(k)
                if front:
                    sizes_hi(f, r)
                output(k, b, 0)
                if front:
                    rest_of_front(f, r)
                squares(k + 1, q, 1)
                if front:
                    next_gate(f, r, k + 2)
                gated_t(k + 1)
                if front:
                    conv_tanh(f, r, 4)
                    exponents(k + 2, 0)
                    tokens(k + 2)
                output(k + 1, b, 1)

            def rest_of_front(f, q):
                conv_tanh(f, q, 1)
                chunk_decays(f, q)
                conv_in(f, q, 3)
                conv_tanh(f, q, 2)

            def next_gate(f, q, k):
                conv_in(f, q, 4)
                gate(k, 0)
                conv_tanh(f, q, 3)

            hi_of(0, 0)
            sizes(0)
            conv_in(0, 0, 0)
            conv_in(0, 0, 1)
            conv_tanh(0, 0, 0)
            conv_in(0, 0, 2)
            sizes_hi(0, 0)
            rest_of_front(0, 0)
            next_gate(0, 0, 1)
            conv_tanh(0, 0, 4)
            exponents(1, 0)
            tokens(1)
            group(0, 0, True, False)
            with act.Fori(0, GROUPS // 2 - 1) as j:
                group(j * 2 + 1, 1, True, True)
                group(j * 2 + 2, 0, True, True)
            group(GROUPS - 1, 1, False, True)
            ffn(1)

        @block.gpsimd
        def _(pool):
            gp = nc.gpsimd
            credit(pool, "pool")

            def lo(u, i, S):
                kind, n, j = unit(u, i)
                if kind == "F":
                    pool.wait_ge(S["guh"], nth(j * FC + (n + 1)))
                    gp.tensor_tensor(gus[:, LO, n % 2, :], gu[:, n % 2, :], gus[:, HI, n % 2, :].bitcast(fp32), ALU.subtract)\
                        .then_inc(S["gul"], 1)
                else:
                    pool.wait_ge(S["coh"], nth(j * EC + (n + 1)))
                    gp.tensor_tensor(coefs[:, LO, n % 2, :], coef[:, n % 2, :], coefs[:, HI, n % 2, :].bitcast(fp32), ALU.subtract)\
                        .then_inc(S["col"], 1)

            def coefficients(i, S, c):
                pool.wait_ge(S["ge"], nth(i * (EC + 1) + (c + 1 if c < EC - 1 else EC + 1)))
                pool.wait_ge(S["sp"], nth(i * EC + (c + 1)))
                pool.wait_ge(S["col"], nth(i * EC + (c - 1)))
                gp.tensor_tensor(coef[:, c % 2, :], TP[:, c % 2, :], E[:, c % 2, :], ALU.mult).then_inc(S["coef"], 1)

            def constants():
                pool.wait_ge(in_c, 16 * len(CONSTS))
                for c in range(CC):
                    gp.tensor_scalar(diagD[:, c, :], ident, dcol[:, c:c + 1], None, ALU.mult).then_inc(prep, 1)
                gp.tensor_copy(after_hi[:, :], tri_after).then_inc(prep, 1)
                gp.memset(hist[:, :, :], 0.0).then_inc(prep, 1)
                gp.memset(state[:, :], 0.0).then_inc(prep, 1)

            def ffn_block(i, S, late=None):
                for u, (kind, n) in enumerate(UNITS):
                    if u:
                        lo(u - 1, i, S)
                    if late and u in late:
                        split_lo(pool, gp, "p", SPLITS[late[u]:late[u] + 1], late[u])
                    if kind == "E":
                        coefficients(i, S, n)
                lo(NU - 1, i, S)

            def ffn(L):
                if L == 0:
                    constants()
                    split_lo(pool, gp, "p", SPLITS[:3], 0)
                    split_lo(pool, gp, "p", SPLITS[3:4], 3)
                    ffn_block(0, ffn_s[L], {2: 4, 3: 5})
                with pool.Fori(1 if L == 0 else 0, BLOCKS) as i:
                    ffn_block(i, ffn_s[L])

            ffn(0)
            pool.wait_ge(in_o, 16)
            gp.tensor_tensor(wo[:, :, :], wo[:, :, :], normw.unsqueeze(2).to_broadcast([P, CC, DM]), ALU.mult).then_inc(prep, 1)
            S = att_s

            def scan_in(b, q):
                pool.wait_ge(S["alo"], nth(b + 1))
                for g in range(AG):
                    pool.wait_ge(S["segps"], nth(2 * (b * AG + g - 1)))
                    for w in (HI, LO):
                        m = gp.tensor_tensor(adiag[:, g, w, :].rearrange("p (h l) -> p h l", h=NH),
                                             tri_incl.unsqueeze(1).to_broadcast([P, NH, P]),
                                             asplit[:, q, w, NH * g:NH * (g + 1)].bitcast(fp32).unsqueeze(2).to_broadcast([P, NH, P]),
                                             ALU.mult)
                    m.then_inc(S["ad"], 1)

            def inputs(k, b, q, g):
                pool.wait_ge(S["xt"], nth(k))
                pool.wait_ge(S["ydps"], nth(k - 2))
                gp.tensor_tensor(hb(xdt[:, g, :]), hb(xtok[:, :]), per_head(dt[:, q, g, :]), ALU.mult).then_inc(S["xdt"], 1)
                pool.wait_ge(S["xdt"], nth(k))
                pool.wait_ge(S["decays"], nth(b + 1))
                pool.wait_ge(S["stps"], nth(k - 1))
                gp.tensor_tensor(hb(xdd[:, :]), hb(xdt[:, g, :]), per_head(decays[:, q, 1, g, :]), ALU.mult).then_inc(S["xdd"], 1)

            def decayed(k, q, g):
                pool.wait_ge(S["offps"], nth(k))
                pool.wait_ge(S["state"], nth(k - 1))
                gp.tensor_tensor(hb(state[:, :]), hb(state[:, :]), per_head(decays[0:NS, q, 2, g, :], NS), ALU.mult).then_inc(S["dec"], 1)

            def group(b, q, front, prev):
                k = b * AG + 1
                decayed(k, q, 0)
                inputs(k + 1, b, q, 1)
                decayed(k + 1, q, 1)
                if front:
                    scan_in(b + 1, 1 - q)
                    inputs(k + 2, b + 1, 1 - q, 0)

            scan_in(0, 0)
            inputs(1, 0, 0, 0)
            group(0, 0, True, False)
            with pool.Fori(0, GROUPS // 2 - 1) as j:
                group(j * 2 + 1, 1, True, True)
                group(j * 2 + 2, 0, True, True)
            group(GROUPS - 1, 1, False, True)
            ffn(1)

        @block.tensor
        def _(pe):
            credit(pe, "pe")

            def mm(out, pairs):
                for n, (lhsT, rhs) in enumerate(pairs):
                    last = nc.tensor.matmul(out, lhsT, rhs, start=n == 0, stop=n == len(pairs) - 1)
                return last

            def transposes(outs_ins):
                for o, t in outs_ins:
                    n = t.shape[0]
                    last = nc.tensor.transpose(o, t, ident[0:n, 0:n])
                return last

            def split3(lhsT, rhs):
                return [(lhsT(a), rhs(b)) for a, b in ((HI, HI), (HI, LO), (LO, HI))]

            def cols(t, g):
                return t[:, P * g:P * (g + 1)]

            def ffn(L):
                S = ffn_s[L]
                def transposed(n):
                    pe.wait_ge(S["xn"], nth((n + 1) * GT))
                    for k in range(KD):
                        if n >= 2:
                            pe.wait_ge(S["rtok"], nth(1))
                            pe.wait_ge(S["q"], nth(2 * n))
                        transposes([(cols(bank[NBANK[n] + k], g), cols(xn[:, n % 2, g, :], k)) for g in range(GT)])\
                            .then_inc(S["hps"], 1)

                def query(n):
                    pe.wait_ge(S["hl"], nth(n * KD + KD))
                    mm(bank[QBANK[n]][:, :], [p for k in range(KD) for p in split3(
                        lambda w: wq[:, w, k, :], lambda w: hT[:, NORDER[n], w, k, :])]).then_inc(S["qps"], 1)

                transposed(0)
                if L == 1:
                    pe.wait_ge(att_s["o"], nth(TILES))
                transposed(1)
                if L == 0:
                    pe.wait_ge(w_lo["v"], 1)
                query(0)
                query(1)
                if L == 0:
                    wait_split(pe, SPLITS[:3])
                products(0, 0, S, True)
                if L == 0:
                    pe.wait_ge(in_k, 16)
                pe.wait_ge(S["q"], nth(4))
                raw_scores(0, S)
                products(1, 0, S, True)
                token_scores(0, S)
                products(2, 0, S, True)
                if L == 0:
                    wait_split(pe, SPLITS[:4])
                    pe.wait_ge(prep, PREPARED)
                accumulate(0, 0, S)
                transposed(2)
                products(3, 0, S, True)
                accumulate(1, 0, S)
                query(2)
                products(4, 0, S, True)
                accumulate(2, 0, S)
                transposed(3)
                query(3)
                products(5, 0, S, True)
                accumulate(3, 0, S)
                pe.wait_ge(S["q"], nth(2 * BLOCKS))
                queries(0, S)
                if L == 0:
                    wait_split(pe, SPLITS)
                with pe.Fori(0, BLOCKS - 1) as i:
                    ffn_block(i, S, True)
                ffn_block(BLOCKS - 1, S, False)

            def raw_scores(i, S):
                pe.wait_ge(S["dds"], nth(i))
                pe.wait_ge(S["ttl"], nth(i))
                mm(bank[6][:, :], [(keys[:, :], qT[:, ds(i * BT, BT)])]).then_inc(S["rps"], 1)

            def token_scores(i, S):
                pe.wait_ge(S["rT"], nth(i + 1))
                transposes([(cols(bank[7], g), cols(rT, g)) for g in range(GT)]).then_inc(S["rtps"], 1)

            def queries(i, S):
                pe.wait_ge(S["tt"], nth(i + 1))
                pe.wait_ge(S["ge"], nth(i * (EC + 1)))
                pe.wait_ge(S["rtok"], nth(i + 1))
                transposes([(cols(bank[6][0:NSEL, :], g), TT[:, g, :]) for g in range(GT)]).then_inc(S["ttps"], 1)
                pe.wait_ge(S["dd"], nth(i * GT + GT))
                transposes([(cols(bank[7][0:NSEL - 1, :], g), DD[:, g, :]) for g in range(GT)]).then_inc(S["ddps"], 1)

            def accumulate(u, i, S):
                kind, n, j = unit(u, i)
                if kind == "F":
                    pe.wait_ge(S["gul"], nth(j * FC + (n + 1)))
                    lhs, w, s = gus, wd, S["gcol"]
                else:
                    pe.wait_ge(S["col"], nth(j * EC + (n + 1)))
                    lhs, w, s = coefs, ue, S["ecol"]
                if u % NU == 0:
                    pe.wait_ge(S["out"], nth(j * GT))
                for g in range(GT):
                    o = bank[4 + g // 2][:, DM * (g % 2):DM * (g % 2 + 1)]
                    for m, (lhsT, rhs) in enumerate(split3(lambda a: cols(lhs[:, a, n % 2, :], g), lambda b: w[:, b, n, :])):
                        last = nc.tensor.matmul(o, lhsT, rhs, start=u % NU == 0 and m == 0 and g % 2 == 0,
                                                stop=u == NU - 1 and m == 2, skip_group_check=True)
                last.then_inc(s, 1)

            def products(u, i, S, more):
                kind, n, j = unit(u, i)
                b = pair(kind, n)
                before, m = UNITS[(u - 2) % NU]
                back = j - 1 if u % NU < 2 else j
                if before == "F":
                    pe.wait_ge(S["gu"], nth(back * FC + (m + 1)))
                else:
                    pe.wait_ge(S["sp"], nth(back * EC + (m + 1)))

                def h(w, k):
                    return hT[:, ds(j, 1), w, k, :].rearrange("p a t -> p (a t)")

                if kind == "F":
                    for w, o, s in ((wg, b, "gps"), (wu, b + 1, "ups")):
                        mm(bank[o][:, :], [p for k in range(KD) for p in split3(
                            lambda q: cols(w[:, q, k, :], n), lambda q: h(q, k))]).then_inc(S[s], 1)
                    return
                if n == 0:
                    pe.wait_ge(S["ttl"], nth(j + 1))
                    pe.wait_ge(S["dds"], nth(j + 1))
                    if more:
                        pe.wait_ge(S["rtok"], nth(j + 2))
                mm(bank[b + 1][:, :], [(sel[:, n, :], TTs[:, w, :]) for w in (HI, LO)]).then_inc(S["lps"], 1)
                if n >= 2:
                    pe.wait_ge(S["ge"], nth(j * (EC + 1) + (n - 1)))
                mm(bank[6 + n % 2][:, :], [(selb[:, n, :], DDs[:, :])]).then_inc(S["dps"], 1)
                mm(bank[b][:, :], [p for k in range(KD) for p in split3(
                    lambda q: cols(de[:, q, k, :], n), lambda q: h(q, k))]).then_inc(S["pps"], 1)
                if n == EC - 1:
                    pe.wait_ge(S["ge"], nth(j * (EC + 1) + n))
                    mm(bank[6][:, :], [(sel[:, EC, :], TTs[:, w, :]) for w in (HI, LO)]).then_inc(S["rbps"], 1)

            def ffn_block(i, S, more):
                if more:
                    raw_scores(i + 1, S)
                for u in range(START, NU + START * more):
                    products(u, i, S, more)
                    if more and u == START:
                        token_scores(i + 1, S)
                    accumulate(u - LAG, i, S)
                    if more and u == QUERIES:
                        queries(i + 1, S)
                if not more:
                    for u in range(NU - LAG, NU):
                        accumulate(u, i, S)

            pe.wait_ge(in_c, 16 * len(CONSTS))
            ffn(0)

            S = att_s
            wait_split(pe, SPLITS + SPLITS_A)

            def hk(q, w, k, g=None):
                return hTb[:, q, w, AT * k:AT * (k + 1)] if g is None else hTb[:, q, w, AT * k + P * g:AT * k + P * (g + 1)]

            def transposed(f):
                pe.wait_ge(S["xn"], nth(f * AG + AG))
                pe.wait_ge(S["u"], nth(f * CONVC))
                transposes([(cols(bank[0], AG * k + g), cols(xn_a[:, g, :], k)) for k in range(KD) for g in range(AG)])\
                    .then_inc(S["hps"], 1)

            def raw_dt(f, q):
                pe.wait_ge(S["hl"], nth(f + 1))
                pe.wait_ge(S["o"], nth((f - 1) * AG))
                for g in range(AG):
                    last = mm(bank[3][:, NH * g:NH * (g + 1)], [p for k in range(KD) for p in split3(
                        lambda w: hk(q, w, k, g), lambda w: wdt[:, w, k, :])])
                last.then_inc(S["dtps"], 1)

            def project(f, q, p):
                pe.wait_ge(S["u"], nth(f * CONVC + (p - 1)))
                if p == 1:
                    pe.wait_ge(S["sz"], nth(f * AG))
                mm(bank[p % 2][:, 0:AT], [m for k in range(KD) for m in split3(
                    lambda w: cols(win[:, w, k, :], CORDER[p]), lambda w: hk(q, w, k))]).then_inc(S["pps"], 1)

            def sums(f, q):
                pe.wait_ge(S["a"], nth(f + 1))
                pe.wait_ge(S["o"], nth((f - 1) * AG + 1))
                arow = a[:, q, :, :].rearrange("p g h -> p (g h)")
                for n, w in enumerate((tri_incl, tri_after, ones)):
                    last = mm(bank[3][:, AG * NH * n:AG * NH * (n + 1)], [(w, arow)])
                last.then_inc(S["cums"], 1)

            def gate(k, q, g):
                pe.wait_ge(S["sz"], nth(k - 1))
                mm(bank[1][:, :], [p for m in range(KD) for p in split3(
                    lambda w: hk(q, w, m, g), lambda w: wz[:, w, m, :])]).then_inc(S["zps"], 1)

            def decay_sums(k, g):
                pe.wait_ge(S["ad"], nth(k))
                pe.wait_ge(S["yoff"], nth(k - 1))
                pe.wait_ge(S["state"], nth(k - 1))
                for n in range(2):
                    mm(bank[4 + n][:, :], [(after_hi[:, :], adiag[:, g, w, 512 * n:512 * (n + 1)])
                                           for w in (HI, LO)]).then_inc(S["segps"], 1)

            def tokens(k, b, q, g):
                pe.wait_ge(S["xc"], nth(b * CONVC + CONVC))
                if g:
                    pe.wait_ge(S["xt"], nth(k - 1))
                else:
                    pe.wait_ge(S["yt"], nth(k - 2))
                transposes([(cols(bank[2], c), cols(xc[:, q, c, :], g)) for c in range(CC)]).then_inc(S["xps"], 1)
                pe.wait_ge(S["bt"], nth(k - 1))
                mm(bank[7][:, 0:P], [(cols(BTt[:, q, :], g), cols(CTt[:, q, :], g))])
                transposes([(bank[7][:, P:P + NS], cols(BTt[:, q, :], g))]).then_inc(S["cbps"], 1)

            def from_before(k, q, g):
                pe.wait_ge(S["state"], nth(k - 1))
                pe.wait_ge(S["lx"], nth(2 * k - 1))
                mm(bank[4][:, :], [(cols(CTt[:, q, :], g), state[:, :])]).then_inc(S["offps"], 1)

            def to_after(k):
                pe.wait_ge(S["lx"], nth(2 * k))
                pe.wait_ge(S["bt"], nth(k))
                pe.wait_ge(S["xdd"], nth(k))
                mm(bank[5][0:NS, :], [(Btok[:, :], xdd[:, :])]).then_inc(S["stps"], 1)

            def within(k, q, g):
                pe.wait_ge(S["m"], nth(k))
                pe.wait_ge(S["xdt"], nth(k))
                pe.wait_ge(S["yadd"], nth(k - 1))
                for c in range(CC):
                    nc.tensor.matmul(cols(bank[6], c), cols(xc[:, q, c, :], g), diagD[:, c, :],
                                     start=c == 0, stop=False, skip_group_check=True)
                for h in range(NH):
                    last = nc.tensor.matmul(bank[6][:, HD * h:HD * (h + 1)], Lx[:, g, h, :], xdt[:, g, HD * h:HD * (h + 1)],
                                            start=False, stop=h == NH - 1, skip_group_check=True)
                last.then_inc(S["ydps"], 1)

            def gated_t(k, g):
                pe.wait_ge(S["yg"], nth(k))
                pe.wait_ge(S["xt"], nth(k + 1 - g))
                pe.wait_ge(S["yt"], nth(k - 1))
                transposes([(cols(bank[2], c), cols(y1[:, g, :], c)) for c in range(CC)]).then_inc(S["ytps"], 1)

            def output(k):
                pe.wait_ge(S["yt"], nth(k))
                pe.wait_ge(S["o"], nth(k - 1))
                mm(bank[3][:, 0:DM], [(ygT[:, c, :], wo[:, c, :]) for c in range(CC)]).then_inc(S["ops"], 1)

            def group(b, q, front, prev):
                k, f, r = b * AG + 1, b + 1, 1 - q
                from_before(k, q, 0)
                if front:
                    transposed(f)
                to_after(k)
                tokens(k + 1, b, q, 1)
                if front:
                    raw_dt(f, r)
                    project(f, r, 0)
                decay_sums(k + 1, 1)
                within(k, q, 0)
                gate(k + 1, q, 1)
                from_before(k + 1, q, 1)
                to_after(k + 1)
                gated_t(k, 0)
                if front:
                    project(f, r, 1)
                    project(f, r, 2)
                within(k + 1, q, 1)
                if front:
                    pe.wait_ge(S["raw"], nth(f + 1))
                output(k)
                if front:
                    rest_of_front(f, r)
                gated_t(k + 1, 1)
                if front:
                    decay_sums(k + 2, 0)
                    tokens(k + 2, f, r, 0)
                    pe.wait_ge(S["decays"], nth(f + 1))
                output(k + 1)

            def rest_of_front(f, q):
                sums(f, q)
                project(f, q, 3)
                project(f, q, 4)
                pe.wait_ge(S["u"], nth(f * CONVC + 4))
                gate(f * AG + 1, q, 0)

            transposed(0)
            raw_dt(0, 0)
            project(0, 0, 0)
            project(0, 0, 1)
            project(0, 0, 2)
            pe.wait_ge(S["raw"], nth(1))
            rest_of_front(0, 0)
            decay_sums(1, 0)
            tokens(1, 0, 0, 0)
            pe.wait_ge(prep, PREPARED + 1)
            group(0, 0, True, False)
            with pe.Fori(0, GROUPS // 2 - 1) as j:
                group(j * 2 + 1, 1, True, True)
                group(j * 2 + 2, 0, True, True)
            group(GROUPS - 1, 1, False, True)
            ffn(1)


def kernel(**inputs):
    import numpy as np
    import concourse.bacc as bacc
    from concourse.bass_utils import run_bass_kernel_spmd

    pre = "L0_attn_"
    w = {k: np.asarray(v) for k, v in inputs.items()}
    f32 = np.float32

    def rows(a, n):
        return np.ascontiguousarray(a.reshape(n, P, -1).transpose(1, 0, 2))

    w_inT = w[pre + "W_in"].T
    k = w["L0_ffn_keys"]
    keys = np.zeros((P, P), f32)
    keys[:NKEY, :NKEY], keys[NKEY:, NKEY:] = k[0], k[1]
    small = np.concatenate([
        w[pre + "conv_w"].reshape(CONVC, P, TAPS).transpose(1, 0, 2).reshape(P, CONVC * TAPS),
        w[pre + "conv_b"].reshape(CONVC, P).T, w[pre + "norm_w"].reshape(CC, P).T,
        np.broadcast_to(w[pre + "dt_bias"], (P, NH)), np.broadcast_to(w[pre + "A_log"], (P, NH)),
        np.repeat(w[pre + "D_param"], HD).reshape(CC, P).T], axis=1)
    r = np.arange(P)
    cst = np.stack([r[:, None] == r, r[:, None] <= r, r[:, None] > r, np.ones((P, P), bool)], axis=1).astype(f32)
    sel = np.zeros((NKEY + XKEYS + 1, EC + 1, P), f32)
    for c in range(EC):
        sel[r % NKEY, c, r] = 1
        sel[NKEY + 2 * c + r // NKEY, c, r] = 1
    sel[NKEY + XKEYS, EC, P - 1] = 1
    arrays = {
        "u": w[pre + "u"], "wq": rows(w["L0_ffn_W_q"], KD), "keys": keys,
        "wg": rows(w["L0_ffn_gate_w"], KD), "wu": rows(w["L0_ffn_up_w"], KD), "wd": rows(w["L0_ffn_down_w"], FC),
        "de": rows(w["L0_ffn_down_embed"].T, KD), "ue": rows(w["L0_ffn_up_embed"], EC),
        "win": rows(w_inT[:, DI:DI + XBC], KD), "wz": rows(w_inT[:, :DI], KD), "wdt": rows(w_inT[:, DI + XBC:], KD),
        "wo": rows(w[pre + "W_out"].T, CC), "small": small, "cst": cst, "sel": sel,
        "iota": np.broadcast_to(np.arange(NKEY, dtype=f32), (P, NKEY)),
    }
    arrays = {n: np.ascontiguousarray(a) for n, a in arrays.items()}
    nc = bacc.Bacc("TRN2", target_bir_lowering=False, num_devices=1)
    A = {n: nc.dram_tensor(f"in_{n}", a.shape, mybir.dt.from_np(a.dtype), kind="ExternalInput").ap()
         for n, a in arrays.items()}
    A["out"] = nc.dram_tensor("out", (1, SEQ, DM), mybir.dt.float32, kind="ExternalOutput").ap()
    program(nc, A)
    res = run_bass_kernel_spmd(nc, [{f"in_{n}": a for n, a in arrays.items()}], core_ids=[0])
    return res.results[0]["out"]
```
